# Optimizing a Trainium2 kernel written in Bass

```python
import numpy as np
import jax
import jax.numpy as jnp

def _softmax(x, axis=-1):
    return jax.nn.softmax(x, axis=axis)

def _gelu(x):
    return jax.nn.gelu(x, approximate=True)

def _silu(x):
    return jax.nn.silu(x)

def _sigmoid(x):
    return jax.nn.sigmoid(x)

def _layernorm(x, axis=-1, eps=1e-05):
    m = jnp.mean(x, axis=axis, keepdims=True)
    v = jnp.var(x, axis=axis, keepdims=True)
    return (x - m) / jnp.sqrt(v + eps)

def _scatter_add(tgt, idx, src, axis=0):
    return tgt.at[idx].add(src)

def _segment_sum(src, seg, n):
    return jax.ops.segment_sum(src, seg, n)
kernel_name = 'mk_flamingo_gated_d2_seqx_r4_294a57'

def setup_inputs(seed: int=0):
    np.random.seed(seed)
    _w = jnp.asarray

    def _rec_inputs():
        import jax
        import jax.numpy as jnp
        _rk = jax.random.key(seed)
        x = -0.0003929 + 0.9999 * jax.random.normal(jax.random.fold_in(_rk, 1), (8, 112, 512), jnp.float32)
        _lenS = 112 - jax.random.randint(jax.random.fold_in(_rk, 7), (8,), 0, max(1, 112 // 4) + 1, jnp.int32)
        _lenS2 = 375 - jax.random.randint(jax.random.fold_in(_rk, 8), (8,), 0, max(1, 375 // 4) + 1, jnp.int32)
        _ctx_2048P = jax.random.normal(jax.random.fold_in(_rk, 11), (8, 16, 512), jnp.float32)
        _ctx_2048c = jax.random.dirichlet(jax.random.fold_in(_rk, 511), 0.3 * jnp.ones((16,), jnp.float32), (8, 375))
        _ctx_2048t = jnp.einsum('bsk,bkd->bsd', _ctx_2048c, _ctx_2048P)
        _ctx_2048t = _ctx_2048t * jax.lax.rsqrt(jnp.mean(jnp.square(_ctx_2048t)) + 1e-12) * 0.953939
        ctx_2048 = -0.000514642 + 1.00011 * (_ctx_2048t + 0.3 * jax.random.normal(jax.random.fold_in(_rk, 611), (8, 375, 512), jnp.float32))
        _validS = jnp.arange(112)[None, :] < _lenS[:, None]
        _validS2 = jnp.arange(375)[None, :] < _lenS2[:, None]
        _causal = jnp.tril(jnp.ones((112, 112), dtype=bool))
        mask_BxS2_ik0 = jnp.where(jnp.broadcast_to(_validS2[:, :], (8, 375)), 0, 1).astype(jnp.int32)
        _g = jax.random.normal(jax.random.fold_in(_rk, 9001), (2, 2), jnp.float32)
        _g = jnp.sign(_g) * jnp.maximum(jnp.abs(_g), 1.0) + (_g == 0) * 1.0
        g_xattn = _g[0]
        g_ffn = _g[1]
        return (x, ctx_2048, mask_BxS2_ik0, g_xattn, g_ffn)
    x, ctx_2048, mask_BxS2_ik0, g_xattn, g_ffn = _rec_inputs()

    def _L0_xattn_setup():
        import jax, jax.numpy as jnp
        import numpy as np
        import math
        H = 512
        NH = 16
        HD = H // NH
        EPS_LN = 1e-05
        RES_SCALE_MAX = 0.3

        def _nan_clean(x, lim=10000.0):
            return jnp.nan_to_num(x, nan=0.0, posinf=lim, neginf=-lim)
        key = jax.random.key(seed)
        ks = jax.random.split(key, 12)
        B, S, T = (4, 512, 64)
        std = 1.0 / math.sqrt(H)
        return {'hidden_states': jax.random.normal(ks[0], (B, S, H), jnp.float32), 'audio_tokens': jax.random.normal(ks[1], (B, T, H), jnp.float32), 'attention_mask': jax.random.randint(ks[2], (B, T), 0, 2, jnp.int32), 'Wq': jax.random.normal(ks[3], (H, H), jnp.float32) * std, 'bq': jnp.zeros((H,), jnp.float32), 'Wk': jax.random.normal(ks[4], (H, H), jnp.float32) * std, 'bk': jnp.zeros((H,), jnp.float32), 'Wv': jax.random.normal(ks[5], (H, H), jnp.float32) * std, 'bv': jnp.zeros((H,), jnp.float32), 'Wo': jax.random.normal(ks[6], (H, H), jnp.float32) * std, 'bo': jnp.zeros((H,), jnp.float32), 'ln_gamma': jnp.ones((H,), jnp.float32), 'ln_beta': jnp.zeros((H,), jnp.float32), 'residual_scale': jnp.float32(0.05)}
    _L0_xattn_all = _L0_xattn_setup()
    _L0_xattn_in = {k: v for k, v in _L0_xattn_all.items() if k in ('Wq', 'bq', 'Wk', 'bk', 'Wv', 'bv', 'Wo', 'bo', 'ln_gamma', 'ln_beta', 'residual_scale')}
    del _L0_xattn_all

    def _L0_ffn_setup():
        import jax, jax.numpy as jnp
        import numpy as np
        HIDDEN = 512
        INTER = 1408
        B, S = (2, 512)

        def _ternary(key, shape):
            return jax.random.randint(key, shape, -1, 2).astype(jnp.float32)
        key = jax.random.key(seed)
        ks = jax.random.split(key, 7)
        x = jax.random.normal(ks[0], (B, S, HIDDEN), dtype=jnp.float32)
        gate_w = _ternary(ks[1], (INTER, HIDDEN))
        up_w = _ternary(ks[2], (INTER, HIDDEN))
        down_w = _ternary(ks[3], (HIDDEN, INTER))
        gate_s = jax.random.uniform(ks[4], (INTER,), minval=0.01, maxval=0.1, dtype=jnp.float32)
        up_s = jax.random.uniform(ks[5], (INTER,), minval=0.01, maxval=0.1, dtype=jnp.float32)
        down_s = jax.random.uniform(ks[6], (HIDDEN,), minval=0.01, maxval=0.1, dtype=jnp.float32)
        return {'x': x, 'gate_w': gate_w, 'up_w': up_w, 'down_w': down_w, 'gate_s': gate_s, 'up_s': up_s, 'down_s': down_s}
    _L0_ffn_all = _L0_ffn_setup()
    _L0_ffn_in = {k: v for k, v in _L0_ffn_all.items() if k in ('gate_w', 'up_w', 'down_w', 'gate_s', 'up_s', 'down_s')}
    del _L0_ffn_all

    def _L1_xattn_setup():
        import jax, jax.numpy as jnp
        import numpy as np
        EPS = 1e-06
        NUM_HEADS = 16

        def _feature_map(x):
            return jnp.where(x > 0, x + 1.0, jnp.exp(x))
        key = jax.random.key(seed)
        ks = jax.random.split(key, 7)
        B, L, S, D = (4, 1024, 1024, 512)
        sc = 1.0 / np.sqrt(D)
        return {'query': jax.random.normal(ks[0], (B, L, D), jnp.float32), 'kv': jax.random.normal(ks[1], (B, S, D), jnp.float32), 'Wq': jax.random.normal(ks[2], (D, D), jnp.float32) * sc, 'Wg': jax.random.normal(ks[3], (D, D), jnp.float32) * sc, 'bg': jnp.ones((D,), jnp.float32), 'Wkv': jax.random.normal(ks[4], (2 * D, D), jnp.float32) * sc, 'Wo': jax.random.normal(ks[5], (D, D), jnp.float32) * sc}
    _L1_xattn_all = _L1_xattn_setup()
    _L1_xattn_in = {k: v for k, v in _L1_xattn_all.items() if k in ('Wq', 'Wg', 'bg', 'Wkv', 'Wo')}
    del _L1_xattn_all

    def _L1_ffn_setup():
        import jax, jax.numpy as jnp
        import numpy as np
        DIM = 512
        INTER = 352
        N_EXPERTS = 16
        TOP_K = 2
        N_SHARED = 2
        SHARED_INTER = N_SHARED * INTER

        def _swiglu(t, wa, wb, wo):
            h = jax.nn.silu(t @ wa.T) * (t @ wb.T)
            return h @ wo.T
        key = jax.random.key(seed)
        ks = jax.random.split(key, 9)
        s = 0.02
        return {'x': jax.random.normal(ks[0], (4, 512, DIM), dtype=jnp.float32), 'gate_w': jax.random.normal(ks[1], (N_EXPERTS, DIM), dtype=jnp.float32) * s, 'w1': jax.random.normal(ks[2], (N_EXPERTS, INTER, DIM), dtype=jnp.float32) * s, 'w2': jax.random.normal(ks[3], (N_EXPERTS, DIM, INTER), dtype=jnp.float32) * s, 'w3': jax.random.normal(ks[4], (N_EXPERTS, INTER, DIM), dtype=jnp.float32) * s, 'sw1': jax.random.normal(ks[5], (SHARED_INTER, DIM), dtype=jnp.float32) * s, 'sw2': jax.random.normal(ks[6], (DIM, SHARED_INTER), dtype=jnp.float32) * s, 'sw3': jax.random.normal(ks[7], (SHARED_INTER, DIM), dtype=jnp.float32) * s}
    _L1_ffn_all = _L1_ffn_setup()
    _L1_ffn_in = {k: v for k, v in _L1_ffn_all.items() if k in ('gate_w', 'w1', 'w2', 'w3', 'sw1', 'sw2', 'sw3')}
    del _L1_ffn_all
    return {'x': x, 'ctx_2048': ctx_2048, 'mask_BxS2_ik0': mask_BxS2_ik0, 'g_xattn': g_xattn, 'g_ffn': g_ffn, 'L0_xattn_Wq': _L0_xattn_in['Wq'], 'L0_xattn_bq': _L0_xattn_in['bq'], 'L0_xattn_Wk': _L0_xattn_in['Wk'], 'L0_xattn_bk': _L0_xattn_in['bk'], 'L0_xattn_Wv': _L0_xattn_in['Wv'], 'L0_xattn_bv': _L0_xattn_in['bv'], 'L0_xattn_Wo': _L0_xattn_in['Wo'], 'L0_xattn_bo': _L0_xattn_in['bo'], 'L0_xattn_ln_gamma': _L0_xattn_in['ln_gamma'], 'L0_xattn_ln_beta': _L0_xattn_in['ln_beta'], 'L0_xattn_residual_scale': _L0_xattn_in['residual_scale'], 'L0_ffn_gate_w': _L0_ffn_in['gate_w'], 'L0_ffn_up_w': _L0_ffn_in['up_w'], 'L0_ffn_down_w': _L0_ffn_in['down_w'], 'L0_ffn_gate_s': _L0_ffn_in['gate_s'], 'L0_ffn_up_s': _L0_ffn_in['up_s'], 'L0_ffn_down_s': _L0_ffn_in['down_s'], 'L1_xattn_Wq': _L1_xattn_in['Wq'], 'L1_xattn_Wg': _L1_xattn_in['Wg'], 'L1_xattn_bg': _L1_xattn_in['bg'], 'L1_xattn_Wkv': _L1_xattn_in['Wkv'], 'L1_xattn_Wo': _L1_xattn_in['Wo'], 'L1_ffn_gate_w': _L1_ffn_in['gate_w'], 'L1_ffn_w1': _L1_ffn_in['w1'], 'L1_ffn_w2': _L1_ffn_in['w2'], 'L1_ffn_w3': _L1_ffn_in['w3'], 'L1_ffn_sw1': _L1_ffn_in['sw1'], 'L1_ffn_sw2': _L1_ffn_in['sw2'], 'L1_ffn_sw3': _L1_ffn_in['sw3']}

def reference(x, ctx_2048, mask_BxS2_ik0, g_xattn, g_ffn, L0_xattn_Wq, L0_xattn_bq, L0_xattn_Wk, L0_xattn_bk, L0_xattn_Wv, L0_xattn_bv, L0_xattn_Wo, L0_xattn_bo, L0_xattn_ln_gamma, L0_xattn_ln_beta, L0_xattn_residual_scale, L0_ffn_gate_w, L0_ffn_up_w, L0_ffn_down_w, L0_ffn_gate_s, L0_ffn_up_s, L0_ffn_down_s, L1_xattn_Wq, L1_xattn_Wg, L1_xattn_bg, L1_xattn_Wkv, L1_xattn_Wo, L1_ffn_gate_w, L1_ffn_w1, L1_ffn_w2, L1_ffn_w3, L1_ffn_sw1, L1_ffn_sw2, L1_ffn_sw3):
    import jax
    import jax.numpy as jnp

    def _L0_xattn_ref(hidden_states, audio_tokens, attention_mask, Wq, bq, Wk, bk, Wv, bv, Wo, bo, ln_gamma, ln_beta, residual_scale):
        import jax, jax.numpy as jnp
        import numpy as np
        import math
        H = 512
        NH = 16
        HD = H // NH
        EPS_LN = 1e-05
        RES_SCALE_MAX = 0.3

        def _nan_clean(x, lim=10000.0):
            return jnp.nan_to_num(x, nan=0.0, posinf=lim, neginf=-lim)
        B, S, _ = hidden_states.shape
        T = audio_tokens.shape[1]
        hs = _nan_clean(hidden_states).astype(jnp.float32)
        at = _nan_clean(audio_tokens).astype(jnp.float32)

        def proj(x, W, b, L):
            y = x @ W.T + b
            return y.reshape(B, L, NH, HD).transpose(0, 2, 1, 3)
        q = _nan_clean(proj(hs, Wq, bq, S))
        k = _nan_clean(proj(at, Wk, bk, T))
        v = _nan_clean(proj(at, Wv, bv, T))
        scale = max(math.sqrt(HD), 1e-08)
        scores = jnp.einsum('bhsd,bhtd->bhst', q, k) / scale
        scores = jnp.clip(scores, -50.0, 50.0)
        scores = jnp.nan_to_num(scores, nan=0.0, posinf=50.0, neginf=-50.0)
        attend = (attention_mask.astype(jnp.float32) > 0.5)[:, None, None, :]
        scores = jnp.where(attend, scores, -10000.0)
        scores = jnp.clip(scores, -50.0, 50.0)
        probs = jax.nn.softmax(scores, axis=-1)
        probs = jnp.nan_to_num(probs, nan=0.0, posinf=1.0, neginf=0.0)
        probs = probs / (probs.sum(axis=-1, keepdims=True) + 1e-08)
        ctx = jnp.einsum('bhst,bhtd->bhsd', probs, v)
        ctx = ctx.transpose(0, 2, 1, 3).reshape(B, S, H)
        delta = _nan_clean(ctx @ Wo.T + bo)
        rs = jnp.clip(residual_scale, 0.0, RES_SCALE_MAX)
        delta = rs * delta
        mu = delta.mean(axis=-1, keepdims=True)
        var = jnp.mean((delta - mu) ** 2, axis=-1, keepdims=True)
        delta = (delta - mu) / jnp.sqrt(var + EPS_LN) * ln_gamma + ln_beta
        return delta

    def _L0_ffn_ref(x, gate_w, up_w, down_w, gate_s, up_s, down_s):
        import jax, jax.numpy as jnp
        import numpy as np
        HIDDEN = 512
        INTER = 1408
        B, S = (2, 512)

        def _ternary(key, shape):
            return jax.random.randint(key, shape, -1, 2).astype(jnp.float32)
        b, s, h = x.shape
        xf = x.reshape(b * s, h)
        g = jnp.einsum('th,ih->ti', xf, gate_w) * gate_s
        u = jnp.einsum('th,ih->ti', xf, up_w) * up_s
        hdn = jax.nn.silu(g) * u
        out = jnp.einsum('ti,hi->th', hdn, down_w) * down_s
        return out.reshape(b, s, -1)

    def _L1_xattn_ref(query, kv, Wq, Wg, bg, Wkv, Wo):
        import jax, jax.numpy as jnp
        import numpy as np
        EPS = 1e-06
        NUM_HEADS = 16

        def _feature_map(x):
            return jnp.where(x > 0, x + 1.0, jnp.exp(x))
        B, L, D = query.shape
        S = kv.shape[1]
        H = NUM_HEADS
        hd = D // H
        q = query @ Wq.T
        gate = jax.nn.sigmoid(query @ Wg.T + bg)
        kvp = kv @ Wkv.T
        k, v = jnp.split(kvp, 2, axis=-1)
        q = _feature_map(q.reshape(B, L, H, hd).transpose(0, 2, 1, 3))
        k = _feature_map(k.reshape(B, S, H, hd).transpose(0, 2, 1, 3))
        v = v.reshape(B, S, H, hd).transpose(0, 2, 1, 3)
        kv_summary = jnp.einsum('bhsd,bhse->bhde', k, v)
        k_sum = k.sum(axis=-2)
        z = 1.0 / (jnp.einsum('bhld,bhd->bhl', q, k_sum)[..., None] + EPS)
        attn = jnp.einsum('bhld,bhde->bhle', q, kv_summary) * z
        attn = attn.transpose(0, 2, 1, 3).reshape(B, L, D)
        out = attn * gate @ Wo.T
        return out

    def _L1_ffn_ref(x, gate_w, w1, w2, w3, sw1, sw2, sw3):
        import jax, jax.numpy as jnp
        import numpy as np
        DIM = 512
        INTER = 352
        N_EXPERTS = 16
        TOP_K = 2
        N_SHARED = 2
        SHARED_INTER = N_SHARED * INTER

        def _swiglu(t, wa, wb, wo):
            h = jax.nn.silu(t @ wa.T) * (t @ wb.T)
            return h @ wo.T
        shape = x.shape
        t = x.reshape(-1, DIM)
        scores = jax.nn.softmax(t @ gate_w.T, axis=-1)
        weights, indices = jax.lax.top_k(scores, TOP_K)
        y = jnp.zeros_like(t)
        for e in range(N_EXPERTS):
            w_e = jnp.sum(jnp.where(indices == e, weights, 0.0), axis=-1)
            y = y + _swiglu(t, w1[e], w3[e], w2[e]) * w_e[:, None]
        z = _swiglu(t, sw1, sw3, sw2)
        return (y + z).reshape(shape)
    x = x + jnp.tanh(g_xattn[0]) * _L0_xattn_ref(_layernorm(x, axis=-1), ctx_2048, mask_BxS2_ik0, L0_xattn_Wq, L0_xattn_bq, L0_xattn_Wk, L0_xattn_bk, L0_xattn_Wv, L0_xattn_bv, L0_xattn_Wo, L0_xattn_bo, L0_xattn_ln_gamma, L0_xattn_ln_beta, L0_xattn_residual_scale)
    x = x + jnp.tanh(g_ffn[0]) * _L0_ffn_ref(_layernorm(x, axis=-1), L0_ffn_gate_w, L0_ffn_up_w, L0_ffn_down_w, L0_ffn_gate_s, L0_ffn_up_s, L0_ffn_down_s)
    x = x + jnp.tanh(g_xattn[1]) * _L1_xattn_ref(_layernorm(x, axis=-1), ctx_2048, L1_xattn_Wq, L1_xattn_Wg, L1_xattn_bg, L1_xattn_Wkv, L1_xattn_Wo)
    x = x + jnp.tanh(g_ffn[1]) * _L1_ffn_ref(_layernorm(x, axis=-1), L1_ffn_gate_w, L1_ffn_w1, L1_ffn_w2, L1_ffn_w3, L1_ffn_sw1, L1_ffn_sw2, L1_ffn_sw3)
    return x

_drawn_inputs = setup_inputs


def setup_inputs(seed=0):
    import zlib

    import numpy as np

    out = dict(_drawn_inputs(seed))
    spreads = {'g_ffn': (-1.0, 0.6),
     'L0_xattn_bq': (0.0, 0.1),
     'L0_xattn_bk': (0.0, 2.0),
     'L0_xattn_bv': (0.0, 0.1),
     'L0_xattn_bo': (0.0, 0.1),
     'L0_xattn_ln_gamma': (1.0, 0.2),
     'L0_xattn_ln_beta': (0.0, 0.1),
     'L1_xattn_bg': (1.0, 0.6)}
    factors = {'L1_xattn_Wq': 8.0,
     'L1_ffn_gate_w': 8.0,
     'L1_ffn_w1': 8.0,
     'L1_ffn_w2': 8.0,
     'L1_ffn_w3': 8.0,
     'L1_ffn_sw1': 8.0,
     'L1_ffn_sw2': 8.0,
     'L1_ffn_sw3': 8.0}
    for name, (base, spread) in spreads.items():
        noise = np.random.default_rng([zlib.crc32(name.encode()), seed]).standard_normal(out[name].shape)
        drawn = base * np.exp(spread * noise) if base else spread * noise
        out[name] = jnp.asarray(drawn.astype(out[name].dtype))
    for name, factor in factors.items():
        out[name] = (out[name] * factor).astype(out[name].dtype)
    return out
```

```python
from contextlib import ExitStack

import concourse.bass as bass
from concourse import mybir

F32 = mybir.dt.float32
I32 = mybir.dt.int32
U32 = mybir.dt.uint32
ALU = mybir.AluOpType
ACT = mybir.ActivationFunctionType
AX = mybir.AxisListType

P = 128
D = 512
KC = D // P
B, S, T = 8, 112, 375
TOK = B * S
NT = TOK // P
HALF = TOK // 2
TC, TP = 3, 125
H, HD = 16, 32
G = D // P
HG = P // HD
INTER = 1408
MC = INTER // P
SHARED = 704
SH_CHUNKS = [P] * 5 + [SHARED - 5 * P]
NE = 16
EI = 352
E_CHUNKS = [P, P, EI - 2 * P]
NSLOT = 4
ROWS_MAX = 29
LN_EPS = 1e-5
Z_EPS = 1e-6
P_EPS = 1e-8
CLIP = 50.0
SCALE = float(HD) ** -0.5


def flamingo(nc, x_in, ctx_in, mask_in, cols_in, rows_in, scal_in, wq0_in, wk0_in, wv0_in, wo0_in,
             gu0_in, wd0_in, wq1_in, wg1_in, wkv1_in, wo1_in, gate_in, sh13_in, sh2_in,
             e13_in, e2_in, out):
    with ExitStack() as stack:
        def sb(name, shape, dt=F32):
            return stack.enter_context(nc.sbuf_tensor(name, shape, dt))

        def sem(name):
            return stack.enter_context(nc.semaphore(name))

        ps = stack.enter_context(nc.psum_tensor("ps", [P, 8, 512], F32))

        x = sb("x", [P, NT, D])
        hT = sb("hT", [P, KC, TOK])
        rows = sb("rows", [P, 5 * D])
        lnt = sb("lnt", [P, 2, D])
        ident = sb("ident", [P, P])
        cols = sb("cols", [P, 12 + 2 * MC])
        scal = sb("scal", [P, 5])
        tg = sb("tg", [P, 4])
        rs = sb("rs", [P, 1])
        eps = sb("eps", [P, 1])
        mask_i = sb("mask_i", [TP, B * TC], I32)
        mscale = sb("mscale", [TP, B * TC])
        mbias = sb("mbias", [TP, B * TC])
        stats = sb("stats", [P, 2, 6])
        mv = sb("mv", [P, 4 * NT, 2])
        std = sb("std", [P, 4 * NT])
        rstd = sb("rstd", [P, 4 * NT])
        dmv = sb("dmv", [P, NT, 2])
        dstd = sb("dstd", [P, NT])
        drstd = sb("drstd", [P, NT])
        ks = sb("ks", [P, B, G])
        zsum = sb("zsum", [S, 2, 8])
        zinv = sb("zinv", [S, 2, 8])
        gate_w = sb("gate_w", [P, KC, NE])
        dest = sb("dest", [P, 2, NT], U32)
        wtop = sb("wtop", [P, NT, 2])
        tile_expert = sb("tile_expert", [P, 32], I32)
        expert_end = sb("expert_end", [P, NE], I32)
        tile_count = sb("tile_count", [P, 3], I32)

        A_QT, A_GT, A_KV = 0, KC * TOK, 2 * KC * TOK
        A_W = A_KV + B * D
        A_C = A_W + 8192
        A_K = A_C + 3072
        A_H = A_K + 6168
        A_O = A_H + 10380
        arena = sb("arena", [P, A_O + 2048])

        def at(off, *dims, rows_=P):
            n = 1
            for d in dims:
                n *= d
            v = arena[0:rows_, off:off + n]
            if len(dims) == 2:
                return v.rearrange("p (a b) -> p a b", a=dims[0])
            if len(dims) == 3:
                return v.rearrange("p (a b c) -> p a b c", a=dims[0], b=dims[1])
            if len(dims) == 4:
                return v.rearrange("p (a b c d) -> p a b c d", a=dims[0], b=dims[1], c=dims[2])
            return v

        qT = at(A_QT, KC, TOK)
        gT = at(A_GT, KC, TOK)
        wq0 = at(A_GT, KC, D)
        kvbd = at(A_KV, B, G, P)
        wk0 = at(A_W, KC, D)
        wv0 = at(A_W + 2048, KC, D)
        wkv1 = at(A_W + 4096, KC, 2 * D)
        ctxT = [at(A_C + s * KC * T, KC, T) for s in range(2)]
        kT = [at(A_K + s * KC * T, KC, T) for s in range(2)]
        v0 = [at(A_K + 3000 + s * 1584, TC, H, HD + 1, rows_=TP) for s in range(2)]
        k1 = at(A_H, TC, D, rows_=TP)
        v1 = at(A_H + 1536, TC, G, P + 1, rows_=TP)
        kexp = at(A_H + 3084, D, rows_=TP)
        krelu = at(A_H + 3596, D, rows_=TP)
        qbd = [at(A_H + 4108 + s * 1792, G, HG, S) for s in range(2)]
        probs = [at(A_H + 7692 + s * 1344, TC, HG * S, rows_=TP) for s in range(2)]
        ctok = lnt[0:S, 0, :]
        wo0 = at(A_O, KC, D)
        dtile = [at(A_W + s * D, D) for s in range(2)]
        gu0 = [at((A_W + m * 1024) if m < 8 else (A_C + (m - 8) * 1024), 2, KC, P) for m in range(MC)]
        wd0 = at(A_K, MC, D)
        h0 = at(A_H, MC, TOK)
        silu = [at(A_O + s * TOK, 2, HALF) for s in range(2)]
        ytmp = at(A_H + 9868, D)
        wq1, wg1, wo1 = (at(A_W + i * 2048, KC, D) for i in range(3))
        qexp = at(A_W + 6144, HALF)
        qrelu = at(A_W + 6144 + HALF, HALF)
        zero = at(A_C, D)
        zrec = at(A_C + D, G, S)
        ksbd = at(A_K, B, G, P)
        sh13 = at(A_H, KC, 2 * SHARED)
        sh2 = at(A_H + 5632, 6, D)
        hsh = at(A_K, 6, TOK)
        h3 = at(A_QT + 17408, NT, D)
        e13_all = arena[:, 0:NSLOT * 4352]
        xg = at(A_H + 8704, D)
        xgT = at(A_H + 9216, KC, P)
        hmoe = at(A_H + 9728, 3 * P)
        hmoeT = at(A_K + 5376, 3, P)
        smoe = at(A_K + 5760, EI)
        ymoe = lnt[:, 0, :]
        back = [[at(A_H + (2 * t + j) * D, D) for j in range(2)] for t in range(NT)]
        RT = NT * NE

        def rt(i):
            return rows[:, i * RT:(i + 1) * RT].rearrange("p (t e) -> p t e", t=NT)

        prob, one0, one1, both, place_, tmp16 = (rt(i) for i in range(6))
        iota16 = rows[:, 672:688]
        thr = rows[:, 688:695]
        cnt = rows[:, 695:711]
        rmax = rows[:, 711:718]
        rsum = rows[:, 718:725]
        top8 = rows[:, 728:784].rearrange("p (t e) -> p t e", t=NT)
        idxf = rows[:, 784:798].rearrange("p (t e) -> p t e", t=NT)
        fdest = rows[:, 800:807]
        scan = [rows[:, 808 + 32 * i:840 + 32 * i] for i in range(2)]
        ntile = rows[:, 872:888]
        nstart = rows[:, 888:904]
        iota29 = rows[:, 904:936]
        cmp = rows[:, 936:936 + 512]
        lower = rows[:, 1448:1576]
        ones = rows[:, 1576:1704]
        texpf = rows[:, 1704:1736]
        idx8 = sb("idx8", [P, NT, 8], U32)

        xs_dram = nc.dram_tensor("sorted_rows", (ROWS_MAX * P, D), F32, kind="Internal").ap()

        x_ld = sem("x_ld")
        small_ld = sem("small_ld")
        wq0_ld = sem("wq0_ld")
        wk0_ld = sem("wk0_ld")
        wv0_ld = sem("wv0_ld")
        wkv1_ld = sem("wkv1_ld")
        wo0_ld = sem("wo0_ld")
        wd0_ld = sem("wd0_ld")
        wq1_ld = sem("wq1_ld")
        wg1_ld = sem("wg1_ld")
        wo1_ld = sem("wo1_ld")
        sh_ld = sem("sh_ld")
        gate_ld = sem("gate_ld")
        consts_set = sem("consts_set")
        eps_set = sem("eps_set")
        tanh_set = sem("tanh_set")
        rows_set = sem("rows_set")
        mask_set = sem("mask_set")
        ones_set = sem("ones_set")
        kT_mm = sem("kT_mm")
        v0_mm = sem("v0_mm")
        k1_mm = sem("k1_mm")
        v1_mm = sem("v1_mm")
        kv_mm = sem("kv_mm")
        sc_mm = sem("sc_mm")
        pv_mm = sem("pv_mm")
        ct_mm = sem("ct_mm")
        q0_mm = sem("q0_mm")
        kT_sv = sem("kT_sv")
        v0_sv = sem("v0_sv")
        k1_exp = sem("k1_exp")
        k1_relu = sem("k1_relu")
        k1_sv = sem("k1_sv")
        v1_sv = sem("v1_sv")
        kv_sv = sem("kv_sv")
        clipped = sem("clipped")
        exped = sem("exped")
        norm_step = sem("norm_step")
        normed = sem("normed")
        ct_sv = sem("ct_sv")
        q0_sv = sem("q0_sv")
        q_spread = sem("q_spread")
        ln_var = sem("ln_var")
        ln_std = sem("ln_std")
        ln_out = sem("ln_out")
        ln_tr = sem("ln_tr")
        ln_T = sem("ln_T")
        d_var = sem("d_var")
        d_std = sem("d_std")
        y_mm = sem("y_mm")
        y_sv = sem("y_sv")
        ff_mm = sem("ff_mm")
        ff_silu = sem("ff_silu")
        ff_h = sem("ff_h")
        q1_mm = sem("q1_mm")
        q1_exp = sem("q1_exp")
        q1_relu = sem("q1_relu")
        q1_sv = sem("q1_sv")
        at_mm = sem("at_mm")
        at_sv = sem("at_sv")
        g1_mm = sem("g1_mm")
        g1_sv = sem("g1_sv")
        gated = sem("gated")
        ksbd_set = sem("ksbd_set")
        zero_set = sem("zero_set")
        filled = sem("filled")
        lg_mm = sem("lg_mm")
        lg_max = sem("lg_max")
        lg_exp = sem("lg_exp")
        lg_sv = sem("lg_sv")
        both_set = sem("both_set")
        rank_mm = sem("rank_mm")
        dest_set = sem("dest_set")
        tables_set = sem("tables_set")
        tri_set = sem("tri_set")
        scattered = sem("scattered")
        w_landed = sem("w_landed")
        xg_ld = sem("xg_ld")
        xg_tr = sem("xg_tr")
        xg_sv = sem("xg_sv")
        gu_mm = sem("gu_mm")
        m_silu = sem("m_silu")
        m_h = sem("m_h")
        hx_tr = sem("hx_tr")
        hx_sv = sem("hx_sv")
        d_mm = sem("d_mm")
        d_sv = sem("d_sv")
        y_st = sem("y_st")
        out_st = sem("out_st")
        dve_step = sem("dve_step")
        pool_step = sem("pool_step")
        act_held = sem("act_held")
        pool_held = sem("pool_held")
        ctx_ld = [sem(f"ctx_ld{i}") for i in range(2)]
        gu0_ld = [sem(f"gu0_ld{m}") for m in range(MC)]
        e_ld = [sem(f"e_ld{i}") for i in range(NSLOT)]

        back_ld = [sem(f"back_ld{t}") for t in range(NT)]

        block = stack.enter_context(nc.Block())

        def counts(engine):
            return [engine.value_load(tile_count[0:1, i:i + 1], min_val=NE - 2 + i, max_val=ROWS_MAX - 2 + i)
                    for i in range(3)]

        @block.sync
        def _(sp):
            sp.dma_start(ctxT[0], ctx_in[0]).then_inc(ctx_ld[0], 16)
            sp.dma_start(wk0, wk0_in).then_inc(wk0_ld, 16)
            sp.dma_start(cols[:], cols_in).then_inc(small_ld, 16)
            sp.dma_start(rows[:], rows_in.partition_broadcast(P)).then_inc(small_ld, 16)
            sp.dma_start(scal[:], scal_in.partition_broadcast(P)).then_inc(small_ld, 16)
            sp.dma_start(mask_i[:], mask_in).then_inc(small_ld, 16)
            sp.dma_start(wv0, wv0_in).then_inc(wv0_ld, 16)
            sp.dma_start(wkv1, wkv1_in).then_inc(wkv1_ld, 16)
            sp.dma_start(x[:], x_in.rearrange("(t p) d -> p t d", p=P)).then_inc(x_ld, 16)
            sp.dma_start(wq0, wq0_in).then_inc(wq0_ld, 16)
            sp.dma_start(ctxT[1], ctx_in[1]).then_inc(ctx_ld[1], 16)
            sp.dma_start(wo0, wo0_in).then_inc(wo0_ld, 16)
            sp.dma_start(gate_w[:], gate_in).then_inc(gate_ld, 16)
            with sp.Fori(2, B - 1, 2) as b:
                for slot in range(2):
                    sp.wait_ge(v1_mm, (b + slot) * 3 - 3)
                    sp.dma_start(ctxT[slot], ctx_in[bass.ds(b + slot, 1)].rearrange("o p k t -> (o p) k t")
                                 ).then_inc(ctx_ld[slot], 16)
            sp.wait_ge(v1_mm, 3 * B)
            for m in list(range(1, MC)):
                sp.dma_start(gu0[m], gu0_in[m]).then_inc(gu0_ld[m], 16)
            sp.wait_ge(pv_mm, 4 * B)
            sp.dma_start(wd0, wd0_in).then_inc(wd0_ld, 16)
            sp.wait_ge(ln_var, 2 * NT)
            sp.dma_start(gu0[0], gu0_in[0]).then_inc(gu0_ld[0], 16)
            sp.wait_ge(ff_mm, MC)
            sp.dma_start(wq1, wq1_in).then_inc(wq1_ld, 16)
            sp.dma_start(wg1, wg1_in).then_inc(wg1_ld, 16)
            sp.dma_start(wo1, wo1_in).then_inc(wo1_ld, 16)
            sp.wait_ge(y_sv, 2 * NT)
            sp.dma_start(sh13, sh13_in).then_inc(sh_ld, 16)
            sp.dma_start(sh2[:, 0:5, :], sh2_in[0:5 * P, :].rearrange("(c p) d -> p c d", p=P)).then_inc(sh_ld, 16)
            sp.dma_start(sh2[0:64, 5, :], sh2_in[5 * P:SHARED, :]).then_inc(sh_ld, 16)
            sp.wait_ge(y_mm, 3 * NT)

            def load_expert(e):
                slot = e % NSLOT
                w = slot * 4352
                sp.dma_start(arena[:, w:w + 2816], e13_in[e]).then_inc(e_ld[slot], 16)
                sp.dma_start(at(w + 2816, 2, D), e2_in[e, 0:2 * P, :].rearrange("(c p) d -> p c d", p=P)).then_inc(e_ld[slot], 16)
                sp.dma_start(at(w + 2816 + 2 * D, D, rows_=EI - 2 * P), e2_in[e, 2 * P:EI, :]).then_inc(e_ld[slot], 16)

            for e in range(NSLOT):
                load_expert(e)
            for e in range(NE):
                sp.wait_ge(e_ld[e % NSLOT], 48 * (e // NSLOT + 1))
                sp.sem_inc(w_landed, 1)
                if e == 0:
                    sp.wait_ge(tables_set, 1)
                elif e - 1 + NSLOT < NE:
                    last = sp.value_load(expert_end[0:1, e - 1:e], min_val=1, max_val=ROWS_MAX)
                    sp.wait_ge(d_mm, last)
                    load_expert(e - 1 + NSLOT)
            out_t = out.rearrange("(t p) d -> t p d", p=P)
            for t in range(NT):
                sp.wait_ge(out_st, 1 + t)
                sp.dma_start(out_t[t], x[:, t, :]).then_inc(x_ld, 16)
            sp.wait_ge(x_ld, 16 * (NT + 1))

        @block.tensor
        def _(pe):
            mm = nc.tensor.matmul

            def keys_T(b, slot, g):
                if g == 0:
                    if slot is not None:
                        pe.wait_ge(ctx_ld[slot], ctx_count(b))
                    pe.wait_ge(wk0_ld, 16)
                bank = 3 + g % 2
                if g >= 2:
                    pe.wait_ge(kT_sv, b * 4 + (g - 1))
                elif b_first(b):
                    pass
                elif g == 0:
                    pe.wait_ge(v0_sv, b * 3)
                else:
                    pe.wait_ge(k1_exp, b * 3)
                    pe.wait_ge(k1_relu, b * 3)
                for k in range(KC):
                    last = mm(ps[:, bank, 0:T], wk0[:, k, g * P:(g + 1) * P], ctxT[slot][:, k, :],
                              start=k == 0, stop=k == KC - 1)
                last.then_inc(kT_mm, 1)

            def values(b, slot, c, after_transposes):
                if c == 0:
                    pe.wait_ge(wv0_ld, 16)
                    pe.wait_ge(wkv1_ld, 16)
                for j, (w, bank, done) in enumerate([(wv0, 3, v0_mm), (wkv1[:, :, 0:D], 4, k1_mm),
                                                     (wkv1[:, :, D:2 * D], 5, v1_mm)]):
                    if j == 0:
                        if c == 0:
                            pe.wait_ge(kT_sv, b * 4 + 3)
                        else:
                            pe.wait_ge(v0_sv, b * 3 + c)
                    elif j == 1 and c == 0:
                        pe.wait_ge(kT_sv, b * 4 + 4)
                    elif j == 1:
                        pe.wait_ge(k1_exp, b * 3 + c)
                        pe.wait_ge(k1_relu, b * 3 + c)
                    else:
                        if not (b_first(b) and c == 0):
                            pe.wait_ge(v1_sv, b * 3 + c)
                        if c == 0 and after_transposes:
                            pe.wait_ge(ct_sv, b - 1)
                    for k in range(KC):
                        last = mm(ps[0:TP, bank, :], ctxT[slot][:, k, c * TP:(c + 1) * TP], w[:, k, :],
                                  start=k == 0, stop=k == KC - 1)
                    last.then_inc(done, 1)

            def kv_summary(b):
                pe.wait_ge(k1_sv, b * 3 + 3)
                pe.wait_ge(v1_sv, b * 3 + 3)
                pe.wait_ge(ones_set, 3)
                if not b_first(b):
                    pe.wait_ge(clipped, b * 4)
                for g in range(G):
                    for c in range(TC):
                        last = mm(ps[:, g // 2, (g % 2) * 129:(g % 2) * 129 + 129],
                                  k1[:, c, g * P:(g + 1) * P], v1[:, c, g, :], start=c == 0, stop=c == TC - 1)
                    if g % 2:
                        last.then_inc(kv_mm, 1)

            def head_transposes(b):
                pe.wait_ge(normed, b * 2 + 2)
                pe.wait_ge(v1_sv, b * 3 + 6 if not is_last(b) else 3 * B)
                for k in range(KC):
                    last = nc.tensor.transpose(ps[:, 5, k * S:(k + 1) * S], ctok[:, k * P:(k + 1) * P], ident[0:S, 0:S])
                last.then_inc(ct_mm, 1)

            def scores(b, slot, g):
                if g == 0:
                    pe.wait_ge(q_spread, b * 4 + 4)
                    pe.wait_ge(kT_sv, b * 4 + 4)
                    pe.wait_ge(kv_sv, b * 2 + 2)
                if g > 0 or not b_first(b):
                    pe.wait_ge(clipped, b * 4 + g)
                for c in range(TC):
                    last = mm(ps[0:TP, c, 0:HG * S], kT[slot][:, g, c * TP:(c + 1) * TP],
                              qbd[slot][:, g, :, :], start=True, stop=True)
                last.then_inc(sc_mm, 1)

            def mix(b, slot, g):
                pe.wait_ge(exped, b * 4 + g + 1)
                pe.wait_ge(v0_sv, b * 3 + 3)
                if g % 2 == 0 and not b_first(b):
                    pe.wait_ge(normed, b * 2 - 1 + g // 2)
                for h in range(HG):
                    o = (g % 2) * 4 + h
                    for c in range(TC):
                        last = mm(ps[0:S, 6 + g // 2, o * 33:o * 33 + 33], probs[g % 2][:, c, h * S:(h + 1) * S],
                                  v0[slot][:, c, 4 * g + h, :], start=c == 0, stop=c == TC - 1)
                last.then_inc(pv_mm, 1)

            def b_first(b):
                return isinstance(b, int) and b == 0

            def is_last(b):
                return isinstance(b, int) and b == B - 1

            def ctx_count(b):
                return 16 * (b // 2 + 1) if isinstance(b, int) else b * 8 + (16 - 8 * ctx_count.odd)

            ctx_count.odd = 0

            def batch(b, slot, more, nslot_odd):
                for g in range(G):
                    scores(b, slot, g)
                    if more:
                        ctx_count.odd = nslot_odd
                        if g == 0:
                            for gg in range(G):
                                keys_T(b + 1, 1 - slot, gg)
                    if g == 0 and not b_first(b):
                        head_transposes(b - 1)
                    if more and g > 0:
                        values(b + 1, 1 - slot, g - 1, not b_first(b))
                    mix(b, slot, g)
                if more:
                    kv_summary(b + 1)

            for g in range(G):
                keys_T(0, 0, g)
            for c in range(TC):
                values(0, 0, c, False)
            kv_summary(0)

            def ln_transposes(n):
                t = n % NT
                bank = (6 if n < NT else 2) + t % 2
                if n == 0:
                    pe.wait_ge(consts_set, 1)
                pe.wait_ge(ln_out, n + 1)
                if t >= 2:
                    pe.wait_ge(ln_T, n - 1)
                elif n >= NT:
                    pe.wait_ge(ln_T, n // NT * NT)
                src = h3[:, t, :] if n >= 3 * NT else lnt[:, n % 2, :]
                for k in range(KC):
                    last = nc.tensor.transpose(ps[:, bank, k * P:(k + 1) * P], src[:, k * P:(k + 1) * P], ident[:])
                last.then_inc(ln_tr, 1)

            for t in range(NT):
                ln_transposes(t)
            pe.wait_ge(ln_T, NT)
            pe.wait_ge(wq0_ld, 16)
            for m in range(KC):
                for n in range(2):
                    i = 2 * m + n
                    if i >= 2:
                        pe.wait_ge(q0_sv, i - 1)
                    for k in range(KC):
                        last = mm(ps[:, 6 + n, 0:HALF], wq0[:, k, m * P:(m + 1) * P],
                                  hT[:, k, n * HALF:(n + 1) * HALF], start=k == 0, stop=k == KC - 1)
                    last.then_inc(q0_mm, 1)

            pe.wait_ge(q0_sv, 8)
            batch(0, 0, True, 1)
            with pe.Fori(1, B - 2, 2) as b:
                batch(b, 1, True, 0)
                batch(b + 1, 0, True, 1)
            batch(B - 1, 1, False, 0)
            head_transposes(B - 1)

            def to_tokens(n, operands):
                if n >= 2:
                    pe.wait_ge(y_sv, n - 1)
                for i, (a, w) in enumerate(operands):
                    last = mm(ps[:, n % 2, :], a, w, start=i == 0, stop=i == len(operands) - 1)
                last.then_inc(y_mm, 1)

            def tokens_then_ln(stage, operands_of):
                for t in range(NT):
                    to_tokens(stage * NT + t, operands_of(t))
                    if t >= 2:
                        ln_transposes((stage + 1) * NT + t - 2)
                for t in (NT - 2, NT - 1):
                    ln_transposes((stage + 1) * NT + t)

            def tok(buf, k, t):
                return buf[:, k, t * P:(t + 1) * P]

            pe.wait_ge(wo0_ld, 16)
            pe.wait_ge(ct_sv, B)
            pe.wait_ge(clipped, 4 * B)
            tokens_then_ln(0, lambda t: [(tok(hT, k, t), wo0[:, k, :]) for k in range(KC)])

            def gate_up(i, m, size, gate, up):
                for j, w in enumerate((gate, up)):
                    for n in range(2):
                        for k in range(KC):
                            last = mm(ps[0:size, 4 * (m % 2) + 2 * j + n, 0:HALF], w(k),
                                      hT[:, k, n * HALF:(n + 1) * HALF], start=k == 0, stop=k == KC - 1)
                last.then_inc(ff_mm, 1)

            pe.wait_ge(ln_T, 2 * NT)
            pe.wait_ge(y_sv, NT)
            for m in range(MC):
                pe.wait_ge(gu0_ld[m], 16)
                if m >= 2:
                    pe.wait_ge(ff_silu, m - 1)
                    pe.wait_ge(ff_h, m - 1)
                gate_up(m, m, P, lambda k: gu0[m][:, 0, k, :], lambda k: gu0[m][:, 1, k, :])
            pe.wait_ge(ff_h, MC)
            pe.wait_ge(wd0_ld, 16)
            tokens_then_ln(1, lambda t: [(tok(h0, m, t), wd0[:, m, :]) for m in range(MC)])

            pe.wait_ge(ln_T, 3 * NT)
            pe.wait_ge(wq1_ld, 16)
            pe.wait_ge(wg1_ld, 16)
            for i in range(8):
                m, n = i // 2, i % 2
                if i >= 4:
                    pe.wait_ge(q1_exp, i - 3)
                    pe.wait_ge(q1_relu, i - 3)
                for k in range(KC):
                    last = mm(ps[:, 4 + i % 4, 0:HALF], wq1[:, k, m * P:(m + 1) * P],
                              hT[:, k, n * HALF:(n + 1) * HALF], start=k == 0, stop=k == KC - 1)
                last.then_inc(q1_mm, 1)
            pe.wait_ge(q1_sv, 8)
            pe.wait_ge(ksbd_set, 5)
            pe.wait_ge(y_sv, 2 * NT)
            for b in range(B):
                if b >= 2:
                    pe.wait_ge(at_sv, b - 1)
                for j, w in enumerate((kvbd, ksbd)):
                    for g in range(G):
                        last = mm(ps[:, 2 * j + b % 2, g * S:(g + 1) * S], w[:, b, g, :],
                                  qT[:, g, b * S:(b + 1) * S], start=True, stop=True)
                last.then_inc(at_mm, 1)
            for i in range(8):
                m, n = i // 2, i % 2
                if i >= 4:
                    pe.wait_ge(g1_sv, i - 3)
                for k in range(KC):
                    last = mm(ps[:, 4 + i % 4, 0:HALF], wg1[:, k, m * P:(m + 1) * P],
                              hT[:, k, n * HALF:(n + 1) * HALF], start=k == 0, stop=k == KC - 1)
                last.then_inc(g1_mm, 1)
            pe.wait_ge(gated, KC)
            pe.wait_ge(wo1_ld, 16)
            tokens_then_ln(2, lambda t: [(tok(qT, k, t), wo1[:, k, :]) for k in range(KC)])

            pe.wait_ge(ln_T, 4 * NT)
            pe.wait_ge(gate_ld, 16)
            pe.wait_ge(y_sv, 3 * NT)
            for t in range(NT):
                for k in range(KC):
                    last = mm(ps[:, 7, t * NE:(t + 1) * NE], tok(hT, k, t), gate_w[:, k, :],
                              start=k == 0, stop=k == KC - 1)
            last.then_inc(lg_mm, 1)
            pe.wait_ge(sh_ld, 48)
            for m, size in enumerate(SH_CHUNKS):
                if m == 1:
                    pe.wait_ge(lg_sv, 1)
                if m >= 2:
                    pe.wait_ge(ff_silu, MC + m - 1)
                    pe.wait_ge(ff_h, MC + m - 1)
                lo = m * P
                gate_up(MC + m, m, size, lambda k: sh13[:, k, lo:lo + size],
                        lambda k: sh13[:, k, SHARED + lo:SHARED + lo + size])
            pe.wait_ge(ff_h, MC + 6)
            pe.wait_ge(both_set, 1)
            pe.wait_ge(tri_set, 4)
            mm(ps[:, 2, 0:RT], lower, both.rearrange("p t e -> p (t e)"), start=True, stop=True)
            mm(ps[:, 3, 0:RT], ones, both.rearrange("p t e -> p (t e)"), start=True, stop=True
               ).then_inc(rank_mm, 1)
            for t in range(NT):
                to_tokens(3 * NT + t, [(hsh[0:z, m, t * P:(t + 1) * P], sh2[0:z, m, :])
                                       for m, z in enumerate(SH_CHUNKS)])

            pe.wait_ge(tables_set, 1)
            last2, last1, tiles = counts(pe)

            def slot_of(n):
                e = pe.value_load(tile_expert[0:1, bass.ds(n, 1)], min_val=0, max_val=NE - 1)
                return e, (e % NSLOT) * 4352

            def rows_T(n):
                pe.wait_ge(xg_ld, n * 16 + 16)
                for k in range(KC):
                    last = nc.tensor.transpose(ps[:, 6, k * P:(k + 1) * P], xg[:, k * P:(k + 1) * P], ident[:])
                last.then_inc(xg_tr, 1)

            def up_expert(n):
                e, w = slot_of(n)
                pe.wait_ge(w_landed, e + 1)
                pe.wait_ge(xg_sv, n + 1)
                for j in range(2):
                    for k in range(KC):
                        last = mm(ps[:, 4 + j, 0:EI], xgT[:, k, :],
                                  arena[:, bass.ds(w + (k * 2 * EI + j * EI), EI)], start=k == 0, stop=k == KC - 1)
                last.then_inc(gu_mm, 1)

            def down_expert(n):
                e, w = slot_of(n)
                pe.wait_ge(hx_sv, n + 1)
                if not b_first(n):
                    pe.wait_ge(d_sv, n)
                for c, z in enumerate(E_CHUNKS):
                    last = mm(ps[:, 3, :], hmoeT[0:z, c, :], arena[0:z, bass.ds(w + (2816 + c * D), D)],
                              start=c == 0, stop=c == 2)
                last.then_inc(d_mm, 1)

            def hidden_T(n):
                pe.wait_ge(m_h, n + 1)
                for c in range(3):
                    last = nc.tensor.transpose(ps[:, 7, c * P:(c + 1) * P], hmoe[:, c * P:(c + 1) * P], ident[:])
                last.then_inc(hx_tr, 1)

            pe.wait_ge(y_sv, 4 * NT)
            rows_T(0)
            up_expert(0)
            rows_T(1)
            hidden_T(0)
            with pe.Fori(1, last1) as n:
                up_expert(n)
                rows_T(n + 1)
                down_expert(n - 1)
                hidden_T(n)
            up_expert(last1)
            down_expert(last2)
            hidden_T(last1)
            down_expert(last1)

        @block.scalar
        def _(act):
            fn = nc.scalar.activation

            def keys_T(b, slot, g):
                act.wait_ge(kT_mm, b * 4 + g + 1)
                fn(kT[slot][:, g, :], ps[:, 3 + g % 2, 0:T], ACT.Identity, bias=cols[:, 4 + g:5 + g]
                   ).then_inc(kT_sv, 1)

            def values(b, c):
                act.wait_ge(k1_mm, b * 3 + c + 1)
                if not (isinstance(b, int) and b == 0 and c == 0):
                    act.wait_ge(k1_sv, b * 3 + c)
                fn(kexp, ps[0:TP, 4, :], ACT.Exp).then_inc(k1_exp, 1)
                act.wait_ge(v1_mm, b * 3 + c + 1)
                fn(v1[:, c, :, 0:P], ps[0:TP, 5, :].rearrange("p (g e) -> p g e", g=G), ACT.Copy
                   ).then_inc(v1_sv, 1)

            def ln(n):
                act.wait_ge(ln_var, n + 1)
                fn(std[:, n:n + 1], mv[:, n, 1:2], ACT.Sqrt, bias=eps[:, 0:1]).then_inc(ln_std, 1)

            def ln_save(n):
                t = n % NT
                act.wait_ge(ln_tr, n + 1)
                fn(hT[:, :, t * P:(t + 1) * P], ps[:, (6 if n < NT else 2) + t % 2, :].rearrange("p (k t) -> p k t", k=KC),
                   ACT.Copy).then_inc(ln_T, 1)

            act.wait_ge(small_ld, 64)
            fn(tg[:], scal[:, 0:4], ACT.Tanh).then_inc(tanh_set, 1)
            for g in range(G):
                keys_T(0, 0, g)
            for c in range(TC):
                values(0, c)
            act.wait_ge(eps_set, 1)
            for t in range(NT):
                ln(t)
            for t in range(NT):
                ln_save(t)
            for m in range(KC):
                for n in range(2):
                    act.wait_ge(q0_mm, 2 * m + n + 1)
                    fn(qT[:, m, n * HALF:(n + 1) * HALF], ps[:, 6 + n, 0:HALF], ACT.Identity,
                       bias=cols[:, m:m + 1]).then_inc(q0_sv, 1)

            act.wait_ge(mask_set, 2)

            def batch(b, slot, more, first):
                for g in range(G):
                    act.wait_ge(clipped, b * 4 + g + 1)
                    act.sem_inc(act_held, 1)
                    for c in range(TC):
                        last = fn(probs[g % 2][:, c, :], probs[g % 2][:, c, :], ACT.Exp,
                                  bias=mbias[:, bass.ds(b * 3 + c, 1)], scale=mscale[:, bass.ds(b * 3 + c, 1)])
                    last.then_inc(exped, 1)
                    if more and g == 0:
                        for gg in range(G):
                            keys_T(b + 1, 1 - slot, gg)
                    if g == 0 and not first:
                        heads_save(b - 1)
                    if more and g > 0:
                        values(b + 1, g - 1)

            def heads_save(b):
                act.wait_ge(ct_mm, b + 1)
                act.sem_inc(act_held, 1)
                fn(hT[:, :, bass.ds(b * S, S)], ps[:, 5, 0:KC * S].rearrange("p (k t) -> p k t", k=KC), ACT.Copy
                   ).then_inc(ct_sv, 1)

            batch(0, 0, True, True)
            with act.Fori(1, B - 2, 2) as b:
                batch(b, 1, True, False)
                batch(b + 1, 0, True, False)
            batch(B - 1, 1, False, False)
            heads_save(B - 1)

            for t in range(NT):
                act.wait_ge(d_var, t + 1)
                fn(dstd[:, t:t + 1], dmv[:, t, 1:2], ACT.Sqrt, bias=eps[:, 0:1]).then_inc(d_std, 1)
                ln(NT + t)
                if t >= 1:
                    ln_save(NT + t - 1)
            ln_save(2 * NT - 1)

            for m in range(MC):
                act.wait_ge(ff_mm, m + 1)
                if m >= 2:
                    act.wait_ge(ff_h, m - 1)
                fn(silu[m % 2], ps[:, 4 * (m % 2):4 * (m % 2) + 2, 0:HALF], ACT.Silu,
                   scale=cols[:, 12 + m:13 + m]).then_inc(ff_silu, 1)

            def ln_stage(k):
                for t in range(NT):
                    ln(k * NT + t)
                    if t >= 1:
                        ln_save(k * NT + t - 1)
                ln_save(k * NT + NT - 1)

            ln_stage(2)
            for i in range(8):
                act.wait_ge(q1_mm, i + 1)
                if i >= 1:
                    act.wait_ge(q1_sv, i)
                fn(qexp, ps[:, 4 + i % 4, 0:HALF], ACT.Exp).then_inc(q1_exp, 1)
            for i in range(8):
                m, n = i // 2, i % 2
                act.wait_ge(g1_mm, i + 1)
                fn(gT[:, m, n * HALF:(n + 1) * HALF], ps[:, 4 + i % 4, 0:HALF], ACT.Sigmoid,
                   bias=cols[:, 8 + m:9 + m]).then_inc(g1_sv, 1)
            ln_stage(3)
            act.wait_ge(lg_max, 1)
            fn(prob.rearrange("p t e -> p (t e)"), prob.rearrange("p t e -> p (t e)"), ACT.Exp).then_inc(lg_exp, 1)
            for m, size in enumerate(SH_CHUNKS):
                act.wait_ge(ff_mm, MC + m + 1)
                act.wait_ge(ff_h, MC + m - 1)
                fn(silu[m % 2][0:size], ps[0:size, 4 * (m % 2):4 * (m % 2) + 2, 0:HALF], ACT.Silu
                   ).then_inc(ff_silu, 1)

            act.wait_ge(tables_set, 1)
            last2, last1, tiles = counts(act)

            def rows_save(n):
                act.wait_ge(xg_tr, n + 1)
                fn(xgT, ps[:, 6, :].rearrange("p (k t) -> p k t", k=KC), ACT.Copy).then_inc(xg_sv, 1)

            def silu_tile(n):
                act.wait_ge(gu_mm, n + 1)
                fn(smoe, ps[:, 4, 0:EI], ACT.Silu).then_inc(m_silu, 1)

            rows_save(0)
            with act.Fori(0, last1) as n:
                silu_tile(n)
                rows_save(n + 1)
            silu_tile(last1)

        @block.vector
        def _(dve):
            v = nc.vector
            count = [0]

            def then(ins):
                count[0] += 1
                ins.then_inc(dve_step, 1)
                dve.wait_ge(dve_step, count[0])

            def ln_stats(n):
                then(v.bn_stats(stats[:, n % 2, :], x[:, n % NT, :]))
                v.bn_aggr(mv[:, n, :], stats[:, n % 2, :]).then_inc(ln_var, 1)

            def ln_norm(n):
                dve.wait_ge(ln_std, n + 1)
                then(v.reciprocal(rstd[:, n:n + 1], std[:, n:n + 1]))
                if n >= 2:
                    dve.wait_ge(ln_tr, n - 1)
                dst = h3[:, n % NT, :] if n >= 3 * NT else lnt[:, n % 2, :]
                v.tensor_scalar(dst, x[:, n % NT, :], mv[:, n, 0:1], rstd[:, n:n + 1], ALU.subtract, ALU.mult
                                ).then_inc(ln_out, 1)

            v.memset(eps[:], LN_EPS).then_inc(eps_set, 1)
            for slot in range(2):
                v.memset(v0[slot][:, :, :, HD:HD + 1], 1.0).then_inc(ones_set, 1)
            v.memset(v1[:, :, :, P:P + 1], 1.0).then_inc(ones_set, 1)
            dve.wait_ge(small_ld, 64)
            then(v.tensor_scalar(mscale[:], mask_i[:], 0.5, None, ALU.is_gt))
            v.tensor_scalar(mbias[:], mscale[:], CLIP, -CLIP, ALU.mult, ALU.add).then_inc(mask_set, 1)
            dve.wait_ge(mask_set, 1)
            v.tensor_scalar(mscale[:], mscale[:], SCALE, None, ALU.mult).then_inc(mask_set, 1)
            bv, bo, gamma, beta, down_s = (rows[:, i * D:(i + 1) * D] for i in range(5))
            then(v.tensor_scalar(rs[:], scal[:, 4:5], 0.0, 0.3, ALU.max, ALU.min))
            dve.wait_ge(tanh_set, 1)
            v.tensor_scalar(bo, bo, rs[:, 0:1], None, ALU.mult).then_inc(rows_set, 1)
            v.tensor_scalar(gamma, gamma, tg[:, 0:1], None, ALU.mult).then_inc(rows_set, 1)
            v.tensor_scalar(beta, beta, tg[:, 0:1], None, ALU.mult).then_inc(rows_set, 1)
            v.tensor_scalar(down_s, down_s, tg[:, 2:3], None, ALU.mult).then_inc(rows_set, 1)
            dve.wait_ge(x_ld, 16)
            for t in range(NT):
                ln_stats(t)

            def values(b, slot, c):
                dve.wait_ge(v0_mm, b * 3 + c + 1)
                v.tensor_tensor(v0[slot][:, c, :, 0:HD], ps[0:TP, 3, :].rearrange("p (h d) -> p h d", h=H),
                                bv[0:TP].rearrange("p (h d) -> p h d", h=H), ALU.add).then_inc(v0_sv, 1)
                dve.wait_ge(k1_exp, b * 3 + c + 1)
                v.tensor_scalar(krelu, ps[0:TP, 4, :], 0.0, None, ALU.max).then_inc(k1_relu, 1)
                dve.wait_ge(k1_relu, b * 3 + c + 1)
                v.scalar_tensor_tensor(k1[:, c, :], kexp, 1.0, krelu, ALU.min, ALU.add).then_inc(k1_sv, 1)

            def kv_save(b):
                for pair in range(2):
                    dve.wait_ge(kv_mm, b * 2 + pair + 1)
                    bank = ps[:, pair, 0:2 * 129].rearrange("p (g e) -> p g e", g=2)
                    for h in range(HG):
                        r = slice(h * HD, (h + 1) * HD)
                        for g in range(2):
                            v.tensor_copy(kv_flat[r, bass.ds(b * D + ((2 * pair + g) * P + h * HD), HD)],
                                          bank[r, g, h * HD:(h + 1) * HD])
                    v.tensor_copy(ks_flat[:, bass.ds(b * G + 2 * pair, 2)], bank[:, :, P]).then_inc(kv_sv, 1)

            kv_flat = at(A_KV, B * D)
            ks_flat = ks[:].rearrange("p b g -> p (b g)")
            dve.wait_ge(pool_step, 3)
            for c in range(TC):
                values(0, 0, c)
            kv_save(0)
            for t in range(NT):
                ln_norm(t)

            def clip(b, g, guard):
                dve.wait_ge(sc_mm, b * 4 + g + 1)
                if guard:
                    dve.wait_ge(pv_mm, b * 4 + g - 1)
                v.tensor_scalar(probs[g % 2], ps[0:TP, 0:TC, 0:HG * S], -CLIP / SCALE, CLIP / SCALE,
                                ALU.max, ALU.min).then_inc(clipped, 1)

            def normalise(b, half, first):
                dve.wait_ge(pv_mm, b * 4 + 2 * half + 2)
                bank = ps[0:S, 6 + half, 0:8 * 33].rearrange("p (h e) -> p h e", h=8)
                v.tensor_copy(zsum[:, half, :], bank[:, :, HD]).then_inc(norm_step, 1)
                dve.wait_ge(norm_step, b * 6 + 3 * half + 1)
                v.scalar_tensor_tensor(zinv[:, half, :], zsum[:, half, :], P_EPS, zsum[:, half, :], ALU.mult, ALU.add
                                       ).then_inc(norm_step, 1)
                dve.wait_ge(norm_step, b * 6 + 3 * half + 2)
                v.reciprocal(zinv[:, half, :], zinv[:, half, :]).then_inc(norm_step, 1)
                dve.wait_ge(norm_step, b * 6 + 3 * half + 3)
                if not first:
                    dve.wait_ge(ct_mm, b)
                v.tensor_tensor(ctok[:, half * 256:(half + 1) * 256].rearrange("p (h d) -> p h d", h=8),
                                bank[:, :, 0:HD], zinv[:, half, :].unsqueeze(2).broadcast_to([S, 8, HD]),
                                ALU.mult).then_inc(normed, 1)

            def batch(b, slot, more, first):
                for g in range(G):
                    if g == 2:
                        normalise(b, 0, first)
                    clip(b, g, not (first and g < 2))
                    if more and g > 0:
                        values(b + 1, 1 - slot, g - 1)
                normalise(b, 1, first)
                if more:
                    kv_save(b + 1)

            batch(0, 0, True, True)
            with dve.Fori(1, B - 2, 2) as b:
                batch(b, 1, True, False)
                batch(b + 1, 0, True, False)
            batch(B - 1, 1, False, False)

            dve.wait_ge(rows_set, 4)
            dve.wait_ge(v1_mm, 3 * B)
            for t in range(NT):
                d = dtile[t % 2]
                dve.wait_ge(y_mm, t + 1)
                v.scalar_tensor_tensor(d, ps[:, t % 2, :], rs[:, 0:1], bo, ALU.mult, ALU.add).then_inc(y_sv, 1)
                dve.wait_ge(y_sv, t + 1)
                then(v.bn_stats(stats[:, 0, :], d))
                v.bn_aggr(dmv[:, t, :], stats[:, 0, :]).then_inc(d_var, 1)
                dve.wait_ge(d_std, t + 1)
                then(v.reciprocal(drstd[:, t:t + 1], dstd[:, t:t + 1]))
                then(v.tensor_scalar(d, d, dmv[:, t, 0:1], drstd[:, t:t + 1], ALU.subtract, ALU.mult))
                then(v.tensor_tensor(d, d, gamma, ALU.mult))
                then(v.tensor_tensor(d, d, beta, ALU.add))
                then(v.tensor_tensor(x[:, t, :], x[:, t, :], d, ALU.add))
                ln_stats(NT + t)
                if t >= 1:
                    ln_norm(NT + t - 1)
            ln_norm(2 * NT - 1)

            def hidden(i, m, size, scale, into):
                dve.wait_ge(ff_mm, i + 1)
                dve.wait_ge(ff_silu, i + 1)
                v.scalar_tensor_tensor(into[0:size, m, :].rearrange("p (n t) -> p n t", n=2),
                                       ps[0:size, 4 * (m % 2) + 2:4 * (m % 2) + 4, 0:HALF], scale,
                                       silu[m % 2][0:size], ALU.mult, ALU.mult).then_inc(ff_h, 1)

            for m in range(MC):
                hidden(m, m, P, cols[:, 12 + MC + m:13 + MC + m], h0)
            for t in range(NT):
                dve.wait_ge(y_mm, NT + t + 1)
                v.tensor_tensor(ytmp, ps[:, (NT + t) % 2, :], down_s, ALU.mult).then_inc(y_sv, 1)
                dve.wait_ge(y_sv, NT + t + 1)
                then(v.tensor_tensor(x[:, t, :], x[:, t, :], ytmp, ALU.add))
                ln_stats(2 * NT + t)
                if t >= 1:
                    ln_norm(2 * NT + t - 1)
            dve.wait_ge(ksbd_set, 1)
            for h in range(HG):
                r = slice(h * HD, (h + 1) * HD)
                v.tensor_copy(at(A_K, B * G, P)[r, :, h * HD:(h + 1) * HD],
                              ks_flat[r, :].unsqueeze(2).broadcast_to([HD, B * G, HD])).then_inc(ksbd_set, 1)
            ln_norm(3 * NT - 1)

            for i in range(8):
                m, n = i // 2, i % 2
                dve.wait_ge(q1_exp, i + 1)
                v.tensor_scalar(qrelu, ps[:, 4 + i % 4, 0:HALF], 0.0, None, ALU.max).then_inc(q1_relu, 1)
                dve.wait_ge(q1_relu, i + 1)
                v.scalar_tensor_tensor(qT[:, m, n * HALF:(n + 1) * HALF], qexp, 1.0, qrelu, ALU.min, ALU.add
                                       ).then_inc(q1_sv, 1)
                dve.wait_ge(q1_sv, i + 1)
            for b in range(B):
                dve.wait_ge(at_mm, b + 1)
                then(v.tensor_scalar(zrec, ps[:, 2 + b % 2, 0:G * S].rearrange("p (g t) -> p g t", g=G),
                                     Z_EPS, None, ALU.add))
                then(v.reciprocal(zrec, zrec))
                v.tensor_tensor(qT[:, :, b * S:(b + 1) * S], ps[:, b % 2, 0:G * S].rearrange("p (g t) -> p g t", g=G),
                                zrec, ALU.mult).then_inc(at_sv, 1)
                dve.wait_ge(at_sv, b + 1)
            for m in range(KC):
                dve.wait_ge(g1_sv, 2 * m + 2)
                v.tensor_tensor(qT[:, m, :], qT[:, m, :], gT[:, m, :], ALU.mult).then_inc(gated, 1)
            dve.wait_ge(filled, 16)
            for t in range(NT):
                dve.wait_ge(y_mm, 2 * NT + t + 1)
                v.scalar_tensor_tensor(x[:, t, :], ps[:, (2 * NT + t) % 2, :], tg[:, 1:2], x[:, t, :], ALU.mult, ALU.add
                                       ).then_inc(y_sv, 1)
                dve.wait_ge(y_sv, 2 * NT + t + 1)
                ln_stats(3 * NT + t)
                if t >= 1:
                    ln_norm(3 * NT + t - 1)
            ln_norm(4 * NT - 1)

            dve.wait_ge(lg_mm, 1)
            dve.wait_ge(tri_set, 4)
            lg = ps[:, 7, 0:RT].rearrange("p (t e) -> p t e", t=NT)
            then(v.tensor_reduce(rmax, lg, AX.X, ALU.max))
            v.tensor_tensor(prob, lg, rmax.unsqueeze(2).broadcast_to([P, NT, NE]), ALU.subtract).then_inc(lg_max, 1)
            dve.wait_ge(lg_exp, 1)
            v.memset(hmoe[:, EI:3 * P], 0.0).then_inc(lg_sv, 1)
            then(v.tensor_reduce(rsum, prob, AX.X, ALU.add))
            then(v.reciprocal(rsum, rsum))
            then(v.tensor_tensor(prob, prob, rsum.unsqueeze(2).broadcast_to([P, NT, NE]), ALU.mult))
            for t in range(NT):
                then(v.max(top8[:, t, :], prob[:, t, :]))
                then(v.max_index(idx8[:, t, :], top8[:, t, :], prob[:, t, :]))
            then(v.tensor_copy(idxf, idx8[:, :, 0:2]))
            then(v.tensor_scalar(wtop[:], top8[:, :, 0:2], tg[:, 3:4], None, ALU.mult))
            ids = iota16.unsqueeze(1).broadcast_to([P, NT, NE])
            then(v.tensor_tensor(one0, ids, idxf[:, :, 0:1].broadcast_to([P, NT, NE]), ALU.is_equal))
            then(v.tensor_tensor(one1, ids, idxf[:, :, 1:2].broadcast_to([P, NT, NE]), ALU.is_equal))
            then(v.tensor_tensor(both, one0, one1, ALU.add))
            v.memset(scan[0][:, 0:16], 0.0).then_inc(both_set, 1)
            v.memset(scan[1][:, 0:16], 0.0)

            def shared_hidden():
                for m, size in enumerate(SH_CHUNKS):
                    hidden(MC + m, m, size, 1.0, hsh)

            shared_hidden()
            dve.wait_ge(rank_mm, 1)
            rank = ps[:, 2, 0:RT].rearrange("p (t e) -> p t e", t=NT)
            total = ps[:, 3, 0:RT].rearrange("p (t e) -> p t e", t=NT)
            then(v.memset(cnt, 0.0))
            for t in range(NT):
                then(v.tensor_tensor(place_[:, t, :], rank[:, t, :], cnt, ALU.add))
                then(v.tensor_tensor(cnt, cnt, total[:, t, :], ALU.add))
            c3 = cmp[:, 0:NE * NT].rearrange("p (e k) -> p e k", e=NE)
            then(v.tensor_tensor(c3, cnt.unsqueeze(2).broadcast_to([P, NE, NT]),
                                 thr.unsqueeze(1).broadcast_to([P, NE, NT]), ALU.is_gt))
            then(v.tensor_reduce(ntile, c3, AX.X, ALU.add))
            then(v.tensor_scalar(scan[0][:, 16:32], ntile, 1.0, None, ALU.max))
            then(v.tensor_copy(ntile, scan[0][:, 16:32]))
            for i in range(4):
                a, b_ = scan[i % 2], scan[1 - i % 2]
                then(v.tensor_tensor(b_[:, 16:32], a[:, 16:32], a[:, 16 - 2 ** i:32 - 2 ** i], ALU.add))
            ends = scan[0][:, 16:32]
            then(v.tensor_tensor(nstart, ends, ntile, ALU.subtract))
            then(v.tensor_scalar(nstart, nstart, float(P), None, ALU.mult))
            then(v.tensor_copy(expert_end[:], ends))
            for i in range(3):
                then(v.tensor_scalar(tile_count[:, i:i + 1], ends[:, NE - 1:NE], float(i - 2), None, ALU.add))
            c4 = cmp.rearrange("p (n e) -> p n e", n=32)
            then(v.tensor_tensor(c4, iota29.unsqueeze(2).broadcast_to([P, 32, NE]),
                                 ends.unsqueeze(1).broadcast_to([P, 32, NE]), ALU.is_ge))
            then(v.tensor_reduce(texpf, c4, AX.X, ALU.add))
            v.tensor_copy(tile_expert[:], texpf).then_inc(tables_set, 1)
            then(v.tensor_tensor(place_, place_, nstart.unsqueeze(1).broadcast_to([P, NT, NE]), ALU.add))
            for j, one in enumerate((one0, one1)):
                then(v.tensor_tensor(tmp16, place_, one, ALU.mult))
                then(v.tensor_reduce(fdest, tmp16, AX.X, ALU.add))
                v.tensor_copy(dest[:, j, :], fdest).then_inc(dest_set, 1)
                dve.wait_ge(dest_set, j + 1)
            for t in range(NT):
                dve.wait_ge(y_mm, 3 * NT + t + 1)
                v.scalar_tensor_tensor(x[:, t, :], ps[:, (3 * NT + t) % 2, :], tg[:, 3:4], x[:, t, :], ALU.mult, ALU.add
                                       ).then_inc(y_sv, 1)

            dve.wait_ge(tables_set, 1)
            last2, last1, tiles = counts(dve)

            def tile_hidden(n):
                dve.wait_ge(gu_mm, n + 1)
                dve.wait_ge(m_silu, n + 1)
                if not (isinstance(n, int) and n == 0):
                    dve.wait_ge(hx_tr, n)
                v.tensor_tensor(hmoe[:, 0:EI], ps[:, 5, 0:EI], smoe, ALU.mult).then_inc(m_h, 1)

            def tile_hidden_save(n):
                dve.wait_ge(hx_tr, n + 1)
                v.tensor_copy(hmoeT, ps[:, 7, 0:3 * P].rearrange("p (c t) -> p c t", c=3)).then_inc(hx_sv, 1)

            def tile_out(n, first=False):
                dve.wait_ge(d_mm, n + 1)
                if not first:
                    dve.wait_ge(y_st, n * 16)
                v.tensor_copy(ymoe, ps[:, 3, :]).then_inc(d_sv, 1)

            tile_hidden(0)
            tile_hidden_save(0)
            tile_hidden(1)
            tile_out(0, True)
            tile_hidden_save(1)
            with dve.Fori(2, tiles) as n:
                tile_hidden(n)
                tile_out(n - 1)
                tile_hidden_save(n)
            tile_out(last1)

            for t in range(NT):
                dve.wait_ge(back_ld[t], 32)
                for j in range(2):
                    last = v.scalar_tensor_tensor(x[:, t, :], back[t][j], wtop[:, t, j:j + 1], x[:, t, :],
                                                  ALU.mult, ALU.add)
                    if j == 0:
                        then(last)
                last.then_inc(out_st, 1)

        @block.gpsimd
        def _(pool):
            nc.gpsimd.memset(ident[:], 0.0).then_inc(pool_step, 1)
            pool.wait_ge(pool_step, 1)
            nc.gpsimd.affine_select(out=ident[:], in_=ident[:], compare_op=ALU.not_equal, fill=1.0, base=0,
                                    pattern=[[-1, P]], channel_multiplier=1).then_inc(consts_set, 1)
            for slot in range(2):
                last = nc.gpsimd.memset(qbd[slot], 0.0)
            last.then_inc(pool_step, 1)
            nc.gpsimd.memset(at(A_KV, B * D), 0.0).then_inc(pool_step, 1)
            pool.wait_ge(pool_step, 3)
            pool.wait_ge(q0_sv, 8)

            def spread(b, slot, guard):
                if guard:
                    pool.wait_ge(sc_mm, b * 4 - 4)
                for h in range(HG):
                    r = slice(h * HD, (h + 1) * HD)
                    nc.gpsimd.tensor_copy(qbd[slot][r, :, h, :], qT[r, :, bass.ds(b * S, S)]
                                          ).then_inc(q_spread, 1)

            spread(0, 0, False)
            spread(1, 1, False)
            with pool.Fori(2, B - 1, 2) as b:
                spread(b, 0, True)
                spread(b + 1, 1, True)

            pool.wait_ge(y_sv, 2 * NT)
            nc.gpsimd.memset(at(A_K, B * D), 0.0).then_inc(ksbd_set, 1)
            nc.gpsimd.memset(zero, 0.0).then_inc(zero_set, 1)
            pool.wait_ge(zero_set, 1)
            pool.dma_start(xs_dram.rearrange("(t p) d -> p t d", p=P),
                           zero.unsqueeze(1).broadcast_to([P, ROWS_MAX, D])).then_inc(filled, 16)
            nc.gpsimd.iota(iota16, pattern=[[1, NE]], base=0, channel_multiplier=0,
                           allow_small_or_imprecise_dtypes=True).then_inc(tri_set, 1)
            nc.gpsimd.iota(thr, pattern=[[P, NT]], base=0, channel_multiplier=0,
                           allow_small_or_imprecise_dtypes=True)
            nc.gpsimd.iota(iota29, pattern=[[1, 32]], base=0, channel_multiplier=0,
                           allow_small_or_imprecise_dtypes=True).then_inc(tri_set, 1)
            nc.gpsimd.memset(ones, 1.0).then_inc(tri_set, 1)
            pool.wait_ge(tri_set, 3)
            nc.gpsimd.affine_select(out=lower, in_=ones, compare_op=ALU.is_gt, fill=0.0, base=0,
                                    pattern=[[1, P]], channel_multiplier=-1).then_inc(tri_set, 1)
            pool.wait_ge(filled, 16)
            pool.wait_ge(dest_set, 2)
            pool.wait_ge(ln_out, 4 * NT)
            for j in range(2):
                for t in range(NT):
                    pool.indirect_dma_start(xs_dram, bass.IndirectOffsetOnAxis(dest[:, j, t:t + 1], 0),
                                            h3[:, t, :], None).then_inc(scattered, 16)
            pool.wait_ge(scattered, 16 * 2 * NT)
            last2, last1, tiles = counts(pool)

            def load(n):
                pool.dma_start(xg, xs_dram[bass.ds(n * P, P), :]).then_inc(xg_ld, 16)

            def store(n):
                pool.wait_ge(d_sv, n + 1)
                pool.dma_start(xs_dram[bass.ds(n * P, P), :], ymoe).then_inc(y_st, 16)

            load(0)
            pool.wait_ge(xg_tr, 1)
            load(1)
            with pool.Fori(2, tiles) as n:
                pool.wait_ge(xg_tr, n)
                load(n)
                store(n - 2)
            store(last2)
            store(last1)
            pool.wait_ge(y_st, tiles * 16)
            pool.sem_inc(pool_held, 1)
            for t in range(NT):
                for j in range(2):
                    pool.indirect_dma_start(back[t][j], None, xs_dram,
                                            bass.IndirectOffsetOnAxis(dest[:, j, t:t + 1], 0)).then_inc(back_ld[t], 16)


def kernel(**inputs):
    import numpy as np
    import concourse.bacc as bacc
    from concourse.bass_utils import run_bass_kernel_spmd

    a = {k: np.asarray(v) for k, v in inputs.items()}

    def w_t(w):
        o, i = w.shape
        return np.ascontiguousarray(w.T.reshape(i // P, P, o).transpose(1, 0, 2))

    def col(v):
        return v.reshape(-1, P).T

    def gu_chunks(w):
        return w.T.reshape(KC, P, MC, P).transpose(2, 1, 0, 3)

    c = np.ascontiguousarray
    feeds = {
        "x": c(a["x"].reshape(TOK, D)),
        "ctx": c(a["ctx_2048"].transpose(0, 2, 1).reshape(B, KC, P, T).transpose(0, 2, 1, 3)),
        "mask": c(a["mask_BxS2_ik0"].reshape(B, TC, TP).transpose(2, 0, 1).reshape(TP, B * TC)),
        "cols": c(np.concatenate([col(a["L0_xattn_bq"]), col(a["L0_xattn_bk"]), col(a["L1_xattn_bg"]),
                                  col(a["L0_ffn_gate_s"]), col(a["L0_ffn_up_s"])], axis=1)),
        "rows": c(np.concatenate([a["L0_xattn_bv"], a["L0_xattn_bo"], a["L0_xattn_ln_gamma"],
                                  a["L0_xattn_ln_beta"], a["L0_ffn_down_s"]])),
        "scal": c(np.concatenate([a["g_xattn"], a["g_ffn"], a["L0_xattn_residual_scale"].reshape(1)])),
        "wq0": w_t(a["L0_xattn_Wq"]),
        "wk0": w_t(a["L0_xattn_Wk"]),
        "wv0": w_t(a["L0_xattn_Wv"]),
        "wo0": w_t(a["L0_xattn_Wo"]),
        "gu0": c(np.stack([gu_chunks(a["L0_ffn_gate_w"]), gu_chunks(a["L0_ffn_up_w"])], axis=2)),
        "wd0": w_t(a["L0_ffn_down_w"]),
        "wq1": w_t(a["L1_xattn_Wq"]),
        "wg1": w_t(a["L1_xattn_Wg"]),
        "wkv1": w_t(a["L1_xattn_Wkv"]),
        "wo1": w_t(a["L1_xattn_Wo"]),
        "gate": w_t(a["L1_ffn_gate_w"]),
        "sh13": w_t(np.concatenate([a["L1_ffn_sw1"], a["L1_ffn_sw3"]])),
        "sh2": c(a["L1_ffn_sw2"].T),
        "e13": c(np.concatenate([a["L1_ffn_w1"], a["L1_ffn_w3"]], axis=1).transpose(0, 2, 1)
                 .reshape(NE, KC, P, 2 * EI).transpose(0, 2, 1, 3).reshape(NE, P, KC * 2 * EI)),
        "e2": c(a["L1_ffn_w2"].transpose(0, 2, 1)),
    }
    nc = bacc.Bacc("TRN2", target_bir_lowering=False, num_devices=1)
    args = [nc.dram_tensor(f"in_{k}", v.shape, mybir.dt.from_np(v.dtype), kind="ExternalInput").ap()
            for k, v in feeds.items()]
    result = nc.dram_tensor("out_x", (TOK, D), F32, kind="ExternalOutput").ap()
    flamingo(nc, *args, result)
    r = run_bass_kernel_spmd(nc, [{f"in_{k}": v for k, v in feeds.items()}], core_ids=[0])
    return r.results[0]["out_x"].reshape(B, S, D)
```

```python
from contextlib import ExitStack

import concourse.bass as bass
from concourse import mybir

F32 = mybir.dt.float32
F32R = mybir.dt.float32r
I32 = mybir.dt.int32
U32 = mybir.dt.uint32
ALU = mybir.AluOpType
ACT = mybir.ActivationFunctionType
AX = mybir.AxisListType

P = 128
D = 512
KC = D // P
B, S, T = 8, 112, 375
TE = T + 1
TOK = B * S
NT = TOK // P
HALF = TOK // 2
TC, TP = 3, 125
H, HD = 16, 32
G = D // P
HG = P // HD
INTER = 1408
MC = INTER // P
SHARED = 704
SH_CHUNKS = [P] * 4 + [96] * 2
SH_AT = [sum(SH_CHUNKS[:i]) for i in range(6)]
SPARE = 4
NE = 16
EI = 352
E_CHUNKS = [P, P, EI - 2 * P]
NSLOT = 4
ROWS_MAX = 29
LN_EPS = 1e-5
Z_EPS = 1e-6
P_EPS = 1e-8
CLIP = 50.0
SCALE = float(HD) ** -0.5


def flamingo(nc, x_in, ctx_in, mask_in, cols_in, rows_in, scal_in, wq0_in, wk0_in, wv0_in, wo0_in,
             gu0_in, wd0_in, wq1_in, wg1_in, wkv1_in, wo1_in, gate_in, sh13_in, sh2_in,
             e13_in, e2_in, out):
    with ExitStack() as stack:
        def sb(name, shape, dt=F32):
            return stack.enter_context(nc.sbuf_tensor(name, shape, dt))

        def sem(name):
            return stack.enter_context(nc.semaphore(name))

        ps = stack.enter_context(nc.psum_tensor("ps", [P, 8, 512], F32))

        x = sb("x", [P, NT, D])
        ident = sb("ident", [P, P])
        cols = sb("cols", [P, 12 + 2 * MC])
        scal = sb("scal", [P, 5])
        tg = sb("tg", [P, 4])
        rs = sb("rs", [P, 1])
        eps = sb("eps", [P, 1])
        mask_i = sb("mask_i", [TP, B * TC], I32)
        mscale = sb("mscale", [TP, B * TC])
        mbias = sb("mbias", [TP, B * TC])
        stats = sb("stats", [P, 2, 6])
        mv = sb("mv", [P, 4 * NT, 2])
        std = sb("std", [P, 4 * NT])
        rstd = sb("rstd", [P, 4 * NT])
        dmv = sb("dmv", [P, NT, 2])
        dstd = sb("dstd", [P, NT])
        drstd = sb("drstd", [P, NT])
        warm = sb("warm", [P, G])
        ks = sb("ks", [P, B, G])
        zsum = sb("zsum", [S, 2, 8])
        zinv = sb("zinv", [S, 2, 8])
        gate_w = sb("gate_w", [P, KC * NE])
        gate_r = sb("gate_r", [P, 2, KC * NE], F32R)
        dest = sb("dest", [P, 2, NT], U32)
        wtop = sb("wtop", [P, NT, 2])
        tile_expert = sb("tile_expert", [P, 32], I32)
        expert_end = sb("expert_end", [P, NE], I32)
        tile_count = sb("tile_count", [P, 4], I32)
        idx8 = sb("idx8", [P, NT, 8], U32)

        WORDS = 48208
        base = -(-nc.sbuf_base // 32) * 32
        arena = nc.alloc_sbuf_tensor_at("arena", [P, WORDS], F32, offset=base)
        arena_r = nc.alloc_sbuf_tensor_at("arena_r", [P, WORDS], F32R, offset=base)

        def shaped(v, dims):
            if len(dims) == 2:
                return v.rearrange("p (a b) -> p a b", a=dims[0])
            if len(dims) == 3:
                return v.rearrange("p (a b c) -> p a b c", a=dims[0], b=dims[1])
            return v

        def at(off, *dims, rows_=P):
            n = 1
            for d in dims:
                n *= d
            return shaped(arena[0:rows_, off:off + n], dims)

        def at_r(off, *dims):
            n = 1
            for d in dims:
                n *= d
            return shaped(arena_r[:, off:off + n], dims)

        def landing(name, off, words):
            return off, nc.alloc_sbuf_tensor_at(name, [P, words], F32, offset=base + 4 * off)

        def halves(high, low, land, *dims):
            n = 1
            for d in dims:
                n *= d
            off, words = land
            return at_r(high, *dims), at_r(low, *dims), shaped(words[:, low - off:low - off + n], dims)

        A_HT, A_Q = 0, 2 * KC * TOK
        hT_both = nc.alloc_sbuf_tensor_at("hT", [P, 2, KC, TOK], F32R, offset=base + 4 * A_HT)
        hT = hT_both[:, 0], hT_both[:, 1]
        qT = at(A_Q, KC, TOK)
        A_KV = A_Q + KC * TOK
        A_BV = A_KV + B * G * HD
        A_LN = A_BV + D
        A_WL = A_LN + 2 * D
        A_WH = A_WL + 8192
        A_C = A_WH + 8192
        A_K = A_C + 4 * KC * TE
        A_V0 = A_K + KC * TE
        A_K1 = A_V0 + 2 * TC * H * (HD + 1)
        A_V1 = A_K1 + TC * D
        A_QB = A_V1 + TC * G * (P + 1)
        A_P = A_QB + G * HG * S
        kvc = at(A_KV, B * G, HD)
        bv = at(A_BV, D)
        lnt = at(A_LN, 2, D)
        ctok = at(A_LN, D, rows_=S)
        kexp = at(A_LN + D, D, rows_=TP)
        land_w = landing("land_w", A_WL, 8192)
        land_c = landing("land_c", A_C, 4 * KC * TE)
        land_q = landing("land_q", A_V0 + 2048, 2048)
        wk0 = halves(A_WH, A_WL, land_w, KC, D)
        wv0 = halves(A_WH + 2048, A_WL + 2048, land_w, KC, D)
        wkv1 = halves(A_WH + 4096, A_WL + 4096, land_w, KC, 2 * D)
        wq0 = halves(A_V0, A_V0 + 2048, land_q, KC, D)
        ctxT = [halves(A_C + (2 * i + 1) * KC * TE, A_C + 2 * i * KC * TE, land_c, KC, TE) for i in range(2)]
        kT = at(A_K, KC, TE)
        v0 = [at(A_V0 + i * TC * H * (HD + 1), TC * H, HD + 1, rows_=TP).rearrange("p (c h) e -> p c h e", c=TC)
              for i in range(2)]
        k1 = at(A_K1, TC, D, rows_=TP)
        v1 = at(A_V1, TC * G, P + 1, rows_=TP).rearrange("p (c g) e -> p c g e", c=TC)
        qbd = at(A_QB, G, HG, S)
        probs = [at(A_P + i * TC * HG * S, TC, HG * S, rows_=TP) for i in range(2)]
        wo0 = halves(A_WH + 4096, A_Q, landing("land_o", A_Q, 2048), KC, D)
        rows = at(A_WH + 6144, 4 * D)
        dtile = [at(A_C + 3072 + i * D, D) for i in range(5)]
        A_GU = [A_WL + m * 1024 if m < 8 else A_C + (m - 8) * 1024 for m in range(MC)]
        gu0 = [halves(A_WH + m % SPARE * 1024, A_GU[m], land_w if m < 8 else land_c, 2 * KC, P) for m in range(MC)]
        A_WD = A_V0
        wd0 = at(A_WD, MC, D)
        A_H0 = [A_Q + m * TOK if m < 4 else A_C + 3072 + (m - 4) * TOK if m < 7 else A_K if m == 7
                else A_WD + MC * D + (m - 8) * TOK for m in range(MC)]
        h0 = [at(A_H0[m], TOK) for m in range(MC)]
        silu0 = [at(A_WH + 4096 + i * TOK, 2, HALF) for i in range(2)]
        ytmp = at(A_WH + 4096, D)
        wq1 = halves(A_WH, A_WL, land_w, KC, D)
        wg1 = halves(A_WH + 2048, A_WL + 2048, land_w, KC, D)
        wo1 = halves(A_WL + 6144, A_WL + 4096, land_w, KC, D)
        qexp = at(A_WH + 4096, HALF)
        qrelu = at(A_WH + 4096 + HALF, HALF)
        zrec = at(A_WH + 4096 + 2 * HALF, G, S)
        zero = at(A_WH + 4096 + 3 * HALF, D)
        gT = at(28160, KC, TOK)
        kvbd = at(31744, B * G, P)
        ksbd = at(35840, B * G, P)
        A_SH = 40192
        land_s = landing("land_s", A_SH, 2 * KC * SHARED)
        sh13 = [halves(23808 + m % SPARE * 1024, A_SH + 2 * KC * SH_AT[m], land_s, 2 * KC, SH_CHUNKS[m])
                for m in range(6)]
        sh2 = at(37120, 6, D)
        hsh = [at(31744 + m * TOK, TOK) for m in range(6)]
        silu1 = [at(45824 + i * TOK, 2, HALF) for i in range(2)]
        A_E = A_KV
        h3 = at(28160, NT, D)
        xg = at(8904, D)
        hmoe = at(9416, 3 * P)
        hmoeT = at(9800, 3, P)
        smoe = at(10184, EI)
        xgT = at(47616, KC, P)
        A_XR = A_SH
        A_YR = A_SH + 2 * D
        back = [[at(31744 + (2 * t + j) * D, D) for j in range(2)] for t in range(NT)]
        RT = NT * NE

        def scratch(off, n):
            return arena[:, A_Q + off:A_Q + off + n]

        def rt(i):
            return scratch(i * RT, RT).rearrange("p (t e) -> p t e", t=NT)

        prob, one0, one1, both, place_, tmp16 = (rt(i) for i in range(6))
        iota16 = scratch(672, NE)
        thr = scratch(688, NT)
        cnt = scratch(695, NE)
        rmax = scratch(711, NT)
        rsum = scratch(718, NT)
        top8 = scratch(728, 56).rearrange("p (t e) -> p t e", t=NT)
        idxf = scratch(784, 14).rearrange("p (t e) -> p t e", t=NT)
        fdest = scratch(800, NT)
        scan = [scratch(808 + 32 * i, 32) for i in range(2)]
        ntile = scratch(872, NE)
        nstart = scratch(888, NE)
        iota29 = scratch(904, 32)
        cmp = scratch(936, 512)
        lower = scratch(1448, P)
        ones = scratch(1576, P)
        texpf = scratch(1704, 32)

        xs_dram = nc.dram_tensor("sorted_rows", (ROWS_MAX * P, D), F32, kind="Internal").ap()

        bv_ld = sem("bv_ld")
        rows_ld = sem("rows_ld")
        w_high = sem("w_high")
        w_low = sem("w_low")
        wq0_high = sem("wq0_high")
        wq0_low = sem("wq0_low")
        c_high = sem("c_high")
        c_low = sem("c_low")
        gu_high = sem("gu_high")
        gu_low = sem("gu_low")
        ln_H = sem("ln_H")
        ct_high = sem("ct_high")
        beta_set = sem("beta_set")
        kvbd_set = sem("kvbd_set")
        at_high = sem("at_high")
        at_low = sem("at_low")
        xs_rdy = sem("xs_rdy")
        x_ld = sem("x_ld")
        small_ld = sem("small_ld")
        wq0_ld = sem("wq0_ld")
        wk0_ld = sem("wk0_ld")
        wv0_ld = sem("wv0_ld")
        wkv1_ld = sem("wkv1_ld")
        wo0_ld = sem("wo0_ld")
        wd0_ld = sem("wd0_ld")
        wq1_ld = sem("wq1_ld")
        wg1_ld = sem("wg1_ld")
        wo1_ld = sem("wo1_ld")
        sh_ld = sem("sh_ld")
        gate_ld = sem("gate_ld")
        consts_set = sem("consts_set")
        eps_set = sem("eps_set")
        tanh_set = sem("tanh_set")
        rows_set = sem("rows_set")
        mask_set = sem("mask_set")
        ones_set = sem("ones_set")
        kT_mm = sem("kT_mm")
        v0_mm = sem("v0_mm")
        k1_mm = sem("k1_mm")
        v1_mm = sem("v1_mm")
        kv_mm = sem("kv_mm")
        sc_mm = sem("sc_mm")
        pv_mm = sem("pv_mm")
        ct_mm = sem("ct_mm")
        q0_mm = sem("q0_mm")
        kT_sv = sem("kT_sv")
        v0_sv = sem("v0_sv")
        k1_exp = sem("k1_exp")
        k1_relu = sem("k1_relu")
        k1_sv = sem("k1_sv")
        v1_sv = sem("v1_sv")
        kv_sv = sem("kv_sv")
        clipped = sem("clipped")
        exped = sem("exped")
        norm_step = sem("norm_step")
        normed = sem("normed")
        ct_sv = sem("ct_sv")
        q0_sv = sem("q0_sv")
        q_spread = sem("q_spread")
        ln_var = sem("ln_var")
        ln_std = sem("ln_std")
        ln_out = sem("ln_out")
        ln_tr = sem("ln_tr")
        ln_T = sem("ln_T")
        d_var = sem("d_var")
        d_std = sem("d_std")
        y_mm = sem("y_mm")
        y_sv = sem("y_sv")
        ff_mm = sem("ff_mm")
        ff_silu = sem("ff_silu")
        ff_h = sem("ff_h")
        q1_mm = sem("q1_mm")
        q1_exp = sem("q1_exp")
        q1_relu = sem("q1_relu")
        q1_sv = sem("q1_sv")
        at_mm = sem("at_mm")
        at_sv = sem("at_sv")
        g1_mm = sem("g1_mm")
        g1_sv = sem("g1_sv")
        gated = sem("gated")
        ksbd_set = sem("ksbd_set")
        zero_set = sem("zero_set")
        filled = sem("filled")
        lg_mm = sem("lg_mm")
        lg_max = sem("lg_max")
        lg_exp = sem("lg_exp")
        lg_sv = sem("lg_sv")
        both_set = sem("both_set")
        rank_mm = sem("rank_mm")
        dest_set = sem("dest_set")
        tables_set = sem("tables_set")
        tri_set = sem("tri_set")
        scattered = sem("scattered")
        w_landed = sem("w_landed")
        xg_ld = sem("xg_ld")
        xg_tr = sem("xg_tr")
        xg_sv = sem("xg_sv")
        gu_mm = sem("gu_mm")
        m_silu = sem("m_silu")
        m_h = sem("m_h")
        hx_tr = sem("hx_tr")
        hx_sv = sem("hx_sv")
        d_mm = sem("d_mm")
        d_sv = sem("d_sv")
        y_st = sem("y_st")
        out_st = sem("out_st")
        dve_step = sem("dve_step")
        pool_step = sem("pool_step")
        act_held = sem("act_held")
        pool_held = sem("pool_held")
        ctx_ld = [sem(f"ctx_ld{i}") for i in range(2)]
        gu0_ld = [sem(f"gu0_ld{m}") for m in range(MC)]
        sh13_ld = [sem(f"sh13_ld{m}") for m in range(6)]
        e_ld = [sem(f"e_ld{i}") for i in range(NSLOT)]

        back_ld = [sem(f"back_ld{t}") for t in range(NT)]

        block = stack.enter_context(nc.Block())

        def counts(engine):
            return [engine.value_load(tile_count[0:1, i:i + 1], min_val=NE - 3 + i, max_val=ROWS_MAX - 3 + i)
                    for i in range(4)]

        WEIGHTS = ("wk0", "wv0", "wkv1", "gate", "wo0", "wq1", "wg1", "wo1")

        def nth(name):
            return WEIGHTS.index(name) + 1

        def ln_bank(n):
            return (6 if n < NT else 0 if n < 2 * NT else 2) + n % NT % 2

        def y_bank(n):
            return (3 if n < NT else 0) + n % 2

        @block.sync
        def _(sp):
            sp.dma_start(ctxT[0][2], ctx_in[0]).then_inc(ctx_ld[0], 16)
            sp.dma_start(wk0[2], wk0_in).then_inc(wk0_ld, 16)
            sp.dma_start(cols[:], cols_in).then_inc(small_ld, 16)
            sp.dma_start(scal[:], scal_in.partition_broadcast(P)).then_inc(small_ld, 16)
            sp.dma_start(mask_i[:], mask_in).then_inc(small_ld, 16)
            sp.dma_start(x[:], x_in.rearrange("(t p) d -> p t d", p=P)).then_inc(x_ld, 16)
            sp.dma_start(wq0[2], wq0_in).then_inc(wq0_ld, 16)
            sp.dma_start(bv, rows_in[0:D].partition_broadcast(P)).then_inc(bv_ld, 16)
            sp.dma_start(wv0[2], wv0_in).then_inc(wv0_ld, 16)
            sp.dma_start(wkv1[2], wkv1_in).then_inc(wkv1_ld, 16)
            sp.dma_start(ctxT[1][2], ctx_in[1]).then_inc(ctx_ld[1], 16)
            sp.dma_start(gate_w[:], gate_in.rearrange("p k e -> p (k e)")).then_inc(gate_ld, 16)
            with sp.Fori(2, B - 1, 2) as b:
                for slot in range(2):
                    sp.wait_ge(v1_mm, (b + slot) * 3 - 3)
                    sp.wait_ge(kT_mm, (b + slot) * 4 - 4)
                    sp.dma_start(ctxT[slot][2],
                                 ctx_in[bass.ds(b + slot, 1)].rearrange("o p k t -> (o p) k t")
                                 ).then_inc(ctx_ld[slot], 16)
            sp.wait_ge(q_spread, 4 * B)
            sp.dma_start(wo0[2], wo0_in).then_inc(wo0_ld, 16)
            sp.wait_ge(kT_mm, 4 * B)
            sp.dma_start(rows, rows_in[D:5 * D].partition_broadcast(P)).then_inc(rows_ld, 16)
            for m in range(MC):
                sp.dma_start(gu0[m][2], gu0_in[m]).then_inc(gu0_ld[m], 16)
            sp.wait_ge(pv_mm, 4 * B)
            sp.wait_ge(kv_mm, 2 * B)
            sp.dma_start(wd0, wd0_in).then_inc(wd0_ld, 16)
            sp.wait_ge(ff_mm, MC)
            sp.dma_start(wq1[2], wq1_in).then_inc(wq1_ld, 16)
            sp.dma_start(wg1[2], wg1_in).then_inc(wg1_ld, 16)
            sp.dma_start(wo1[2], wo1_in).then_inc(wo1_ld, 16)
            sp.wait_ge(y_mm, 2 * NT)
            for m, size in enumerate(SH_CHUNKS):
                sp.dma_start(sh13[m][2], sh13_in[:, 2 * KC * SH_AT[m]:2 * KC * (SH_AT[m] + size)].rearrange(
                    "p (k c) -> p k c", c=size)).then_inc(sh13_ld[m], 16)
            sp.wait_ge(at_mm, B)
            sp.dma_start(sh2[:, 0:4, :], sh2_in[0:4 * P, :].rearrange("(c p) d -> p c d", p=P)).then_inc(sh_ld, 16)
            sp.dma_start(sh2[0:96, 4:6, :], sh2_in[4 * P:SHARED, :].rearrange("(c p) d -> p c d", p=96)
                         ).then_inc(sh_ld, 16)
            sp.wait_ge(y_mm, 3 * NT)

            def load_expert(e):
                slot = e % NSLOT
                w = A_E + slot * 4352
                sp.dma_start(arena[:, w:w + 2816], e13_in[e]).then_inc(e_ld[slot], 16)
                sp.dma_start(at(w + 2816, 2, D), e2_in[e, 0:2 * P, :].rearrange("(c p) d -> p c d", p=P)).then_inc(e_ld[slot], 16)
                sp.dma_start(at(w + 2816 + 2 * D, D, rows_=EI - 2 * P), e2_in[e, 2 * P:EI, :]).then_inc(e_ld[slot], 16)

            for e in range(NSLOT):
                if e == NSLOT - 1:
                    sp.wait_ge(ff_mm, MC + 6)
                load_expert(e)
            def post(e):
                sp.wait_ge(e_ld[e % NSLOT], 48 * (e // NSLOT + 1))
                sp.sem_inc(w_landed, 1)

            post(0)
            post(1)
            sp.wait_ge(tables_set, 1)
            for e in range(2, NE):
                if e - 2 + NSLOT < NE:
                    last = sp.value_load(expert_end[0:1, e - 2:e - 1], min_val=1, max_val=ROWS_MAX)
                    post(e)
                    sp.wait_ge(d_mm, last)
                    load_expert(e - 2 + NSLOT)
                else:
                    post(e)
            out_t = out.rearrange("(t p) d -> t p d", p=P)
            for t in range(NT):
                sp.wait_ge(out_st, 1 + t)
                sp.dma_start(out_t[t], x[:, t, :]).then_inc(x_ld, 16)
            sp.wait_ge(x_ld, 16 * (NT + 1))

        @block.tensor
        def _(pe):
            mm = nc.tensor.matmul

            def piece(pair, k, first, width):
                return tuple(half[:, k, first:first + width] for half in pair[:2])

            def product(into, operands):
                for i, (a, w) in enumerate(operands):
                    mm(into, a[0], w[0], start=i == 0, stop=False)
                    mm(into, a[0], w[1], start=False, stop=False)
                    last = mm(into, a[1], w[0], start=False, stop=i == len(operands) - 1)
                return last

            def first_batch(b):
                return isinstance(b, int) and b == 0

            def keys_T(b, slot, g):
                if g >= 2:
                    pe.wait_ge(kT_sv, b * 4 + (g - 1))
                elif not first_batch(b):
                    if g == 0:
                        pe.wait_ge(v0_sv, b * 3 + 3)
                    else:
                        pe.wait_ge(k1_relu, b * 3 + 3)
                product(ps[:, 3 + g % 2, 0:TE], [(piece(wk0, k, g * P, P), piece(ctxT[slot], k, 0, TE))
                                                 for k in range(KC)]).then_inc(kT_mm, 1)

            def values(b, slot, c, transposed):
                if c == 0:
                    pe.wait_ge(c_low, b + 1)
                for j, (w, first, bank, done) in enumerate([(wv0, 0, 3, v0_mm), (wkv1, 0, 4, k1_mm),
                                                            (wkv1, D, 5, v1_mm)]):
                    if j < 2 and c == 0 and first_batch(b):
                        pe.wait_ge(kT_sv, 3 + j)
                    elif j < 2 and c == 0:
                        pe.wait_ge(kv_sv, b * 2 - 1 + j)
                    elif j == 0:
                        pe.wait_ge(v0_sv, b * 3 + c)
                    elif j == 1:
                        pe.wait_ge(k1_relu, b * 3 + c)
                    else:
                        if not (first_batch(b) and c == 0):
                            pe.wait_ge(v1_sv, b * 3 + c)
                        if c == 1 and transposed:
                            pe.wait_ge(ct_sv, b - 1)
                    product(ps[0:TP, bank, :], [(piece(ctxT[slot], k, c * TP, TP), piece(w, k, first, D))
                                                for k in range(KC)]).then_inc(done, 1)

            def kv_summary(b):
                pe.wait_ge(k1_sv, b * 3 + 3)
                pe.wait_ge(v1_sv, b * 3 + 3)
                if first_batch(b):
                    pe.wait_ge(ones_set, 3)
                    pe.wait_ge(v0_sv, 3)
                for g in range(G):
                    if g % 2 == 0 and not first_batch(b):
                        pe.wait_ge(kT_sv, b * 4 + 3 + g // 2)
                    for c in range(TC):
                        last = mm(ps[:, 3 + g // 2, (g % 2) * 129:(g % 2) * 129 + 129],
                                  k1[:, c, g * P:(g + 1) * P], v1[:, c, g, :], start=c == 0, stop=c == TC - 1)
                    if g % 2:
                        last.then_inc(kv_mm, 1)

            def head_transposes(b, values_done):
                pe.wait_ge(normed, b * 2 + 2)
                pe.wait_ge(v1_sv, values_done)
                for k in range(KC):
                    last = nc.tensor.transpose(ps[:, 5, k * S:(k + 1) * S], ctok[:, k * P:(k + 1) * P], ident[0:S, 0:S])
                last.then_inc(ct_mm, 1)

            def scores(b, g):
                if g == 0:
                    pe.wait_ge(q_spread, b * 4 + 4)
                    pe.wait_ge(kT_sv, b * 4 + 4)
                if g > 0 or not first_batch(b):
                    pe.wait_ge(clipped, b * 4 + g)
                for c in range(TC):
                    last = mm(ps[0:TP, c, 0:HG * S], kT[:, g, c * TP:(c + 1) * TP],
                              qbd[:, g, :, :], start=True, stop=True)
                last.then_inc(sc_mm, 1)

            def mix(b, slot, g):
                pe.wait_ge(exped, b * 4 + g + 1)
                if g == 0:
                    pe.wait_ge(v0_sv, b * 3 + 3)
                if g % 2 == 0 and not first_batch(b):
                    pe.wait_ge(normed, b * 2 - 1 + g // 2)
                for h in range(HG):
                    o = (g % 2) * 4 + h
                    for c in range(TC):
                        last = mm(ps[0:S, 6 + g // 2, o * 33:o * 33 + 33], probs[g % 2][:, c, h * S:(h + 1) * S],
                                  v0[slot][:, c, 4 * g + h, :], start=c == 0, stop=c == TC - 1)
                last.then_inc(pv_mm, 1)

            def batch(b, slot, more=True):
                for g in range(G):
                    scores(b, g)
                    if g == 1 and not first_batch(b):
                        head_transposes(b - 1, b * 3 + 4 if more else 3 * B)
                    if more and g < 3:
                        values(b + 1, 1 - slot, g, not first_batch(b))
                    if more and g == 3:
                        for gg in range(G):
                            keys_T(b + 1, 1 - slot, gg)
                    mix(b, slot, g)
                if more:
                    kv_summary(b + 1)

            def ln_transposes(n):
                t = n % NT
                bank = ln_bank(n)
                if n == 0:
                    pe.wait_ge(consts_set, 1)
                pe.wait_ge(ln_out, n + 1)
                if t >= 2:
                    pe.wait_ge(ln_T, n - 1)
                elif n >= NT:
                    pe.wait_ge(ln_T, n // NT * NT)
                src = h3[:, t, :] if n >= 3 * NT else lnt[:, n % 2, :]
                for k in range(KC):
                    last = nc.tensor.transpose(ps[:, bank, k * P:(k + 1) * P], src[:, k * P:(k + 1) * P], ident[:])
                last.then_inc(ln_tr, 1)

            def last_transposes(stage):
                for t in range(4 if stage == 1 else NT - 2, NT):
                    ln_transposes(stage * NT + t)
                pe.wait_ge(ln_T, (stage + 1) * NT)

            pe.wait_ge(c_low, 1)
            pe.wait_ge(w_low, nth("wk0"))
            keys_T(0, 0, 0)
            keys_T(0, 0, 1)
            ln_transposes(0)
            ln_transposes(1)
            keys_T(0, 0, 2)
            ln_transposes(2)
            keys_T(0, 0, 3)
            ln_transposes(3)
            ln_transposes(4)
            pe.wait_ge(ln_T, 4)
            pe.wait_ge(wq0_low, 1)
            for i in range(8):
                n, m = i // 4, i % 4
                if i == 2:
                    last_transposes(0)
                if i >= 2:
                    pe.wait_ge(q0_sv, i - 1)
                product(ps[:, i % 2, 0:HALF], [(piece(wq0, k, m * P, P), piece(hT, k, n * HALF, HALF))
                                               for k in range(KC)]).then_inc(q0_mm, 1)

            pe.wait_ge(w_low, nth("wkv1"))
            for c in range(TC):
                values(0, 0, c, False)
            kv_summary(0)
            pe.wait_ge(q0_sv, 8)
            batch(0, 0)
            with pe.Fori(1, B - 4, 2) as b:
                batch(b, 1)
                batch(b + 1, 0)
            batch(B - 3, 1)
            batch(B - 2, 0)

            def tok(pair, k, t):
                return piece(pair, k, t * P, P)

            def to_tokens(n, product_of):
                if n % NT >= 2:
                    pe.wait_ge(y_sv, n - 1)
                product_of(n % NT, ps[:, y_bank(n), :]).then_inc(y_mm, 1)

            def tokens_then_ln(stage, product_of):
                for t in range(NT):
                    n = stage * NT + t
                    if t < 2:
                        pe.wait_ge(y_sv, n - 1)
                    to_tokens(n, product_of)
                    if t >= 2:
                        ln_transposes((stage + 1) * NT + t - 2)

            def output_of_0(t, into):
                pe.wait_ge(ct_sv, (t * P + P - 1) // S + 1)
                return product(into, [(tok(hT, k, t), piece(wo0, k, 0, D)) for k in range(KC)])

            for g in range(G):
                scores(B - 1, g)
                if g == 0:
                    pe.wait_ge(w_low, nth("wo0"))
                    pe.wait_ge(kv_sv, 2 * B)
                if g == 1:
                    head_transposes(B - 2, 3 * B)
                to_tokens(g, output_of_0)
                mix(B - 1, 1, g)
            head_transposes(B - 1, 3 * B)
            pe.wait_ge(clipped, 4 * B)
            for t in range(4, NT):
                to_tokens(t, output_of_0)
            for t in range(4):
                ln_transposes(NT + t)

            def gate_up(m, pair, size, stage=None):
                for n in range(2):
                    if stage is not None and n == 1:
                        last_transposes(stage)
                    for j in range(2):
                        last = product(ps[0:size, 4 * (1 - m % 2) + 2 * j + n, 0:HALF],
                                       [(piece(pair, j * KC + k, 0, size), piece(hT, k, n * HALF, HALF))
                                        for k in range(KC)])
                last.then_inc(ff_mm, 1)

            pe.wait_ge(normed, 2 * B)
            pe.wait_ge(y_sv, NT)
            pe.wait_ge(ln_T, NT + 4)
            for m in range(MC):
                pe.wait_ge(gu_low, m + 1)
                if m >= 2:
                    pe.wait_ge(ff_h, m - 1)
                gate_up(m, gu0[m], P, 1 if m == 0 else None)
            pe.wait_ge(ff_h, MC)
            pe.wait_ge(wd0_ld, 16)

            def down_of_0(t, into):
                for m in range(MC):
                    last = mm(into, h0[m][:, t * P:(t + 1) * P], wd0[:, m, :], start=m == 0, stop=m == MC - 1)
                return last

            tokens_then_ln(1, down_of_0)

            def query(i):
                n, m = i // 4, i % 4
                if i >= 4:
                    pe.wait_ge(q1_relu, i - 3)
                product(ps[:, 4 + i % 4, 0:HALF], [(piece(wq1, k, m * P, P), piece(hT, k, n * HALF, HALF))
                                                   for k in range(KC)]).then_inc(q1_mm, 1)

            def attend(b):
                pe.wait_ge(q1_sv, 4 if b < 4 else 8)
                if b >= 2:
                    pe.wait_ge(at_sv, b - 1)
                for j, w in enumerate((kvbd, ksbd)):
                    for g in range(G):
                        last = mm(ps[:, 2 * j + b % 2, g * S:(g + 1) * S], w[:, b * G + g, :],
                                  qT[:, g, b * S:(b + 1) * S], start=True, stop=True)
                last.then_inc(at_mm, 1)

            def gate(i):
                n, m = i // 4, i % 4
                if i < 4:
                    pe.wait_ge(q1_relu, 5 + i)
                else:
                    pe.wait_ge(g1_sv, i - 3)
                product(ps[:, 4 + i % 4, 0:HALF], [(piece(wg1, k, m * P, P), piece(hT, k, n * HALF, HALF))
                                                   for k in range(KC)]).then_inc(g1_mm, 1)

            pe.wait_ge(ln_T, 2 * NT + 4)
            pe.wait_ge(w_low, nth("wq1"))
            query(0)
            query(1)
            last_transposes(2)
            query(2)
            query(3)
            query(4)
            pe.wait_ge(kvbd_set, 5)
            pe.wait_ge(ksbd_set, 5)
            pe.wait_ge(kv_sv, 2 * B)
            pe.wait_ge(y_sv, 2 * NT)
            for b in range(3):
                attend(b)
                query(5 + b)
            pe.wait_ge(w_low, nth("wg1"))
            for b in range(3, B):
                attend(b)
                gate(b - 3)
            for i in range(B - 3, 8):
                gate(i)

            def output_of_1(t, into):
                pe.wait_ge(at_low, 4 if (t + 1) * P <= HALF else 8)
                return product(into, [(tok(hT, k, t), piece(wo1, k, 0, D)) for k in range(KC)])

            pe.wait_ge(w_low, nth("wo1"))
            pe.wait_ge(at_sv, B)
            tokens_then_ln(2, output_of_1)

            pe.wait_ge(ln_T, 3 * NT + 4)
            pe.wait_ge(g1_sv, 8)
            for m, size in enumerate(SH_CHUNKS):
                pe.wait_ge(gu_low, MC + m + 1)
                if m >= 2:
                    pe.wait_ge(ff_h, MC + m - 1)
                if m == 1:
                    pe.wait_ge(lg_sv, 1)
                    gate_up(m, sh13[m], size)
                elif m == 0:
                    for n in range(2):
                        if n == 1:
                            last_transposes(3)
                            pe.wait_ge(y_sv, 3 * NT)
                            for t in range(NT):
                                last = product(ps[:, 1, t * NE:(t + 1) * NE],
                                               [(tok(hT, k, t), (gate_r[:, 0, k * NE:(k + 1) * NE],
                                                                 gate_r[:, 1, k * NE:(k + 1) * NE]))
                                                for k in range(KC)])
                            last.then_inc(lg_mm, 1)
                        for j in range(2):
                            last = product(ps[0:size, 4 + 2 * j + n, 0:HALF],
                                           [(piece(sh13[0], j * KC + k, 0, size), piece(hT, k, n * HALF, HALF))
                                            for k in range(KC)])
                    last.then_inc(ff_mm, 1)
                else:
                    gate_up(m, sh13[m], size)
            pe.wait_ge(ff_h, MC + 6)
            pe.wait_ge(both_set, 1)
            pe.wait_ge(tri_set, 4)
            mm(ps[:, 6, 0:RT], lower, both.rearrange("p t e -> p (t e)"), start=True, stop=True)
            mm(ps[:, 7, 0:RT], ones, both.rearrange("p t e -> p (t e)"), start=True, stop=True
               ).then_inc(rank_mm, 1)
            pe.wait_ge(sh_ld, 32)
            for t in range(NT):
                pe.wait_ge(y_sv, 3 * NT + t - 1)
                for m, z in enumerate(SH_CHUNKS):
                    last = mm(ps[:, (3 * NT + t) % 2, :], hsh[m][0:z, t * P:(t + 1) * P], sh2[0:z, m, :],
                              start=m == 0, stop=m == 5)
                last.then_inc(y_mm, 1)

            pe.wait_ge(tables_set, 1)
            last3, last2, last1, tiles = counts(pe)

            def slot_of(n):
                e = pe.value_load(tile_expert[0:1, bass.ds(n, 1)], min_val=0, max_val=NE - 1)
                return e, A_E + (e % NSLOT) * 4352

            def rows_T(n):
                pe.wait_ge(xs_rdy, n + 1)
                for k in range(KC):
                    last = nc.tensor.transpose(ps[:, 6, k * P:(k + 1) * P], xg[:, k * P:(k + 1) * P], ident[:])
                last.then_inc(xg_tr, 1)

            def up_expert(n):
                e, w = slot_of(n)
                pe.wait_ge(w_landed, e + 1)
                pe.wait_ge(xg_sv, n + 1)
                for j in range(2):
                    for k in range(KC):
                        last = mm(ps[:, 4 + j, 0:EI], xgT[:, k, :],
                                  arena[:, bass.ds(w + (k * 2 * EI + j * EI), EI)], start=k == 0, stop=k == KC - 1)
                last.then_inc(gu_mm, 1)

            def down_expert(n):
                e, w = slot_of(n)
                pe.wait_ge(hx_sv, n + 1)
                if not first_batch(n):
                    pe.wait_ge(d_sv, n)
                for c, z in enumerate(E_CHUNKS):
                    last = mm(ps[:, 3, :], hmoeT[0:z, c, :], arena[0:z, bass.ds(w + (2816 + c * D), D)],
                              start=c == 0, stop=c == 2)
                last.then_inc(d_mm, 1)

            def hidden_T(n):
                pe.wait_ge(m_h, n + 1)
                for c in range(3):
                    last = nc.tensor.transpose(ps[:, 7, c * P:(c + 1) * P], hmoe[:, c * P:(c + 1) * P], ident[:])
                last.then_inc(hx_tr, 1)

            rows_T(0)
            up_expert(0)
            rows_T(1)
            hidden_T(0)
            with pe.Fori(1, last1) as n:
                up_expert(n)
                rows_T(n + 1)
                down_expert(n - 1)
                hidden_T(n)
            up_expert(last1)
            down_expert(last2)
            hidden_T(last1)
            down_expert(last1)

        @block.scalar
        def _(act):
            fn = nc.scalar.activation

            def high(name, pair, landed):
                act.wait_ge(landed, 16)
                fn(pair[0], pair[2], ACT.Copy).then_inc(w_high, 1)

            def keys_T(b, g):
                act.wait_ge(kT_mm, b * 4 + g + 1)
                fn(kT[:, g, :], ps[:, 3 + g % 2, 0:TE], ACT.Identity, bias=cols[:, 4 + g:5 + g]
                   ).then_inc(kT_sv, 1)

            def values(b, c):
                act.wait_ge(k1_mm, b * 3 + c + 1)
                if not (isinstance(b, int) and b == 0 and c == 0):
                    act.wait_ge(k1_sv, b * 3 + c)
                fn(kexp, ps[0:TP, 4, :], ACT.Exp).then_inc(k1_exp, 1)
                act.wait_ge(v1_mm, b * 3 + c + 1)
                fn(v1[:, c, :, 0:P], ps[0:TP, 5, :].rearrange("p (g e) -> p g e", g=G), ACT.Copy
                   ).then_inc(v1_sv, 1)

            def ln(n):
                act.wait_ge(ln_var, n + 1)
                fn(std[:, n:n + 1], mv[:, n, 1:2], ACT.Sqrt, bias=eps[:, 0:1]).then_inc(ln_std, 1)

            def ln_save(n):
                t = n % NT
                act.wait_ge(ln_tr, n + 1)
                fn(hT[0][:, :, t * P:(t + 1) * P], ps[:, ln_bank(n), :].rearrange("p (k t) -> p k t", k=KC),
                   ACT.Copy).then_inc(ln_H, 1)

            def context_high(slot, loads):
                act.wait_ge(ctx_ld[slot], loads)
                fn(ctxT[slot][0], ctxT[slot][2], ACT.Copy).then_inc(c_high, 1)

            def heads_save(b):
                act.wait_ge(ct_mm, b + 1)
                act.sem_inc(act_held, 1)
                fn(hT[0][:, :, bass.ds(b * S, S)], ps[:, 5, 0:KC * S].rearrange("p (k t) -> p k t", k=KC), ACT.Copy
                   ).then_inc(ct_high, 1)

            def feed_high(i, pair, landed, freed=None):
                act.wait_ge(landed, 16)
                if freed is not None:
                    act.wait_ge(ff_mm, freed)
                fn(pair[0], pair[2], ACT.Copy).then_inc(gu_high, 1)

            context_high(0, 16)
            high("wk0", wk0, wk0_ld)
            act.wait_ge(small_ld, 48)
            fn(tg[:], scal[:, 0:4], ACT.Tanh).then_inc(tanh_set, 1)
            act.wait_ge(eps_set, 1)
            for t in range(NT):
                ln(t)
            keys_T(0, 0)
            keys_T(0, 1)
            ln_save(0)
            act.wait_ge(wq0_ld, 16)
            fn(wq0[0], wq0[2], ACT.Copy).then_inc(wq0_high, 1)
            ln_save(1)
            keys_T(0, 2)
            ln_save(2)
            keys_T(0, 3)
            for t in range(3, NT):
                ln_save(t)
            for i in range(8):
                n, m = i // 4, i % 4
                act.wait_ge(q0_mm, i + 1)
                fn(qT[:, m, n * HALF:(n + 1) * HALF], ps[:, i % 2, 0:HALF], ACT.Identity,
                   bias=cols[:, m:m + 1]).then_inc(q0_sv, 1)
                if i == 2:
                    high("wv0", wv0, wv0_ld)
                if i == 3:
                    high("wkv1", wkv1, wkv1_ld)
                if i == 5:
                    act.wait_ge(gate_ld, 16)
                    fn(gate_r[:, 0, :], gate_w[:], ACT.Copy).then_inc(w_high, 1)
                    context_high(1, 16)
            for c in range(TC):
                values(0, c)
            act.wait_ge(mask_set, 2)

            def batch(b, slot, first=False, more=True, split=None):
                for g in range(G):
                    act.wait_ge(clipped, b * 4 + g + 1)
                    act.sem_inc(act_held, 1)
                    for c in range(TC):
                        done = fn(probs[g % 2][:, c, :], probs[g % 2][:, c, :], ACT.Exp,
                                  bias=mbias[:, bass.ds(b * 3 + c, 1)], scale=mscale[:, bass.ds(b * 3 + c, 1)])
                    done.then_inc(exped, 1)
                    if g == 1 and not first:
                        heads_save(b - 1)
                    if g == 2 and split is not None:
                        context_high(slot, split)
                    if more and g < 3:
                        values(b + 1, g)
                    if more and g == 3:
                        for gg in range(G):
                            keys_T(b + 1, gg)

            batch(0, 0, first=True, split=32)
            with act.Fori(1, B - 4, 2) as b:
                batch(b, 1, split=b * 8 + 24)
                batch(b + 1, 0, split=b * 8 + 40)
            batch(B - 3, 1, split=B * 8)
            batch(B - 2, 0)
            high("wo0", wo0, wo0_ld)

            def delta_std(t):
                act.wait_ge(d_var, t + 1)
                fn(dstd[:, t:t + 1], dmv[:, t, 1:2], ACT.Sqrt, bias=eps[:, 0:1]).then_inc(d_std, 1)

            for g in range(G):
                act.wait_ge(clipped, (B - 1) * 4 + g + 1)
                for c in range(TC):
                    b = (B - 1) * 3 + c
                    done = fn(probs[g % 2][:, c, :], probs[g % 2][:, c, :], ACT.Exp,
                              bias=mbias[:, b:b + 1], scale=mscale[:, b:b + 1])
                done.then_inc(exped, 1)
                if g == 1:
                    heads_save(B - 2)
                if g >= 2:
                    feed_high(g - 2, gu0[g - 2], gu0_ld[g - 2])
                if g >= 1:
                    ln(NT + g - 1)
                delta_std(g)
                if g < G - 1:
                    fn(warm[:, g:g + 1], eps[:], ACT.Exp)
            heads_save(B - 1)
            ln(NT + 3)
            delta_std(4)
            delta_std(5)
            for t in range(3):
                ln_save(NT + t)
            delta_std(6)
            ln_save(NT + 3)
            for t in range(4, NT):
                ln(NT + t)
            for t in range(4, NT):
                ln_save(NT + t)

            for m in range(MC):
                if m + 2 < MC:
                    feed_high(m + 2, gu0[m + 2], gu0_ld[m + 2], m - 1 if m >= 2 else None)
                act.wait_ge(ff_mm, m + 1)
                if m >= 2:
                    act.wait_ge(ff_h, m - 1)
                fn(silu0[m % 2], ps[:, 4 * (1 - m % 2):4 * (1 - m % 2) + 2, 0:HALF], ACT.Silu,
                   scale=cols[:, 12 + m:13 + m]).then_inc(ff_silu, 1)

            for t in range(NT):
                ln(2 * NT + t)
                if t == 1:
                    high("wq1", wq1, wq1_ld)
                if t == 2:
                    high("wg1", wg1, wg1_ld)
                if t == 3:
                    high("wo1", wo1, wo1_ld)
                if t >= 2:
                    ln_save(2 * NT + t - 2)
            ln_save(3 * NT - 2)
            ln_save(3 * NT - 1)
            for i in range(8):
                act.wait_ge(q1_mm, i + 1)
                if i >= 1:
                    act.wait_ge(q1_sv, i)
                fn(qexp, ps[:, 4 + i % 4, 0:HALF], ACT.Exp).then_inc(q1_exp, 1)
                if i < HG:
                    r = slice(i * HD, (i + 1) * HD)
                    act.wait_ge(ksbd_set, 1)
                    fn(ksbd[r, :, r], ks[r].rearrange("p b g -> p (b g)").unsqueeze(2).broadcast_to([HD, B * G, HD]),
                       ACT.Copy).then_inc(ksbd_set, 1)

            def gated_high(i):
                n, m = i // 4, i % 4
                act.wait_ge(gated, i + 1)
                act.wait_ge(g1_mm, 4 * n + 4)
                fn(hT[0][:, m, n * HALF:(n + 1) * HALF], qT[:, m, n * HALF:(n + 1) * HALF], ACT.Copy
                   ).then_inc(at_high, 1)

            for i in range(8):
                n, m = i // 4, i % 4
                act.wait_ge(g1_mm, i + 1)
                fn(gT[:, m, n * HALF:(n + 1) * HALF], ps[:, 4 + i % 4, 0:HALF], ACT.Sigmoid,
                   bias=cols[:, 8 + m:9 + m]).then_inc(g1_sv, 1)
                if i >= 4:
                    gated_high(i - 4)
            for i in range(4, 8):
                gated_high(i)
            for t in range(NT):
                ln(3 * NT + t)
                if t >= 2:
                    ln_save(3 * NT + t - 2)
                if t in (3, 4):
                    feed_high(MC + t - 3, sh13[t - 3], sh13_ld[t - 3])
            ln_save(4 * NT - 2)
            ln_save(4 * NT - 1)
            act.wait_ge(lg_max, 1)
            fn(prob.rearrange("p t e -> p (t e)"), prob.rearrange("p t e -> p (t e)"), ACT.Exp).then_inc(lg_exp, 1)
            for m, size in enumerate(SH_CHUNKS):
                if m == 1:
                    act.wait_ge(filled, 16)
                if m + 2 < 6:
                    feed_high(MC + m + 2, sh13[m + 2], sh13_ld[m + 2], MC + m - 1 if m >= 2 else None)
                act.wait_ge(ff_mm, MC + m + 1)
                act.wait_ge(ff_h, MC + m - 1)
                fn(silu1[m % 2][0:size], ps[0:size, 4 * (1 - m % 2):4 * (1 - m % 2) + 2, 0:HALF], ACT.Silu
                   ).then_inc(ff_silu, 1)

            act.wait_ge(tables_set, 1)
            last3, last2, last1, tiles = counts(act)

            def rows_save(n):
                act.wait_ge(xg_tr, n + 1)
                fn(xgT, ps[:, 6, :].rearrange("p (k t) -> p k t", k=KC), ACT.Copy).then_inc(xg_sv, 1)

            def silu_tile(n):
                act.wait_ge(gu_mm, n + 1)
                fn(smoe, ps[:, 4, 0:EI], ACT.Silu).then_inc(m_silu, 1)

            rows_save(0)
            with act.Fori(0, last1) as n:
                silu_tile(n)
                rows_save(n + 1)
            silu_tile(last1)

        @block.vector
        def _(dve):
            v = nc.vector
            count = [0]

            def then(ins):
                count[0] += 1
                ins.then_inc(dve_step, 1)
                dve.wait_ge(dve_step, count[0])

            def low(name, pair):
                dve.wait_ge(w_high, nth(name))
                v.tensor_tensor(pair[1], pair[2], pair[0].bitcast(F32), ALU.subtract).then_inc(w_low, 1)

            def context_low(slot, b):
                dve.wait_ge(c_high, b + 1)
                v.tensor_tensor(ctxT[slot][1], ctxT[slot][2], ctxT[slot][0].bitcast(F32), ALU.subtract
                                ).then_inc(c_low, 1)

            def feed_low(i, pair):
                dve.wait_ge(gu_high, i + 1)
                v.tensor_tensor(pair[1], pair[2], pair[0].bitcast(F32), ALU.subtract).then_inc(gu_low, 1)

            def ln_stats(n):
                then(v.bn_stats(stats[:, n % 2, :], x[:, n % NT, :]))
                v.bn_aggr(mv[:, n, :], stats[:, n % 2, :]).then_inc(ln_var, 1)

            def ln_norm(n):
                dve.wait_ge(ln_std, n + 1)
                then(v.reciprocal(rstd[:, n:n + 1], std[:, n:n + 1]))
                if n >= 2:
                    dve.wait_ge(ln_tr, n - 1)
                dst = h3[:, n % NT, :] if n >= 3 * NT else lnt[:, n % 2, :]
                v.tensor_scalar(dst, x[:, n % NT, :], mv[:, n, 0:1], rstd[:, n:n + 1], ALU.subtract, ALU.mult
                                ).then_inc(ln_out, 1)

            def ln_low(n):
                t = n % NT
                dve.wait_ge(ln_H, n + 1)
                v.tensor_tensor(hT[1][:, :, t * P:(t + 1) * P],
                                ps[:, ln_bank(n), :].rearrange("p (k t) -> p k t", k=KC),
                                hT[0][:, :, t * P:(t + 1) * P].bitcast(F32), ALU.subtract).then_inc(ln_T, 1)

            v.memset(eps[:], LN_EPS).then_inc(eps_set, 1)
            context_low(0, 0)
            low("wk0", wk0)
            dve.wait_ge(small_ld, 48)
            then(v.tensor_scalar(mscale[:], mask_i[:], 0.5, None, ALU.is_gt))
            v.tensor_scalar(mbias[:], mscale[:], CLIP, -CLIP, ALU.mult, ALU.add).then_inc(mask_set, 1)
            dve.wait_ge(mask_set, 1)
            v.tensor_scalar(mscale[:], mscale[:], SCALE, None, ALU.mult).then_inc(mask_set, 1)
            dve.wait_ge(x_ld, 16)
            for t in range(NT):
                ln_stats(t)
                if t == 2:
                    ln_norm(0)
            for t in range(1, NT):
                ln_norm(t)
                ln_low(t - 1)
            ln_low(NT - 1)
            then(v.tensor_scalar(rs[:], scal[:, 4:5], 0.0, 0.3, ALU.max, ALU.min))
            low("wv0", wv0)
            low("wkv1", wkv1)
            dve.wait_ge(w_high, nth("gate"))
            v.tensor_tensor(gate_r[:, 1, :], gate_w[:], gate_r[:, 0, :].bitcast(F32), ALU.subtract).then_inc(w_low, 1)
            context_low(1, 1)
            dve.wait_ge(q0_mm, 8)
            for slot in range(2):
                v.memset(v0[slot][:, :, :, HD:HD + 1], 1.0).then_inc(ones_set, 1)
            v.memset(v1[:, :, :, P:P + 1], 1.0).then_inc(ones_set, 1)
            dve.wait_ge(bv_ld, 16)

            def values(b, slot, c):
                dve.wait_ge(v0_mm, b * 3 + c + 1)
                v.tensor_tensor(v0[slot][:, c, :, 0:HD], ps[0:TP, 3, :].rearrange("p (h d) -> p h d", h=H),
                                bv[0:TP].rearrange("p (h d) -> p h d", h=H), ALU.add).then_inc(v0_sv, 1)
                dve.wait_ge(k1_exp, b * 3 + c + 1)
                v.tensor_scalar(k1[:, c, :], ps[0:TP, 4, :], 0.0, None, ALU.max).then_inc(k1_relu, 1)
                dve.wait_ge(k1_relu, b * 3 + c + 1)
                v.scalar_tensor_tensor(k1[:, c, :], kexp, 1.0, k1[:, c, :], ALU.min, ALU.add).then_inc(k1_sv, 1)

            ks_flat = ks[:].rearrange("p b g -> p (b g)")

            def kv_save(b):
                for pair in range(2):
                    dve.wait_ge(kv_mm, b * 2 + pair + 1)
                    bank = ps[:, 3 + pair, 0:2 * 129].rearrange("p (g e) -> p g e", g=2)
                    for h in range(HG):
                        r = slice(h * HD, (h + 1) * HD)
                        v.tensor_scalar(kvc[r, bass.ds(b * G + 2 * pair, 2), :], bank[r, :, h * HD:(h + 1) * HD],
                                        1.0, None, ALU.mult)
                    v.tensor_copy(ks_flat[:, bass.ds(b * G + 2 * pair, 2)], bank[:, :, P]).then_inc(kv_sv, 1)

            for c in range(TC):
                values(0, 0, c)
            kv_save(0)

            def clip(b, g, guard):
                dve.wait_ge(sc_mm, b * 4 + g + 1)
                if guard:
                    dve.wait_ge(pv_mm, b * 4 + g - 1)
                v.tensor_scalar(probs[g % 2], ps[0:TP, 0:TC, 0:HG * S], -CLIP / SCALE, CLIP / SCALE,
                                ALU.max, ALU.min).then_inc(clipped, 1)

            def normalise(b, half, first):
                dve.wait_ge(pv_mm, b * 4 + 2 * half + 2)
                bank = ps[0:S, 6 + half, 0:8 * 33].rearrange("p (h e) -> p h e", h=8)
                v.tensor_copy(zsum[:, half, :], bank[:, :, HD]).then_inc(norm_step, 1)
                dve.wait_ge(norm_step, b * 6 + 3 * half + 1)
                v.scalar_tensor_tensor(zinv[:, half, :], zsum[:, half, :], P_EPS, zsum[:, half, :], ALU.mult, ALU.add
                                       ).then_inc(norm_step, 1)
                dve.wait_ge(norm_step, b * 6 + 3 * half + 2)
                v.reciprocal(zinv[:, half, :], zinv[:, half, :]).then_inc(norm_step, 1)
                dve.wait_ge(norm_step, b * 6 + 3 * half + 3)
                if not first:
                    dve.wait_ge(ct_mm, b)
                v.tensor_tensor(ctok[:, half * 256:(half + 1) * 256].rearrange("p (h d) -> p h d", h=8),
                                bank[:, :, 0:HD], zinv[:, half, :].unsqueeze(2).broadcast_to([S, 8, HD]),
                                ALU.mult).then_inc(normed, 1)

            def heads_low(b):
                dve.wait_ge(ct_high, b + 1)
                v.tensor_tensor(hT[1][:, :, bass.ds(b * S, S)], ps[:, 5, 0:KC * S].rearrange("p (k t) -> p k t", k=KC),
                                hT[0][:, :, bass.ds(b * S, S)].bitcast(F32), ALU.subtract).then_inc(ct_sv, 1)

            def batch(b, slot, first=False, more=True, split=True):
                for g in range(G):
                    clip(b, g, not (first and g < 2))
                    if g == 1 and not first:
                        heads_low(b - 1)
                    if g == 2:
                        normalise(b, 0, first)
                        if split:
                            context_low(slot, b + 2)
                    if more and g < 3:
                        values(b + 1, 1 - slot, g)
                normalise(b, 1, first)
                if more:
                    kv_save(b + 1)

            batch(0, 0, first=True)
            with dve.Fori(1, B - 4, 2) as b:
                batch(b, 1)
                batch(b + 1, 0)
            batch(B - 3, 1)
            batch(B - 2, 0, split=False)
            low("wo0", wo0)

            bo, gamma, beta, down_s = (rows[:, i * D:(i + 1) * D] for i in range(4))

            def delta(t):
                dve.wait_ge(y_mm, t + 1)
                if t >= 5:
                    dve.wait_ge(ln_var, NT + t - 4)
                v.scalar_tensor_tensor(dtile[t % 5], ps[:, y_bank(t), :], rs[:, 0:1], bo, ALU.mult, ALU.add
                                       ).then_inc(y_sv, 1)
                dve.wait_ge(y_sv, t + 1)
                then(v.bn_stats(stats[:, 0, :], dtile[t % 5]))
                v.bn_aggr(dmv[:, t, :], stats[:, 0, :]).then_inc(d_var, 1)

            def residual(t):
                d = dtile[t % 5]
                dve.wait_ge(d_std, t + 1)
                then(v.reciprocal(drstd[:, t:t + 1], dstd[:, t:t + 1]))
                then(v.scalar_tensor_tensor(d, d, dmv[:, t, 0:1], gamma, ALU.subtract, ALU.mult))
                dve.wait_ge(beta_set, t + 1)
                then(v.scalar_tensor_tensor(x[:, t, :], d, drstd[:, t:t + 1], x[:, t, :], ALU.mult, ALU.add))
                ln_stats(NT + t)

            for g in range(G):
                clip(B - 1, g, True)
                if g == 0:
                    dve.wait_ge(rows_ld, 16)
                    dve.wait_ge(tanh_set, 1)
                    v.tensor_scalar(beta, beta, tg[:, 0:1], None, ALU.mult).then_inc(rows_set, 1)
                    v.tensor_scalar(bo, bo, rs[:, 0:1], None, ALU.mult).then_inc(rows_set, 1)
                    v.tensor_scalar(gamma, gamma, tg[:, 0:1], None, ALU.mult).then_inc(rows_set, 1)
                    dve.wait_ge(rows_set, 3)
                if g == 1:
                    heads_low(B - 2)
                if g == 2:
                    normalise(B - 1, 0, False)
                if g >= 1:
                    residual(g - 1)
                delta(g)
                if g >= 2:
                    feed_low(g - 2, gu0[g - 2])
            normalise(B - 1, 1, False)
            heads_low(B - 1)
            ln_norm(NT)
            residual(3)
            ln_norm(NT + 1)
            delta(4)
            delta(5)
            ln_norm(NT + 2)
            ln_low(NT)
            ln_norm(NT + 3)
            ln_low(NT + 1)
            ln_low(NT + 2)
            delta(6)
            ln_low(NT + 3)
            residual(4)
            ln_norm(NT + 4)
            residual(5)
            ln_norm(NT + 5)
            residual(6)
            ln_low(NT + 4)
            ln_norm(NT + 6)
            ln_low(NT + 5)
            ln_low(NT + 6)
            v.tensor_scalar(down_s, down_s, tg[:, 2:3], None, ALU.mult).then_inc(rows_set, 1)

            def hidden(i, m, size, scale, silu, into):
                dve.wait_ge(ff_mm, i + 1)
                dve.wait_ge(ff_silu, i + 1)
                v.scalar_tensor_tensor(into[0:size].rearrange("p (n t) -> p n t", n=2),
                                       ps[0:size, 4 * (1 - m % 2) + 2:4 * (1 - m % 2) + 4, 0:HALF], scale,
                                       silu[0:size], ALU.mult, ALU.mult).then_inc(ff_h, 1)

            for m in range(MC):
                if m + 2 < MC:
                    feed_low(m + 2, gu0[m + 2])
                hidden(m, m, P, cols[:, 12 + MC + m:13 + MC + m], silu0[m % 2], h0[m])
            dve.wait_ge(rows_set, 4)
            for t in range(NT):
                dve.wait_ge(y_mm, NT + t + 1)
                v.tensor_tensor(ytmp, ps[:, y_bank(NT + t), :], down_s, ALU.mult).then_inc(y_sv, 1)
                dve.wait_ge(y_sv, NT + t + 1)
                then(v.tensor_tensor(x[:, t, :], x[:, t, :], ytmp, ALU.add))
                ln_stats(2 * NT + t)
                if t >= 1:
                    ln_norm(2 * NT + t - 1)
                if t == 1:
                    low("wq1", wq1)
                if t == 2:
                    low("wg1", wg1)
                if t == 3:
                    low("wo1", wo1)
                if t >= 2:
                    ln_low(2 * NT + t - 2)
            ln_norm(3 * NT - 1)
            ln_low(3 * NT - 2)
            ln_low(3 * NT - 1)

            def query(i):
                n, m = i // 4, i % 4
                dve.wait_ge(q1_exp, i + 1)
                v.tensor_scalar(qrelu, ps[:, 4 + i % 4, 0:HALF], 0.0, None, ALU.max).then_inc(q1_relu, 1)
                dve.wait_ge(q1_relu, i + 1)
                v.scalar_tensor_tensor(qT[:, m, n * HALF:(n + 1) * HALF], qexp, 1.0, qrelu, ALU.min, ALU.add
                                       ).then_inc(q1_sv, 1)
                dve.wait_ge(q1_sv, i + 1)

            def attend(b):
                dve.wait_ge(at_mm, b + 1)
                then(v.tensor_scalar(zrec, ps[:, 2 + b % 2, 0:G * S].rearrange("p (g t) -> p g t", g=G),
                                     Z_EPS, None, ALU.add))
                then(v.reciprocal(zrec, zrec))
                v.tensor_tensor(qT[:, :, b * S:(b + 1) * S], ps[:, b % 2, 0:G * S].rearrange("p (g t) -> p g t", g=G),
                                zrec, ALU.mult).then_inc(at_sv, 1)
                dve.wait_ge(at_sv, b + 1)

            def gate(i):
                n, m = i // 4, i % 4
                dve.wait_ge(g1_sv, i + 1)
                v.tensor_tensor(qT[:, m, n * HALF:(n + 1) * HALF], qT[:, m, n * HALF:(n + 1) * HALF],
                                gT[:, m, n * HALF:(n + 1) * HALF], ALU.mult).then_inc(gated, 1)

            def gated_low(i):
                n, m = i // 4, i % 4
                dve.wait_ge(at_high, i + 1)
                v.tensor_tensor(hT[1][:, m, n * HALF:(n + 1) * HALF], qT[:, m, n * HALF:(n + 1) * HALF],
                                hT[0][:, m, n * HALF:(n + 1) * HALF].bitcast(F32), ALU.subtract).then_inc(at_low, 1)

            for i in range(5):
                query(i)
                if i < HG:
                    r = slice(i * HD, (i + 1) * HD)
                    dve.wait_ge(kvbd_set, 1)
                    v.tensor_copy(kvbd[r, :, r], kvc[r, :, :]).then_inc(kvbd_set, 1)
            for b in range(3):
                attend(b)
                query(5 + b)
            for b in range(3, B):
                attend(b)
                if b >= 4:
                    gate(b - 4)
            for i in range(4):
                gated_low(i)
            for i in range(4, 8):
                gate(i)
                gated_low(i)
            for t in range(NT):
                dve.wait_ge(y_mm, 2 * NT + t + 1)
                v.scalar_tensor_tensor(x[:, t, :], ps[:, (2 * NT + t) % 2, :], tg[:, 1:2], x[:, t, :], ALU.mult, ALU.add
                                       ).then_inc(y_sv, 1)
                dve.wait_ge(y_sv, 2 * NT + t + 1)
                ln_stats(3 * NT + t)
                if t >= 1:
                    ln_norm(3 * NT + t - 1)
                if t >= 2:
                    ln_low(3 * NT + t - 2)
                if t in (3, 4):
                    feed_low(MC + t - 3, sh13[t - 3])
            ln_norm(4 * NT - 1)
            ln_low(4 * NT - 2)
            ln_low(4 * NT - 1)

            dve.wait_ge(lg_mm, 1)
            dve.wait_ge(tri_set, 4)
            lg = ps[:, 1, 0:RT].rearrange("p (t e) -> p t e", t=NT)
            then(v.tensor_reduce(rmax, lg, AX.X, ALU.max))
            v.tensor_tensor(prob, lg, rmax.unsqueeze(2).broadcast_to([P, NT, NE]), ALU.subtract).then_inc(lg_max, 1)
            dve.wait_ge(lg_exp, 1)
            v.memset(hmoe[:, EI:3 * P], 0.0).then_inc(lg_sv, 1)
            feed_low(MC + 2, sh13[2])
            then(v.tensor_reduce(rsum, prob, AX.X, ALU.add))
            then(v.reciprocal(rsum, rsum))
            then(v.tensor_tensor(prob, prob, rsum.unsqueeze(2).broadcast_to([P, NT, NE]), ALU.mult))
            for t in range(NT):
                then(v.max(top8[:, t, :], prob[:, t, :]))
                then(v.max_index(idx8[:, t, :], top8[:, t, :], prob[:, t, :]))
            then(v.tensor_copy(idxf, idx8[:, :, 0:2]))
            then(v.tensor_scalar(wtop[:], top8[:, :, 0:2], tg[:, 3:4], None, ALU.mult))
            ids = iota16.unsqueeze(1).broadcast_to([P, NT, NE])
            then(v.tensor_tensor(one0, ids, idxf[:, :, 0:1].broadcast_to([P, NT, NE]), ALU.is_equal))
            then(v.tensor_tensor(one1, ids, idxf[:, :, 1:2].broadcast_to([P, NT, NE]), ALU.is_equal))
            then(v.tensor_tensor(both, one0, one1, ALU.add))
            v.memset(scan[0][:, 0:16], 0.0).then_inc(both_set, 1)
            v.memset(scan[1][:, 0:16], 0.0)
            for m, size in enumerate(SH_CHUNKS):
                if 3 <= m + 2 < 6:
                    feed_low(MC + m + 2, sh13[m + 2])
                hidden(MC + m, m, size, 1.0, silu1[m % 2], hsh[m])

            dve.wait_ge(rank_mm, 1)
            rank = ps[:, 6, 0:RT].rearrange("p (t e) -> p t e", t=NT)
            total = ps[:, 7, 0:RT].rearrange("p (t e) -> p t e", t=NT)
            then(v.memset(cnt, 0.0))
            for t in range(NT):
                then(v.tensor_tensor(place_[:, t, :], rank[:, t, :], cnt, ALU.add))
                then(v.tensor_tensor(cnt, cnt, total[:, t, :], ALU.add))
            c3 = cmp[:, 0:NE * NT].rearrange("p (e k) -> p e k", e=NE)
            then(v.tensor_tensor(c3, cnt.unsqueeze(2).broadcast_to([P, NE, NT]),
                                 thr.unsqueeze(1).broadcast_to([P, NE, NT]), ALU.is_gt))
            then(v.tensor_reduce(ntile, c3, AX.X, ALU.add))
            then(v.tensor_scalar(scan[0][:, 16:32], ntile, 1.0, None, ALU.max))
            then(v.tensor_copy(ntile, scan[0][:, 16:32]))
            for i in range(4):
                a, b_ = scan[i % 2], scan[1 - i % 2]
                then(v.tensor_tensor(b_[:, 16:32], a[:, 16:32], a[:, 16 - 2 ** i:32 - 2 ** i], ALU.add))
            ends = scan[0][:, 16:32]
            then(v.tensor_tensor(nstart, ends, ntile, ALU.subtract))
            then(v.tensor_scalar(nstart, nstart, float(P), None, ALU.mult))
            then(v.tensor_tensor(place_, place_, nstart.unsqueeze(1).broadcast_to([P, NT, NE]), ALU.add))
            for j, one in enumerate((one0, one1)):
                then(v.tensor_tensor(tmp16, place_, one, ALU.mult))
                then(v.tensor_reduce(fdest, tmp16, AX.X, ALU.add))
                v.tensor_copy(dest[:, j, :], fdest).then_inc(dest_set, 1)
                dve.wait_ge(dest_set, j + 1)
            then(v.tensor_copy(expert_end[:], ends))
            for i in range(4):
                then(v.tensor_scalar(tile_count[:, i:i + 1], ends[:, NE - 1:NE], float(i - 3), None, ALU.add))
            c4 = cmp.rearrange("p (n e) -> p n e", n=32)
            then(v.tensor_tensor(c4, iota29.unsqueeze(2).broadcast_to([P, 32, NE]),
                                 ends.unsqueeze(1).broadcast_to([P, 32, NE]), ALU.is_ge))
            then(v.tensor_reduce(texpf, c4, AX.X, ALU.add))
            v.tensor_copy(tile_expert[:], texpf).then_inc(tables_set, 1)
            for t in range(NT):
                dve.wait_ge(y_mm, 3 * NT + t + 1)
                v.scalar_tensor_tensor(x[:, t, :], ps[:, (3 * NT + t) % 2, :], tg[:, 3:4], x[:, t, :], ALU.mult, ALU.add
                                       ).then_inc(y_sv, 1)

            dve.wait_ge(tables_set, 1)
            last3, last2, last1, tiles = counts(dve)

            def tile_hidden(n):
                dve.wait_ge(gu_mm, n + 1)
                dve.wait_ge(m_silu, n + 1)
                if not (isinstance(n, int) and n == 0):
                    dve.wait_ge(hx_tr, n)
                v.tensor_tensor(hmoe[:, 0:EI], ps[:, 5, 0:EI], smoe, ALU.mult).then_inc(m_h, 1)

            def tile_hidden_save(n):
                dve.wait_ge(hx_tr, n + 1)
                v.tensor_copy(hmoeT, ps[:, 7, 0:3 * P].rearrange("p (c t) -> p c t", c=3)).then_inc(hx_sv, 1)

            def tile_out(n, stored=None):
                dve.wait_ge(d_mm, n + 1)
                if stored is not None:
                    dve.wait_ge(y_st, stored)
                v.tensor_scalar(arena[:, bass.ds(A_YR + (n % 2) * D, D)], ps[:, 3, :], 1.0, None, ALU.mult
                                ).then_inc(d_sv, 1)

            tile_hidden(0)
            tile_hidden_save(0)
            tile_hidden(1)
            tile_out(0)
            tile_hidden_save(1)
            tile_hidden(2)
            tile_out(1)
            tile_hidden_save(2)
            with dve.Fori(3, tiles) as n:
                tile_hidden(n)
                tile_out(n - 1, n * 16 - 32)
                tile_hidden_save(n)
            tile_out(last1, last2 * 16)

            for t in range(NT):
                dve.wait_ge(back_ld[t], 32)
                for j in range(2):
                    last = v.scalar_tensor_tensor(x[:, t, :], back[t][j], wtop[:, t, j:j + 1], x[:, t, :],
                                                  ALU.mult, ALU.add)
                    if j == 0:
                        then(last)
                last.then_inc(out_st, 1)

        @block.gpsimd
        def _(pool):
            nc.gpsimd.memset(ident[:], 0.0).then_inc(pool_step, 1)
            pool.wait_ge(pool_step, 1)
            nc.gpsimd.affine_select(out=ident[:], in_=ident[:], compare_op=ALU.not_equal, fill=1.0, base=0,
                                    pattern=[[-1, P]], channel_multiplier=1).then_inc(consts_set, 1)
            nc.gpsimd.memset(qbd, 0.0).then_inc(pool_step, 1)
            pool.wait_ge(wq0_high, 1)
            nc.gpsimd.tensor_tensor(wq0[1], wq0[2], wq0[0].bitcast(F32), ALU.subtract).then_inc(wq0_low, 1)
            pool.wait_ge(pool_step, 2)
            pool.wait_ge(q0_sv, 8)

            def spread(b):
                for h in range(HG):
                    r = slice(h * HD, (h + 1) * HD)
                    nc.gpsimd.tensor_copy(qbd[r, :, h, :], qT[r, :, bass.ds(b * S, S)]).then_inc(q_spread, 1)

            spread(0)
            with pool.Fori(1, B) as b:
                pool.wait_ge(sc_mm, b * 4)
                spread(b)

            pool.wait_ge(rows_set, 1)
            for t in range(NT):
                nc.gpsimd.tensor_tensor(x[:, t, :], x[:, t, :], rows[:, 2 * D:3 * D], ALU.add).then_inc(beta_set, 1)

            pool.wait_ge(y_mm, 2 * NT)
            nc.gpsimd.memset(kvbd, 0.0).then_inc(kvbd_set, 1)
            nc.gpsimd.memset(ksbd, 0.0).then_inc(ksbd_set, 1)
            nc.gpsimd.memset(zero, 0.0).then_inc(zero_set, 1)
            pool.wait_ge(zero_set, 1)
            pool.dma_start(xs_dram.rearrange("(t p) d -> p t d", p=P),
                           zero.unsqueeze(1).broadcast_to([P, ROWS_MAX, D])).then_inc(filled, 16)
            pool.wait_ge(at_low, 8)
            nc.gpsimd.iota(iota16, pattern=[[1, NE]], base=0, channel_multiplier=0,
                           allow_small_or_imprecise_dtypes=True).then_inc(tri_set, 1)
            nc.gpsimd.iota(thr, pattern=[[P, NT]], base=0, channel_multiplier=0,
                           allow_small_or_imprecise_dtypes=True)
            nc.gpsimd.iota(iota29, pattern=[[1, 32]], base=0, channel_multiplier=0,
                           allow_small_or_imprecise_dtypes=True).then_inc(tri_set, 1)
            nc.gpsimd.memset(ones, 1.0).then_inc(tri_set, 1)
            pool.wait_ge(tri_set, 3)
            nc.gpsimd.affine_select(out=lower, in_=ones, compare_op=ALU.is_gt, fill=0.0, base=0,
                                    pattern=[[1, P]], channel_multiplier=-1).then_inc(tri_set, 1)
            pool.wait_ge(filled, 16)
            pool.wait_ge(dest_set, 2)
            pool.wait_ge(ln_out, 4 * NT)
            for j in range(2):
                for t in range(NT):
                    pool.indirect_dma_start(xs_dram, bass.IndirectOffsetOnAxis(dest[:, j, t:t + 1], 0),
                                            h3[:, t, :], None).then_inc(scattered, 16)
            pool.wait_ge(scattered, 16 * 2 * NT)
            pool.wait_ge(tables_set, 1)
            last3, last2, last1, tiles = counts(pool)

            def load(n):
                pool.dma_start(arena[:, bass.ds(A_XR + (n % 2) * D, D)], xs_dram[bass.ds(n * P, P), :]
                               ).then_inc(xg_ld, 16)

            def place(n):
                nc.gpsimd.tensor_copy(xg, arena[:, bass.ds(A_XR + (n % 2) * D, D)]).then_inc(xs_rdy, 1)

            def store(n, stored=None):
                pool.wait_ge(d_sv, n + 1)
                if stored is not None:
                    pool.wait_ge(y_st, stored)
                pool.dma_start(xs_dram[bass.ds(n * P, P), :], arena[:, bass.ds(A_YR + (n % 2) * D, D)]
                               ).then_inc(y_st, 16)

            load(0)
            pool.wait_ge(xg_ld, 16)
            load(1)
            place(0)
            pool.wait_ge(xg_ld, 32)
            pool.wait_ge(xs_rdy, 1)
            load(2)
            pool.wait_ge(xg_tr, 1)
            place(1)
            pool.wait_ge(xg_ld, 48)
            pool.wait_ge(xs_rdy, 2)
            load(3)
            pool.wait_ge(xg_tr, 2)
            place(2)
            store(0)
            with pool.Fori(3, last1) as n:
                pool.wait_ge(xg_ld, n * 16 + 16)
                pool.wait_ge(xs_rdy, n)
                load(n + 1)
                pool.wait_ge(xg_tr, n)
                place(n)
                store(n - 2, n * 16 - 32)
            pool.wait_ge(xg_ld, tiles * 16)
            pool.wait_ge(xg_tr, last1)
            place(last1)
            store(last3, last3 * 16)
            store(last2, last2 * 16)
            store(last1, last1 * 16)
            pool.wait_ge(y_st, tiles * 16)
            pool.sem_inc(pool_held, 1)
            for t in range(NT):
                for j in range(2):
                    pool.indirect_dma_start(back[t][j], None, xs_dram,
                                            bass.IndirectOffsetOnAxis(dest[:, j, t:t + 1], 0)).then_inc(back_ld[t], 16)


def kernel(**inputs):
    import numpy as np
    import concourse.bacc as bacc
    from concourse.bass_utils import run_bass_kernel_spmd

    a = {k: np.asarray(v) for k, v in inputs.items()}

    def w_t(w):
        o, i = w.shape
        return np.ascontiguousarray(w.T.reshape(i // P, P, o).transpose(1, 0, 2))

    def col(v):
        return v.reshape(-1, P).T

    def gate_up_chunks(gate, up, at, size):
        return np.concatenate([w_t(gate[at:at + size]), w_t(up[at:at + size])], axis=1)

    c = np.ascontiguousarray
    feeds = {
        "x": c(a["x"].reshape(TOK, D)),
        "ctx": c(np.pad(a["ctx_2048"].transpose(0, 2, 1), ((0, 0), (0, 0), (0, TE - T)))
                 .reshape(B, KC, P, TE).transpose(0, 2, 1, 3)),
        "mask": c(a["mask_BxS2_ik0"].reshape(B, TC, TP).transpose(2, 0, 1).reshape(TP, B * TC)),
        "cols": c(np.concatenate([col(a["L0_xattn_bq"]), col(a["L0_xattn_bk"]), col(a["L1_xattn_bg"]),
                                  col(a["L0_ffn_gate_s"]), col(a["L0_ffn_up_s"])], axis=1)),
        "rows": c(np.concatenate([a["L0_xattn_bv"], a["L0_xattn_bo"], a["L0_xattn_ln_gamma"],
                                  a["L0_xattn_ln_beta"], a["L0_ffn_down_s"]])),
        "scal": c(np.concatenate([a["g_xattn"], a["g_ffn"], a["L0_xattn_residual_scale"].reshape(1)])),
        "wq0": w_t(a["L0_xattn_Wq"]),
        "wk0": w_t(a["L0_xattn_Wk"]),
        "wv0": w_t(a["L0_xattn_Wv"]),
        "wo0": w_t(a["L0_xattn_Wo"]),
        "gu0": c(np.stack([gate_up_chunks(a["L0_ffn_gate_w"], a["L0_ffn_up_w"], m * P, P) for m in range(MC)])),
        "wd0": w_t(a["L0_ffn_down_w"]),
        "wq1": w_t(a["L1_xattn_Wq"]),
        "wg1": w_t(a["L1_xattn_Wg"]),
        "wkv1": w_t(a["L1_xattn_Wkv"]),
        "wo1": w_t(a["L1_xattn_Wo"]),
        "gate": w_t(a["L1_ffn_gate_w"]),
        "sh13": c(np.concatenate([gate_up_chunks(a["L1_ffn_sw1"], a["L1_ffn_sw3"], at, z).reshape(P, 2 * KC * z)
                                  for at, z in zip(SH_AT, SH_CHUNKS)], axis=1)),
        "sh2": c(a["L1_ffn_sw2"].T),
        "e13": c(np.concatenate([a["L1_ffn_w1"], a["L1_ffn_w3"]], axis=1).transpose(0, 2, 1)
                 .reshape(NE, KC, P, 2 * EI).transpose(0, 2, 1, 3).reshape(NE, P, KC * 2 * EI)),
        "e2": c(a["L1_ffn_w2"].transpose(0, 2, 1)),
    }
    nc = bacc.Bacc("TRN2", target_bir_lowering=False, num_devices=1)
    args = [nc.dram_tensor(f"in_{k}", v.shape, mybir.dt.from_np(v.dtype), kind="ExternalInput").ap()
            for k, v in feeds.items()]
    result = nc.dram_tensor("out_x", (TOK, D), F32, kind="ExternalOutput").ap()
    flamingo(nc, *args, result)
    r = run_bass_kernel_spmd(nc, [{f"in_{k}": v for k, v in feeds.items()}], core_ids=[0])
    return r.results[0]["out_x"].reshape(B, S, D)
```

```python
from contextlib import ExitStack

import concourse.bass as bass
from concourse import mybir

F32 = mybir.dt.float32
F32R = mybir.dt.float32r
I32 = mybir.dt.int32
U32 = mybir.dt.uint32
ALU = mybir.AluOpType
ACT = mybir.ActivationFunctionType
AX = mybir.AxisListType

P = 128
D = 512
KC = D // P
B, S, T = 8, 112, 375
TE = T + 1
TOK = B * S
NT = TOK // P
HALF = TOK // 2
TC, TP = 3, 125
H, HD = 16, 32
G = D // P
HG = P // HD
INTER = 1408
MC = INTER // P
SHARED = 704
SH_CHUNKS = [P] * 4 + [96] * 2
SH_AT = [sum(SH_CHUNKS[:i]) for i in range(6)]
SPARE = 4
NE = 16
EI = 352
E_CHUNKS = [P, P, EI - 2 * P]
NSLOT = 4
ROWS_MAX = 29
LN_EPS = 1e-5
Z_EPS = 1e-6
P_EPS = 1e-8
CLIP = 50.0
SCALE = float(HD) ** -0.5


def flamingo(nc, x_in, ctx_in, mask_in, cols_in, rows_in, scal_in, wq0_in, wk0_in, wv0_in, wo0_in,
             gu0_in, wd0_in, wq1_in, wg1_in, wkv1_in, wo1_in, gate_in, sh13_in, sh2_in,
             e13_in, e2_in, out):
    with ExitStack() as stack:
        def sb(name, shape, dt=F32):
            return stack.enter_context(nc.sbuf_tensor(name, shape, dt))

        def sem(name):
            return stack.enter_context(nc.semaphore(name))

        ps = stack.enter_context(nc.psum_tensor("ps", [P, 8, 512], F32))

        ident = sb("ident", [P, P])
        cols = sb("cols", [P, 12 + 2 * MC])
        scal = sb("scal", [P, 5])
        tg = sb("tg", [P, 4])
        rs = sb("rs", [P, 1])
        eps = sb("eps", [P, 1])
        z_eps = sb("z_eps", [P, 1])
        mask_i = sb("mask_i", [TP, B * TC], I32)
        mscale = sb("mscale", [TP, B * TC])
        mbias = sb("mbias", [TP, B * TC])
        stats = sb("stats", [P, 2, 6])
        mv = sb("mv", [P, 4 * NT, 2])
        std = sb("std", [P, 4 * NT])
        rstd = sb("rstd", [P, 4 * NT])
        dmv = sb("dmv", [P, NT, 2])
        dstd = sb("dstd", [P, NT])
        drstd = sb("drstd", [P, NT])
        warm = sb("warm", [P, G])
        ks = sb("ks", [P, B, G])
        zsum = sb("zsum", [S, 2, 8])
        zinv = sb("zinv", [S, 2, 8])
        gate_w = sb("gate_w", [P, KC * NE])
        gate_r = sb("gate_r", [P, 2, KC * NE], F32R)
        dest = sb("dest", [P, 2, NT], U32)
        wtop = sb("wtop", [P, NT, 2])
        tile_expert = sb("tile_expert", [P, 32], I32)
        expert_end = sb("expert_end", [P, NE], I32)
        tile_count = sb("tile_count", [P, 4], I32)
        idx8 = sb("idx8", [P, NT, 8], U32)

        WORDS = 48400
        x_base = -(-nc.sbuf_base // 32) * 32
        base = x_base + 4 * NT * D
        x = nc.alloc_sbuf_tensor_at("x", [P, NT, D], F32, offset=x_base)
        arena = nc.alloc_sbuf_tensor_at("arena", [P, WORDS], F32, offset=base)
        arena_r = nc.alloc_sbuf_tensor_at("arena_r", [P, WORDS], F32R, offset=base)

        def shaped(v, dims):
            if len(dims) == 2:
                return v.rearrange("p (a b) -> p a b", a=dims[0])
            if len(dims) == 3:
                return v.rearrange("p (a b c) -> p a b c", a=dims[0], b=dims[1])
            return v

        def at(off, *dims, rows_=P):
            n = 1
            for d in dims:
                n *= d
            return shaped(arena[0:rows_, off:off + n], dims)

        def at_r(off, *dims):
            n = 1
            for d in dims:
                n *= d
            return shaped(arena_r[:, off:off + n], dims)

        def landing(name, off, words):
            return off, nc.alloc_sbuf_tensor_at(name, [P, words], F32, offset=base + 4 * off)

        def halves(high, low, land, *dims):
            n = 1
            for d in dims:
                n *= d
            off, words = land
            return at_r(high, *dims), at_r(low, *dims), shaped(words[:, low - off:low - off + n], dims)

        A_HT, A_Q = 0, 2 * KC * TOK
        hT_both = nc.alloc_sbuf_tensor_at("hT", [P, 2, KC, TOK], F32R, offset=base + 4 * A_HT)
        hT = hT_both[:, 0], hT_both[:, 1]
        qT = at(A_Q, KC, TOK)
        A_KV = A_Q + KC * TOK
        A_BV = A_KV + B * G * HD
        A_LN = A_BV + D
        A_WL = A_LN + 2 * D
        A_WH = A_WL + 8192
        A_C = A_WH + 8192
        A_K = A_C + 4 * KC * TE
        A_V0 = A_K + KC * TE
        A_K1 = A_V0 + 2 * TC * H * (HD + 1)
        A_V1 = A_K1 + TC * D
        A_QB = -(-(A_V1 + TC * G * (P + 1)) // 8) * 8
        A_P = A_QB + G * HG * S
        kvc = at(A_KV, B * G, HD)
        bv = at(A_BV, D)
        lnt = at(A_LN, 2, D)
        ctok = at(A_LN, D, rows_=S)
        kexp = at(A_LN + D, D, rows_=TP)
        land_w = landing("land_w", A_WL, 8192)
        land_c = landing("land_c", A_C, 4 * KC * TE)
        land_q = landing("land_q", A_V0 + 2048, 2048)
        wk0 = halves(A_WH, A_WL, land_w, KC, D)
        wk0_part = [tuple(half[:, :, i * D // 2:(i + 1) * D // 2] for half in wk0) for i in range(2)]
        wv0 = halves(A_WH + 2048, A_WL + 2048, land_w, KC, D)
        wkv1 = halves(A_WH + 4096, A_WL + 4096, land_w, KC, 2 * D)
        wq0 = halves(A_V0, A_V0 + 2048, land_q, KC, D)
        ctx_raw = land_c[1][:, 0:KC * TE].rearrange("p (k t) -> p k t", k=KC)
        ctxT = at_r(A_C + KC * TE, KC, TE), at_r(A_C + 2 * KC * TE, KC, TE)
        kT = at_r(A_K, KC, TE), at_r(A_C + 3 * KC * TE, KC, TE)
        v0 = [at(A_V0 + i * TC * H * (HD + 1), TC * H, HD + 1, rows_=TP).rearrange("p (c h) e -> p c h e", c=TC)
              for i in range(2)]
        k1 = at(A_K1, TC, D, rows_=TP)
        v1 = at(A_V1, TC * G, P + 1, rows_=TP).rearrange("p (c g) e -> p c g e", c=TC)
        RT_AT = 4
        at_q = [base + 4 * (A_P + 2 * TC * HG * S)] + [x_base + 4 * (RT_AT * D + i * HG * S) for i in range(G - 1)]
        queries_h = nc.alloc_sbuf_tensor_at("queries_h", [P, G, HG, S], F32R, offset=base + 4 * A_QB)
        queries_l = [nc.alloc_sbuf_tensor_at(f"queries_l{g}", [P, HG, S], F32R, offset=at_q[g]) for g in range(G)]
        probs = [at(A_P + i * TC * HG * S, TC, HG * S, rows_=TP) for i in range(2)]
        wo0 = halves(A_WH + 4096, A_Q, landing("land_o", A_Q, 2048), KC, D)
        rows = at(A_WH + 6144, 4 * D)
        dtile = [at(A_C + 3072 + i * D, D) for i in range(5)]
        A_GU = [A_WL + m * 1024 if m < 8 else A_C + (m - 8) * 1024 for m in range(MC)]
        gu0 = [halves(A_WH + m % SPARE * 1024, A_GU[m], land_w if m < 8 else land_c, 2 * KC, P) for m in range(MC)]
        A_WD = A_V0
        wd0 = at(A_WD, MC, D)
        A_H0 = [A_Q + m * TOK if m < 4 else A_C + 3072 + (m - 4) * TOK if m < 7 else A_K if m == 7
                else A_WD + MC * D + (m - 8) * TOK for m in range(MC)]
        h0 = [at(A_H0[m], TOK) for m in range(MC)]
        silu0 = [at(A_WH + 4096 + i * TOK, 2, HALF) for i in range(2)]
        ytmp = at(A_WH + 4096, D)
        wq1 = halves(A_WH, A_WL, land_w, KC, D)
        wg1 = halves(A_WH + 2048, A_WL + 2048, land_w, KC, D)
        wo1 = halves(A_WL + 6144, A_WL + 4096, land_w, KC, D)
        qexp = at(A_WH + 4096, HALF)
        qrelu = at(A_WH + 4096 + HALF, HALF)
        zrec = [at(A_WH + 4096 + 2 * HALF, G, S), at(A_WH + 4096 + 3 * HALF + D, G, S)]
        zero = at(A_WH + 4096 + 3 * HALF, D)
        gT = at(28160, KC, TOK)
        kvbd = at(31744, B * G, P)
        ksbd = at(35840, B * G, P)
        A_SH = 40192
        land_s = landing("land_s", A_SH, 2 * KC * SHARED)
        sh13 = [halves(23808 + m % SPARE * 1024, A_SH + 2 * KC * SH_AT[m], land_s, 2 * KC, SH_CHUNKS[m])
                for m in range(6)]
        sh2 = at(37120, 6, D)
        hsh = [at(31744 + m * TOK, TOK) for m in range(6)]
        silu1 = [at(45824 + i * TOK, 2, HALF) for i in range(2)]
        A_E = A_KV
        h3 = at(28160, NT, D)
        xg = at(8904, D)
        hmoe = at(9416, 3 * P)
        hmoeT = at(9800, 3, P)
        smoe = at(10184, EI)
        xgT = at(47616, KC, P)
        A_XR = A_SH
        A_YR = A_SH + 2 * D
        back = [[at(31744 + (2 * t + j) * D, D) for j in range(2)] for t in range(NT)]
        RT = NT * NE

        def scratch(off, n):
            return arena[:, A_Q + off:A_Q + off + n]

        def rt(i):
            return scratch(i * RT, RT).rearrange("p (t e) -> p t e", t=NT)

        prob, one0, one1, both, place_, tmp16 = (rt(i) for i in range(6))
        iota16 = scratch(672, NE)
        thr = scratch(688, NT)
        cnt = scratch(695, NE)
        rmax = scratch(711, NT)
        rsum = scratch(718, NT)
        top8 = scratch(728, 56).rearrange("p (t e) -> p t e", t=NT)
        idxf = scratch(784, 14).rearrange("p (t e) -> p t e", t=NT)
        fdest = scratch(800, NT)
        scan = [scratch(808 + 32 * i, 32) for i in range(2)]
        ntile = scratch(872, NE)
        nstart = scratch(888, NE)
        iota29 = scratch(904, 32)
        cmp = scratch(936, 512)
        lower = scratch(1448, P)
        ones = scratch(1576, P)
        texpf = scratch(1704, 32)

        xs_dram = nc.dram_tensor("sorted_rows", (ROWS_MAX * P, D), F32, kind="Internal").ap()

        bv_ld = sem("bv_ld")
        rows_ld = sem("rows_ld")
        w_high = sem("w_high")
        w_low = sem("w_low")
        wq0_high = sem("wq0_high")
        wq0_low = sem("wq0_low")
        c_high = sem("c_high")
        c_low = sem("c_low")
        gu_high = sem("gu_high")
        gu_low = sem("gu_low")
        ln_H = sem("ln_H")
        ct_high = sem("ct_high")
        beta_set = sem("beta_set")
        kvbd_set = sem("kvbd_set")
        at_high = sem("at_high")
        at_low = sem("at_low")
        xs_rdy = sem("xs_rdy")
        x_again = sem("x_again")
        x_ld = sem("x_ld")
        small_ld = sem("small_ld")
        wq0_ld = sem("wq0_ld")
        wk0a_ld = sem("wk0a_ld")
        wk0b_ld = sem("wk0b_ld")
        wv0_ld = sem("wv0_ld")
        wkv1_ld = sem("wkv1_ld")
        wo0_ld = sem("wo0_ld")
        wd0_ld = sem("wd0_ld")
        wq1_ld = sem("wq1_ld")
        wg1_ld = sem("wg1_ld")
        wo1_ld = sem("wo1_ld")
        sh_ld = sem("sh_ld")
        gate_ld = sem("gate_ld")
        consts_set = sem("consts_set")
        eps_set = sem("eps_set")
        tanh_set = sem("tanh_set")
        rows_set = sem("rows_set")
        mask_set = sem("mask_set")
        ones_set = sem("ones_set")
        kT_mm = sem("kT_mm")
        v0_mm = sem("v0_mm")
        k1_mm = sem("k1_mm")
        v1_mm = sem("v1_mm")
        kv_mm = sem("kv_mm")
        sc_mm = sem("sc_mm")
        pv_mm = sem("pv_mm")
        ct_mm = sem("ct_mm")
        q0_mm = sem("q0_mm")
        kT_high = sem("kT_high")
        kT_sv = sem("kT_sv")
        v0_sv = sem("v0_sv")
        k1_exp = sem("k1_exp")
        k1_relu = sem("k1_relu")
        k1_sv = sem("k1_sv")
        v1_sv = sem("v1_sv")
        kv_sv = sem("kv_sv")
        clipped = sem("clipped")
        exped = sem("exped")
        norm_step = sem("norm_step")
        normed = sem("normed")
        ct_sv = sem("ct_sv")
        q0_sv = sem("q0_sv")
        qbd_zero = sem("qbd_zero")
        q_high = sem("q_high")
        q_spread = sem("q_spread")
        ln_var = sem("ln_var")
        ln_std = sem("ln_std")
        ln_out = sem("ln_out")
        ln_tr = sem("ln_tr")
        ln_T = sem("ln_T")
        d_var = sem("d_var")
        d_std = sem("d_std")
        y_mm = sem("y_mm")
        y_sv = sem("y_sv")
        ff_mm = sem("ff_mm")
        ff_silu = sem("ff_silu")
        ff_h = sem("ff_h")
        q1_mm = sem("q1_mm")
        q1_exp = sem("q1_exp")
        q1_relu = sem("q1_relu")
        q1_sv = sem("q1_sv")
        at_mm = sem("at_mm")
        at_z = sem("at_z")
        at_sv = sem("at_sv")
        g1_mm = sem("g1_mm")
        g1_sv = sem("g1_sv")
        gated = sem("gated")
        ksbd_set = sem("ksbd_set")
        zero_set = sem("zero_set")
        filled = sem("filled")
        lg_mm = sem("lg_mm")
        lg_max = sem("lg_max")
        lg_exp = sem("lg_exp")
        lg_sv = sem("lg_sv")
        both_set = sem("both_set")
        rank_mm = sem("rank_mm")
        dest_set = sem("dest_set")
        tables_set = sem("tables_set")
        tri_set = sem("tri_set")
        scattered = sem("scattered")
        w_landed = sem("w_landed")
        xg_ld = sem("xg_ld")
        xg_tr = sem("xg_tr")
        xg_sv = sem("xg_sv")
        gu_mm = sem("gu_mm")
        m_silu = sem("m_silu")
        m_h = sem("m_h")
        hx_tr = sem("hx_tr")
        hx_sv = sem("hx_sv")
        d_mm = sem("d_mm")
        d_sv = sem("d_sv")
        y_st = sem("y_st")
        out_st = sem("out_st")
        dve_step = sem("dve_step")
        pool_step = sem("pool_step")
        act_held = sem("act_held")
        pool_held = sem("pool_held")
        ctx_ld = sem("ctx_ld")
        gu0_ld = [sem(f"gu0_ld{m}") for m in range(MC)]
        sh13_ld = [sem(f"sh13_ld{m}") for m in range(6)]
        e_ld = [sem(f"e_ld{i}") for i in range(NSLOT)]

        back_ld = [sem(f"back_ld{t}") for t in range(NT)]

        block = stack.enter_context(nc.Block())

        def counts(engine):
            return [engine.value_load(tile_count[0:1, i:i + 1], min_val=NE - 3 + i, max_val=ROWS_MAX - 3 + i)
                    for i in range(4)]

        WEIGHTS = ("wk0a", "wk0b", "wv0", "wkv1", "gate", "wo0", "wq1", "wg1", "wo1")

        def nth(name):
            return WEIGHTS.index(name) + 1

        def ln_bank(n):
            if NT <= n < 2 * NT:
                return (1, 0, 1, 0, 1, 3, 1)[n - NT]
            return (6 if n < NT else 2) + n % NT % 2

        def y_bank(n):
            return (3 if n < NT else 0) + n % 2

        @block.sync
        def _(sp):
            sp.dma_start(wk0_part[0][2], wk0_in[:, :, 0:D // 2]).then_inc(wk0a_ld, 16)
            sp.dma_start(ctx_raw, ctx_in[0]).then_inc(ctx_ld, 16)
            sp.dma_start(wk0_part[1][2], wk0_in[:, :, D // 2:D]).then_inc(wk0b_ld, 16)
            sp.dma_start(cols[:], cols_in).then_inc(small_ld, 16)
            sp.dma_start(scal[:], scal_in.partition_broadcast(P)).then_inc(small_ld, 16)
            sp.dma_start(mask_i[:], mask_in).then_inc(small_ld, 16)
            sp.dma_start(x[:], x_in.rearrange("(t p) d -> p t d", p=P)).then_inc(x_ld, 16)
            sp.dma_start(wq0[2], wq0_in).then_inc(wq0_ld, 16)
            sp.dma_start(bv, rows_in[0:D].partition_broadcast(P)).then_inc(bv_ld, 16)
            sp.dma_start(wv0[2], wv0_in).then_inc(wv0_ld, 16)
            sp.dma_start(wkv1[2], wkv1_in).then_inc(wkv1_ld, 16)
            sp.dma_start(gate_w[:], gate_in.rearrange("p k e -> p (k e)")).then_inc(gate_ld, 16)
            sp.wait_ge(c_low, 1)
            sp.dma_start(ctx_raw, ctx_in[1]).then_inc(ctx_ld, 16)
            with sp.Fori(2, B) as b:
                sp.wait_ge(c_low, b)
                sp.dma_start(ctx_raw, ctx_in[bass.ds(b, 1)].rearrange("o p k t -> (o p) k t")).then_inc(ctx_ld, 16)
            sp.wait_ge(q_spread, 4 * B)
            sp.dma_start(wo0[2], wo0_in).then_inc(wo0_ld, 16)
            sp.wait_ge(kT_mm, 4 * B)
            sp.dma_start(rows, rows_in[D:5 * D].partition_broadcast(P)).then_inc(rows_ld, 16)
            for m in range(MC):
                sp.dma_start(gu0[m][2], gu0_in[m]).then_inc(gu0_ld[m], 16)
            sp.wait_ge(sc_mm, 4 * B)
            sp.dma_start(x[:, RT_AT:NT, :], x_in.rearrange("(t p) d -> p t d", p=P)[:, RT_AT:NT, :]).then_inc(x_again, 16)
            sp.wait_ge(pv_mm, 4 * B)
            sp.wait_ge(kv_mm, 2 * B)
            sp.dma_start(wd0, wd0_in).then_inc(wd0_ld, 16)
            sp.wait_ge(ff_mm, MC)
            sp.dma_start(wq1[2], wq1_in).then_inc(wq1_ld, 16)
            sp.dma_start(wg1[2], wg1_in).then_inc(wg1_ld, 16)
            sp.dma_start(wo1[2], wo1_in).then_inc(wo1_ld, 16)
            sp.wait_ge(y_mm, 2 * NT)
            for m, size in enumerate(SH_CHUNKS):
                sp.dma_start(sh13[m][2], sh13_in[:, 2 * KC * SH_AT[m]:2 * KC * (SH_AT[m] + size)].rearrange(
                    "p (k c) -> p k c", c=size)).then_inc(sh13_ld[m], 16)
            sp.wait_ge(at_mm, B)
            sp.dma_start(sh2[:, 0:4, :], sh2_in[0:4 * P, :].rearrange("(c p) d -> p c d", p=P)).then_inc(sh_ld, 16)
            sp.dma_start(sh2[0:96, 4:6, :], sh2_in[4 * P:SHARED, :].rearrange("(c p) d -> p c d", p=96)
                         ).then_inc(sh_ld, 16)
            sp.wait_ge(y_mm, 3 * NT)

            def load_expert(e):
                slot = e % NSLOT
                w = A_E + slot * 4352
                sp.dma_start(arena[:, w:w + 2816], e13_in[e]).then_inc(e_ld[slot], 16)
                sp.dma_start(at(w + 2816, 2, D), e2_in[e, 0:2 * P, :].rearrange("(c p) d -> p c d", p=P)).then_inc(e_ld[slot], 16)
                sp.dma_start(at(w + 2816 + 2 * D, D, rows_=EI - 2 * P), e2_in[e, 2 * P:EI, :]).then_inc(e_ld[slot], 16)

            for e in range(NSLOT):
                if e == NSLOT - 1:
                    sp.wait_ge(ff_mm, MC + 6)
                load_expert(e)
            def post(e):
                sp.wait_ge(e_ld[e % NSLOT], 48 * (e // NSLOT + 1))
                sp.sem_inc(w_landed, 1)

            post(0)
            post(1)
            sp.wait_ge(tables_set, 1)
            for e in range(2, NE):
                if e - 2 + NSLOT < NE:
                    last = sp.value_load(expert_end[0:1, e - 2:e - 1], min_val=1, max_val=ROWS_MAX)
                    post(e)
                    sp.wait_ge(d_mm, last)
                    load_expert(e - 2 + NSLOT)
                else:
                    post(e)
            out_t = out.rearrange("(t p) d -> t p d", p=P)
            for t in range(NT):
                sp.wait_ge(out_st, 1 + t)
                sp.dma_start(out_t[t], x[:, t, :]).then_inc(x_ld, 16)
            sp.wait_ge(x_ld, 16 * (NT + 1))

        @block.tensor
        def _(pe):
            mm = nc.tensor.matmul

            def piece(pair, k, first, width):
                return tuple(half[:, k, first:first + width] for half in pair[:2])

            def product(into, operands):
                for i, (a, w) in enumerate(operands):
                    mm(into, a[0], w[0], start=i == 0, stop=False)
                    mm(into, a[0], w[1], start=False, stop=False)
                    last = mm(into, a[1], w[0], start=False, stop=i == len(operands) - 1)
                return last

            def first_batch(b):
                return isinstance(b, int) and b == 0

            def keys_T(b, g):
                if g >= 2:
                    pe.wait_ge(kT_sv, b * 4 + (g - 1))
                elif not first_batch(b):
                    if g == 0:
                        pe.wait_ge(v0_sv, b * 3 + 3)
                    else:
                        pe.wait_ge(k1_relu, b * 3 + 3)
                product(ps[:, 3 + g % 2, 0:TE], [(piece(wk0, k, g * P, P), piece(ctxT, k, 0, TE))
                                                 for k in range(KC)]).then_inc(kT_mm, 1)

            def values(b, c, transposed):
                if c == 0:
                    pe.wait_ge(c_low, b + 1)
                for j, (w, first, bank, done) in enumerate([(wv0, 0, 3, v0_mm), (wkv1, 0, 4, k1_mm),
                                                            (wkv1, D, 5, v1_mm)]):
                    if j < 2 and c == 0 and first_batch(b):
                        pe.wait_ge(kT_sv, 3 + j)
                    elif j < 2 and c == 0:
                        pe.wait_ge(kv_sv, b * 2 - 1 + j)
                    elif j == 0:
                        pe.wait_ge(v0_sv, b * 3 + c)
                    elif j == 1:
                        pe.wait_ge(k1_relu, b * 3 + c)
                    else:
                        if not (first_batch(b) and c == 0):
                            pe.wait_ge(v1_sv, b * 3 + c)
                        if c == 1 and transposed:
                            pe.wait_ge(ct_sv, b - 1)
                    product(ps[0:TP, bank, :], [(piece(ctxT, k, c * TP, TP), piece(w, k, first, D))
                                                for k in range(KC)]).then_inc(done, 1)

            def kv_summary(b):
                pe.wait_ge(k1_sv, b * 3 + 3)
                pe.wait_ge(v1_sv, b * 3 + 3)
                if first_batch(b):
                    pe.wait_ge(ones_set, 3)
                    pe.wait_ge(v0_sv, 3)
                for g in range(G):
                    if g % 2 == 0 and not first_batch(b):
                        pe.wait_ge(kT_sv, b * 4 + 3 + g // 2)
                    for c in range(TC):
                        last = mm(ps[:, 3 + g // 2, (g % 2) * 129:(g % 2) * 129 + 129],
                                  k1[:, c, g * P:(g + 1) * P], v1[:, c, g, :], start=c == 0, stop=c == TC - 1)
                    if g % 2:
                        last.then_inc(kv_mm, 1)

            def head_transposes(b, values_done):
                pe.wait_ge(normed, b * 2 + 2)
                pe.wait_ge(v1_sv, values_done)
                for k in range(KC):
                    last = nc.tensor.transpose(ps[:, 5, k * S:(k + 1) * S], ctok[:, k * P:(k + 1) * P], ident[0:S, 0:S])
                last.then_inc(ct_mm, 1)

            def scores(b, g):
                if g == 0:
                    pe.wait_ge(q_spread, b * 4 + 4)
                    pe.wait_ge(kT_sv, b * 4 + 4)
                if g > 0 or not first_batch(b):
                    pe.wait_ge(clipped, b * 4 + g)
                for c in range(TC):
                    last = product(ps[0:TP, c, 0:HG * S], [(piece(kT, g, c * TP, TP),
                                                            (queries_h[:, g, :, :], queries_l[g][:]))])
                last.then_inc(sc_mm, 1)

            def mix(b, slot, g):
                pe.wait_ge(exped, b * 4 + g + 1)
                if g == 0:
                    pe.wait_ge(v0_sv, b * 3 + 3)
                if g % 2 == 0 and not first_batch(b):
                    pe.wait_ge(normed, b * 2 - 1 + g // 2)
                for h in range(HG):
                    o = (g % 2) * 4 + h
                    for c in range(TC):
                        last = mm(ps[0:S, 6 + g // 2, o * 33:o * 33 + 33], probs[g % 2][:, c, h * S:(h + 1) * S],
                                  v0[slot][:, c, 4 * g + h, :], start=c == 0, stop=c == TC - 1)
                last.then_inc(pv_mm, 1)

            def batch(b, slot, summary=True):
                for g in range(G):
                    scores(b, g)
                    if g == 1 and not first_batch(b):
                        head_transposes(b - 1, b * 3 + 4)
                    if g < 3:
                        values(b + 1, g, not first_batch(b))
                    else:
                        for gg in range(G):
                            keys_T(b + 1, gg)
                    mix(b, slot, g)
                if summary:
                    kv_summary(b + 1)

            def ln_transposes(n):
                t = n % NT
                bank = ln_bank(n)
                if n == 0:
                    pe.wait_ge(consts_set, 1)
                pe.wait_ge(ln_out, n + 1)
                if t >= 2:
                    pe.wait_ge(ln_T, n - 1)
                elif n >= NT:
                    pe.wait_ge(ln_T, n // NT * NT)
                src = h3[:, t, :] if n >= 3 * NT else lnt[:, n % 2, :]
                for k in range(KC):
                    last = nc.tensor.transpose(ps[:, bank, k * P:(k + 1) * P], src[:, k * P:(k + 1) * P], ident[:])
                last.then_inc(ln_tr, 1)

            def last_transposes(stage):
                for t in range(NT - 2, NT):
                    ln_transposes(stage * NT + t)

            pe.wait_ge(c_low, 1)
            pe.wait_ge(w_low, nth("wk0a"))
            keys_T(0, 0)
            keys_T(0, 1)
            ln_transposes(0)
            ln_transposes(1)
            pe.wait_ge(w_low, nth("wk0b"))
            keys_T(0, 2)
            ln_transposes(2)
            keys_T(0, 3)
            ln_transposes(3)
            ln_transposes(4)
            pe.wait_ge(ln_T, 4)
            pe.wait_ge(wq0_low, 2)
            for i in range(8):
                n, m = i // 4, i % 4
                if i == 2:
                    last_transposes(0)
                if i == 4:
                    pe.wait_ge(ln_T, NT)
                if i >= 2:
                    pe.wait_ge(q0_sv, i - 1)
                product(ps[:, i % 2, 0:HALF], [(piece(wq0, k, m * P, P), piece(hT, k, n * HALF, HALF))
                                               for k in range(KC)]).then_inc(q0_mm, 1)

            pe.wait_ge(w_low, nth("wkv1"))
            for c in range(TC):
                values(0, c, False)
            kv_summary(0)
            pe.wait_ge(q0_sv, 8)
            batch(0, 0)
            with pe.Fori(1, B - 4, 2) as b:
                batch(b, 1)
                batch(b + 1, 0)
            batch(B - 3, 1)
            batch(B - 2, 0, summary=False)

            def tok(pair, k, t):
                return piece(pair, k, t * P, P)

            def to_tokens(n, product_of):
                if n % NT >= 2:
                    pe.wait_ge(y_sv, n - 1)
                product_of(n % NT, ps[:, y_bank(n), :]).then_inc(y_mm, 1)

            def tokens_then_ln(stage, product_of):
                for t in range(NT):
                    n = stage * NT + t
                    if t < 2:
                        pe.wait_ge(y_sv, n - 1)
                    to_tokens(n, product_of)
                    if t >= 2:
                        ln_transposes((stage + 1) * NT + t - 2)

            def output_of_0(t, into):
                pe.wait_ge(ct_sv, (t * P + P - 1) // S + 1)
                return product(into, [(tok(hT, k, t), piece(wo0, k, 0, D)) for k in range(KC)])

            for g in range(G):
                scores(B - 1, g)
                if g == 0:
                    kv_summary(B - 1)
                if g == 1:
                    head_transposes(B - 2, 3 * B)
                    pe.wait_ge(w_low, nth("wo0"))
                    pe.wait_ge(kv_sv, 2 * B)
                if g >= 1:
                    to_tokens(g - 1, output_of_0)
                mix(B - 1, 1, g)
            to_tokens(3, output_of_0)
            head_transposes(B - 1, 3 * B)
            pe.wait_ge(clipped, 4 * B)
            for t in range(4, NT):
                to_tokens(t, output_of_0)
            for t in range(4):
                ln_transposes(NT + t)

            def gate_up(m, pair, size, n, j):
                return product(ps[0:size, 4 * (1 - m % 2) + 2 * j + n, 0:HALF],
                               [(piece(pair, j * KC + k, 0, size), piece(hT, k, n * HALF, HALF)) for k in range(KC)])

            pe.wait_ge(normed, 2 * B)
            pe.wait_ge(y_sv, NT - 1)
            pe.wait_ge(ln_T, NT + 4)
            pe.wait_ge(gu_low, 1)
            gate_up(0, gu0[0], P, 0, 0)
            gate_up(0, gu0[0], P, 0, 1)
            ln_transposes(NT + 4)
            pe.wait_ge(gu_low, 2)
            gate_up(1, gu0[1], P, 0, 1)
            pe.wait_ge(y_sv, NT)
            ln_transposes(NT + 5)
            ln_transposes(NT + 6)
            gate_up(1, gu0[1], P, 0, 0)
            pe.wait_ge(ln_T, 2 * NT)
            gate_up(0, gu0[0], P, 1, 0)
            gate_up(0, gu0[0], P, 1, 1).then_inc(ff_mm, 1)
            gate_up(1, gu0[1], P, 1, 0)
            gate_up(1, gu0[1], P, 1, 1).then_inc(ff_mm, 1)
            for m in range(2, MC):
                pe.wait_ge(gu_low, m + 1)
                pe.wait_ge(ff_h, m - 1)
                for n, j in ((0, 0), (0, 1), (1, 0)):
                    gate_up(m, gu0[m], P, n, j)
                gate_up(m, gu0[m], P, 1, 1).then_inc(ff_mm, 1)
            pe.wait_ge(ff_h, MC - 1)
            pe.wait_ge(wd0_ld, 16)

            def down_of_0(t, into):
                for m in range(MC):
                    if t == 0 and m == MC - 1:
                        pe.wait_ge(ff_h, MC)
                    last = mm(into, h0[m][:, t * P:(t + 1) * P], wd0[:, m, :], start=m == 0, stop=m == MC - 1)
                return last

            tokens_then_ln(1, down_of_0)

            def query(i):
                n, m = i // 4, i % 4
                if i >= 4:
                    pe.wait_ge(q1_relu, i - 3)
                product(ps[:, 4 + i % 4, 0:HALF], [(piece(wq1, k, m * P, P), piece(hT, k, n * HALF, HALF))
                                                   for k in range(KC)]).then_inc(q1_mm, 1)

            def attend(b):
                pe.wait_ge(q1_sv, 4 if b < 4 else 8)
                if b >= 2:
                    pe.wait_ge(at_sv, b - 1)
                for j, w in enumerate((kvbd, ksbd)):
                    for g in range(G):
                        last = mm(ps[:, 2 * j + b % 2, g * S:(g + 1) * S], w[:, b * G + g, :],
                                  qT[:, g, b * S:(b + 1) * S], start=True, stop=True)
                last.then_inc(at_mm, 1)

            def gate(i):
                n, m = i // 4, i % 4
                if i < 4:
                    pe.wait_ge(q1_relu, 5 + i)
                else:
                    pe.wait_ge(g1_sv, i - 3)
                product(ps[:, 4 + i % 4, 0:HALF], [(piece(wg1, k, m * P, P), piece(hT, k, n * HALF, HALF))
                                                   for k in range(KC)]).then_inc(g1_mm, 1)

            pe.wait_ge(ln_T, 2 * NT + 4)
            pe.wait_ge(w_low, nth("wq1"))
            query(0)
            query(1)
            last_transposes(2)
            query(2)
            query(3)
            pe.wait_ge(ln_T, 3 * NT)
            query(4)
            query(5)
            pe.wait_ge(kvbd_set, 5)
            pe.wait_ge(ksbd_set, 5)
            pe.wait_ge(kv_sv, 2 * B)
            pe.wait_ge(y_sv, 2 * NT)
            for b in range(2):
                attend(b)
                query(6 + b)
            pe.wait_ge(w_low, nth("wg1"))
            for b in range(2, B):
                attend(b)
                gate(b - 2)
            for i in range(B - 2, 8):
                gate(i)

            def output_of_1(t, into):
                pe.wait_ge(at_low, 4 if (t + 1) * P <= HALF else 8)
                return product(into, [(tok(hT, k, t), piece(wo1, k, 0, D)) for k in range(KC)])

            pe.wait_ge(w_low, nth("wo1"))
            pe.wait_ge(at_sv, B)
            tokens_then_ln(2, output_of_1)

            pe.wait_ge(ln_T, 3 * NT + 4)
            pe.wait_ge(g1_sv, 8)
            pe.wait_ge(gu_low, MC + 1)
            gate_up(0, sh13[0], P, 0, 0)
            gate_up(0, sh13[0], P, 0, 1)
            last_transposes(3)
            pe.wait_ge(y_sv, 3 * NT)
            pe.wait_ge(gu_low, MC + 2)
            gate_up(1, sh13[1], P, 0, 0)
            pe.wait_ge(ln_T, 4 * NT)
            for t in range(NT):
                last = product(ps[:, 1, t * NE:(t + 1) * NE],
                               [(tok(hT, k, t), (gate_r[:, 0, k * NE:(k + 1) * NE], gate_r[:, 1, k * NE:(k + 1) * NE]))
                                for k in range(KC)])
            last.then_inc(lg_mm, 1)
            gate_up(0, sh13[0], P, 1, 0)
            gate_up(0, sh13[0], P, 1, 1).then_inc(ff_mm, 1)
            gate_up(1, sh13[1], P, 0, 1)
            pe.wait_ge(lg_sv, 1)
            gate_up(1, sh13[1], P, 1, 0)
            gate_up(1, sh13[1], P, 1, 1).then_inc(ff_mm, 1)
            for m in range(2, 6):
                size = SH_CHUNKS[m]
                pe.wait_ge(gu_low, MC + m + 1)
                pe.wait_ge(ff_h, MC + m - 1)
                for n, j in ((0, 0), (0, 1), (1, 0)):
                    gate_up(m, sh13[m], size, n, j)
                gate_up(m, sh13[m], size, 1, 1).then_inc(ff_mm, 1)
            pe.wait_ge(ff_h, MC + 5)
            pe.wait_ge(both_set, 1)
            pe.wait_ge(tri_set, 4)
            mm(ps[:, 6, 0:RT], lower, both.rearrange("p t e -> p (t e)"), start=True, stop=True)
            mm(ps[:, 7, 0:RT], ones, both.rearrange("p t e -> p (t e)"), start=True, stop=True
               ).then_inc(rank_mm, 1)
            pe.wait_ge(ff_h, MC + 6)
            pe.wait_ge(sh_ld, 32)
            for t in range(NT):
                pe.wait_ge(y_sv, 3 * NT + t - 1)
                for m, z in enumerate(SH_CHUNKS):
                    last = mm(ps[:, (3 * NT + t) % 2, :], hsh[m][0:z, t * P:(t + 1) * P], sh2[0:z, m, :],
                              start=m == 0, stop=m == 5)
                last.then_inc(y_mm, 1)

            pe.wait_ge(tables_set, 1)
            last3, last2, last1, tiles = counts(pe)

            def slot_of(n):
                e = pe.value_load(tile_expert[0:1, bass.ds(n, 1)], min_val=0, max_val=NE - 1)
                return e, A_E + (e % NSLOT) * 4352

            def rows_T(n):
                pe.wait_ge(xs_rdy, n + 1)
                for k in range(KC):
                    last = nc.tensor.transpose(ps[:, 6, k * P:(k + 1) * P], xg[:, k * P:(k + 1) * P], ident[:])
                last.then_inc(xg_tr, 1)

            def up_expert(n):
                e, w = slot_of(n)
                pe.wait_ge(w_landed, e + 1)
                pe.wait_ge(xg_sv, n + 1)
                for j in range(2):
                    for k in range(KC):
                        last = mm(ps[:, 4 + j, 0:EI], xgT[:, k, :],
                                  arena[:, bass.ds(w + (k * 2 * EI + j * EI), EI)], start=k == 0, stop=k == KC - 1)
                last.then_inc(gu_mm, 1)

            def down_expert(n):
                e, w = slot_of(n)
                pe.wait_ge(hx_sv, n + 1)
                if not first_batch(n):
                    pe.wait_ge(d_sv, n)
                for c, z in enumerate(E_CHUNKS):
                    last = mm(ps[:, 3, :], hmoeT[0:z, c, :], arena[0:z, bass.ds(w + (2816 + c * D), D)],
                              start=c == 0, stop=c == 2)
                last.then_inc(d_mm, 1)

            def hidden_T(n):
                pe.wait_ge(m_h, n + 1)
                for c in range(3):
                    last = nc.tensor.transpose(ps[:, 7, c * P:(c + 1) * P], hmoe[:, c * P:(c + 1) * P], ident[:])
                last.then_inc(hx_tr, 1)

            rows_T(0)
            up_expert(0)
            rows_T(1)
            hidden_T(0)
            with pe.Fori(1, last1) as n:
                up_expert(n)
                rows_T(n + 1)
                down_expert(n - 1)
                hidden_T(n)
            up_expert(last1)
            down_expert(last2)
            hidden_T(last1)
            down_expert(last1)

        @block.scalar
        def _(act):
            fn = nc.scalar.activation

            def high(name, pair, landed):
                act.wait_ge(landed, 16)
                fn(pair[0], pair[2], ACT.Copy).then_inc(w_high, 1)

            def keys_T(b, g):
                act.wait_ge(kT_mm, b * 4 + g + 1)
                fn(kT[0][:, g, :], ps[:, 3 + g % 2, 0:TE], ACT.Identity, bias=cols[:, 4 + g:5 + g]
                   ).then_inc(kT_high, 1)

            def spread(b):
                for h in range(HG):
                    r = slice(h * HD, (h + 1) * HD)
                    fn(queries_h[r, :, h, :], qT[r, :, bass.ds(b * S, S)], ACT.Copy).then_inc(q_high, 1)

            def values(b, c):
                act.wait_ge(k1_mm, b * 3 + c + 1)
                if not (isinstance(b, int) and b == 0 and c == 0):
                    act.wait_ge(k1_sv, b * 3 + c)
                fn(kexp, ps[0:TP, 4, :], ACT.Exp).then_inc(k1_exp, 1)
                act.wait_ge(v1_mm, b * 3 + c + 1)
                fn(v1[:, c, :, 0:P], ps[0:TP, 5, :].rearrange("p (g e) -> p g e", g=G), ACT.Copy
                   ).then_inc(v1_sv, 1)

            def ln(n):
                act.wait_ge(ln_var, n + 1)
                fn(std[:, n:n + 1], mv[:, n, 1:2], ACT.Sqrt, bias=eps[:, 0:1]).then_inc(ln_std, 1)

            def ln_save(n):
                t = n % NT
                act.wait_ge(ln_tr, n + 1)
                fn(hT[0][:, :, t * P:(t + 1) * P], ps[:, ln_bank(n), :].rearrange("p (k t) -> p k t", k=KC),
                   ACT.Copy).then_inc(ln_H, 1)

            def context_high(b):
                act.wait_ge(ctx_ld, b * 16 + 16)
                fn(ctxT[0], ctx_raw, ACT.Copy).then_inc(c_high, 1)

            def heads_save(b):
                act.wait_ge(ct_mm, b + 1)
                act.sem_inc(act_held, 1)
                fn(hT[0][:, :, bass.ds(b * S, S)], ps[:, 5, 0:KC * S].rearrange("p (k t) -> p k t", k=KC), ACT.Copy
                   ).then_inc(ct_high, 1)

            def feed_high(i, pair, landed, freed=None):
                act.wait_ge(landed, 16)
                if freed is not None:
                    act.wait_ge(ff_mm, freed)
                fn(pair[0], pair[2], ACT.Copy).then_inc(gu_high, 1)

            high("wk0a", wk0_part[0], wk0a_ld)
            context_high(0)
            high("wk0b", wk0_part[1], wk0b_ld)
            act.wait_ge(small_ld, 48)
            fn(tg[:], scal[:, 0:4], ACT.Tanh).then_inc(tanh_set, 1)
            act.wait_ge(eps_set, 1)
            keys_T(0, 0)
            ln(0)
            ln(1)
            keys_T(0, 1)
            ln(2)
            ln_save(0)
            ln(3)
            ln_save(1)
            act.wait_ge(wq0_ld, 16)
            fn(wq0[0], wq0[2], ACT.Copy).then_inc(wq0_high, 1)
            ln(4)
            keys_T(0, 2)
            ln(5)
            ln_save(2)
            ln(6)
            keys_T(0, 3)
            for t in range(3, NT):
                ln_save(t)
            for i in range(8):
                n, m = i // 4, i % 4
                act.wait_ge(q0_mm, i + 1)
                fn(qT[:, m, n * HALF:(n + 1) * HALF], ps[:, i % 2, 0:HALF], ACT.Identity,
                   bias=cols[:, m:m + 1]).then_inc(q0_sv, 1)
                if i == 2:
                    high("wv0", wv0, wv0_ld)
                if i == 3:
                    high("wkv1", wkv1, wkv1_ld)
                if i == 5:
                    act.wait_ge(gate_ld, 16)
                    fn(gate_r[:, 0, :], gate_w[:], ACT.Copy).then_inc(w_high, 1)
            act.wait_ge(qbd_zero, 1)
            act.wait_ge(q0_sv, 8)
            spread(0)
            for c in range(TC):
                values(0, c)
            context_high(1)
            act.wait_ge(mask_set, 2)

            def batch(b, first=False, split=True):
                for g in range(G):
                    if g == 3:
                        keys_T(b + 1, 0)
                    act.wait_ge(clipped, b * 4 + g + 1)
                    act.sem_inc(act_held, 1)
                    for c in range(TC):
                        done = fn(probs[g % 2][:, c, :], probs[g % 2][:, c, :], ACT.Exp,
                                  bias=mbias[:, bass.ds(b * 3 + c, 1)], scale=mscale[:, bass.ds(b * 3 + c, 1)])
                    done.then_inc(exped, 1)
                    if g == 1 and not first:
                        heads_save(b - 1)
                    if g < 3:
                        values(b + 1, g)
                keys_T(b + 1, 1)
                act.wait_ge(q_spread, b * 4 + 4)
                act.sem_inc(act_held, 1)
                spread(b + 1)
                keys_T(b + 1, 2)
                keys_T(b + 1, 3)
                if split:
                    context_high(b + 2)

            batch(0, first=True)
            with act.Fori(1, B - 2) as b:
                batch(b)
            batch(B - 2, split=False)

            def delta_std(t):
                act.wait_ge(d_var, t + 1)
                fn(dstd[:, t:t + 1], dmv[:, t, 1:2], ACT.Sqrt, bias=eps[:, 0:1]).then_inc(d_std, 1)

            for g in range(G):
                act.wait_ge(clipped, (B - 1) * 4 + g + 1)
                for c in range(TC):
                    b = (B - 1) * 3 + c
                    done = fn(probs[g % 2][:, c, :], probs[g % 2][:, c, :], ACT.Exp,
                              bias=mbias[:, b:b + 1], scale=mscale[:, b:b + 1])
                done.then_inc(exped, 1)
                if g == 0:
                    high("wo0", wo0, wo0_ld)
                if g == 1:
                    heads_save(B - 2)
                if g >= 2:
                    feed_high(g - 2, gu0[g - 2], gu0_ld[g - 2])
                    ln(NT + g - 2)
                if g >= 1:
                    delta_std(g - 1)
                if g in (1, 2):
                    fn(warm[:, g:g + 1], eps[:], ACT.Exp)
            delta_std(3)
            heads_save(B - 1)
            ln(NT + 2)
            delta_std(4)
            ln(NT + 3)
            delta_std(5)
            for t in range(4):
                ln_save(NT + t)
            delta_std(6)
            for t in range(4, NT):
                ln(NT + t)
            for t in range(4, NT):
                ln_save(NT + t)

            for m in range(MC):
                if m + 2 < MC:
                    feed_high(m + 2, gu0[m + 2], gu0_ld[m + 2], m - 1 if m >= 2 else None)
                act.wait_ge(ff_mm, m + 1)
                if m >= 2:
                    act.wait_ge(ff_h, m - 1)
                fn(silu0[m % 2], ps[:, 4 * (1 - m % 2):4 * (1 - m % 2) + 2, 0:HALF], ACT.Silu,
                   scale=cols[:, 12 + m:13 + m]).then_inc(ff_silu, 1)

            for t in range(NT):
                ln(2 * NT + t)
                if t == 1:
                    high("wq1", wq1, wq1_ld)
                if t == 2:
                    high("wg1", wg1, wg1_ld)
                if t == 3:
                    high("wo1", wo1, wo1_ld)
                if t >= 2:
                    ln_save(2 * NT + t - 2)
            ln_save(3 * NT - 2)
            ln_save(3 * NT - 1)
            def query(i):
                act.wait_ge(q1_mm, i + 1)
                if i >= 1:
                    act.wait_ge(q1_sv, i)
                fn(qexp, ps[:, 4 + i % 4, 0:HALF], ACT.Exp).then_inc(q1_exp, 1)

            def normalisers(b):
                act.wait_ge(at_mm, b + 1)
                if b >= 2:
                    act.wait_ge(at_sv, b - 1)
                fn(zrec[b % 2], ps[:, 2 + b % 2, 0:G * S].rearrange("p (g t) -> p g t", g=G), ACT.Identity,
                   bias=z_eps[:, 0:1]).then_inc(at_z, 1)

            for i in range(6):
                query(i)
                if i < HG:
                    r = slice(i * HD, (i + 1) * HD)
                    act.wait_ge(ksbd_set, 1)
                    fn(ksbd[r, :, r], ks[r].rearrange("p b g -> p (b g)").unsqueeze(2).broadcast_to([HD, B * G, HD]),
                       ACT.Copy).then_inc(ksbd_set, 1)
            for b in range(2):
                normalisers(b)
                query(6 + b)

            def gated_high(i):
                n, m = i // 4, i % 4
                act.wait_ge(gated, i + 1)
                act.wait_ge(g1_mm, 4 * n + 4)
                fn(hT[0][:, m, n * HALF:(n + 1) * HALF], qT[:, m, n * HALF:(n + 1) * HALF], ACT.Copy
                   ).then_inc(at_high, 1)

            for i in range(8):
                n, m = i // 4, i % 4
                if i + 2 < B:
                    normalisers(i + 2)
                act.wait_ge(g1_mm, i + 1)
                fn(gT[:, m, n * HALF:(n + 1) * HALF], ps[:, 4 + i % 4, 0:HALF], ACT.Sigmoid,
                   bias=cols[:, 8 + m:9 + m]).then_inc(g1_sv, 1)
                if i >= 5:
                    gated_high(i - 5)
            for i in range(3, 8):
                gated_high(i)
            for t in range(NT):
                ln(3 * NT + t)
                if t >= 2:
                    ln_save(3 * NT + t - 2)
                if t in (3, 4):
                    feed_high(MC + t - 3, sh13[t - 3], sh13_ld[t - 3])
            ln_save(4 * NT - 2)
            ln_save(4 * NT - 1)
            act.wait_ge(lg_max, 1)
            fn(prob.rearrange("p t e -> p (t e)"), prob.rearrange("p t e -> p (t e)"), ACT.Exp).then_inc(lg_exp, 1)
            for m, size in enumerate(SH_CHUNKS):
                if m == 1:
                    act.wait_ge(filled, 16)
                if m + 2 < 6:
                    feed_high(MC + m + 2, sh13[m + 2], sh13_ld[m + 2], MC + m - 1 if m >= 2 else None)
                act.wait_ge(ff_mm, MC + m + 1)
                act.wait_ge(ff_h, MC + m - 1)
                fn(silu1[m % 2][0:size], ps[0:size, 4 * (1 - m % 2):4 * (1 - m % 2) + 2, 0:HALF], ACT.Silu
                   ).then_inc(ff_silu, 1)

            act.wait_ge(tables_set, 1)
            last3, last2, last1, tiles = counts(act)

            def rows_save(n):
                act.wait_ge(xg_tr, n + 1)
                fn(xgT, ps[:, 6, :].rearrange("p (k t) -> p k t", k=KC), ACT.Copy).then_inc(xg_sv, 1)

            def silu_tile(n):
                act.wait_ge(gu_mm, n + 1)
                fn(smoe, ps[:, 4, 0:EI], ACT.Silu).then_inc(m_silu, 1)

            rows_save(0)
            with act.Fori(0, last1) as n:
                silu_tile(n)
                rows_save(n + 1)
            silu_tile(last1)

        @block.vector
        def _(dve):
            v = nc.vector
            count = [0]

            def then(ins):
                count[0] += 1
                ins.then_inc(dve_step, 1)
                dve.wait_ge(dve_step, count[0])

            def low(name, pair):
                dve.wait_ge(w_high, nth(name))
                v.tensor_tensor(pair[1], pair[2], pair[0].bitcast(F32), ALU.subtract).then_inc(w_low, 1)

            def context_low(b):
                dve.wait_ge(c_high, b + 1)
                v.tensor_tensor(ctxT[1], ctx_raw, ctxT[0].bitcast(F32), ALU.subtract).then_inc(c_low, 1)

            def keys_low(b, g):
                dve.wait_ge(kT_high, b * 4 + g + 1)
                v.scalar_tensor_tensor(kT[1][:, g, :], ps[:, 3 + g % 2, 0:TE], cols[:, 4 + g:5 + g],
                                       kT[0][:, g, :].bitcast(F32), ALU.add, ALU.subtract).then_inc(kT_sv, 1)

            def spread(b):
                for h in range(HG):
                    r = slice(h * HD, (h + 1) * HD)
                    dve.wait_ge(q_high, b * 4 + h + 1)
                    for g in range(G):
                        last = v.tensor_tensor(queries_l[g][r, h, :], qT[r, g, bass.ds(b * S, S)],
                                               queries_h[r, g, h, :].bitcast(F32), ALU.subtract)
                    last.then_inc(q_spread, 1)

            def feed_low(i, pair):
                dve.wait_ge(gu_high, i + 1)
                v.tensor_tensor(pair[1], pair[2], pair[0].bitcast(F32), ALU.subtract).then_inc(gu_low, 1)

            def ln_stats(n):
                then(v.bn_stats(stats[:, n % 2, :], x[:, n % NT, :]))
                v.bn_aggr(mv[:, n, :], stats[:, n % 2, :]).then_inc(ln_var, 1)

            def ln_norm(n):
                dve.wait_ge(ln_std, n + 1)
                then(v.reciprocal(rstd[:, n:n + 1], std[:, n:n + 1]))
                if n >= 2:
                    dve.wait_ge(ln_tr, n - 1)
                dst = h3[:, n % NT, :] if n >= 3 * NT else lnt[:, n % 2, :]
                v.tensor_scalar(dst, x[:, n % NT, :], mv[:, n, 0:1], rstd[:, n:n + 1], ALU.subtract, ALU.mult
                                ).then_inc(ln_out, 1)

            def ln_low(n):
                t = n % NT
                dve.wait_ge(ln_H, n + 1)
                v.tensor_tensor(hT[1][:, :, t * P:(t + 1) * P],
                                ps[:, ln_bank(n), :].rearrange("p (k t) -> p k t", k=KC),
                                hT[0][:, :, t * P:(t + 1) * P].bitcast(F32), ALU.subtract).then_inc(ln_T, 1)

            v.memset(z_eps[:], Z_EPS)
            v.memset(eps[:], LN_EPS).then_inc(eps_set, 1)
            low("wk0a", wk0_part[0])
            context_low(0)
            low("wk0b", wk0_part[1])
            dve.wait_ge(small_ld, 48)
            then(v.tensor_scalar(mscale[:], mask_i[:], 0.5, None, ALU.is_gt))
            v.tensor_scalar(mbias[:], mscale[:], CLIP, -CLIP, ALU.mult, ALU.add).then_inc(mask_set, 1)
            dve.wait_ge(mask_set, 1)
            v.tensor_scalar(mscale[:], mscale[:], SCALE, None, ALU.mult).then_inc(mask_set, 1)
            keys_low(0, 0)
            dve.wait_ge(x_ld, 16)
            ln_stats(0)
            ln_stats(1)
            ln_norm(0)
            keys_low(0, 1)
            ln_stats(2)
            ln_norm(1)
            ln_low(0)
            ln_stats(3)
            ln_norm(2)
            ln_low(1)
            ln_stats(4)
            ln_norm(3)
            dve.wait_ge(wq0_high, 1)
            v.tensor_tensor(wq0[1][:, 0:2], wq0[2][:, 0:2], wq0[0][:, 0:2].bitcast(F32), ALU.subtract).then_inc(wq0_low, 1)
            keys_low(0, 2)
            ln_stats(5)
            ln_low(2)
            ln_stats(6)
            keys_low(0, 3)
            for t in range(4, NT):
                ln_norm(t)
                ln_low(t - 1)
            ln_low(NT - 1)
            then(v.tensor_scalar(rs[:], scal[:, 4:5], 0.0, 0.3, ALU.max, ALU.min))
            low("wv0", wv0)
            low("wkv1", wkv1)
            dve.wait_ge(w_high, nth("gate"))
            v.tensor_tensor(gate_r[:, 1, :], gate_w[:], gate_r[:, 0, :].bitcast(F32), ALU.subtract).then_inc(w_low, 1)
            dve.wait_ge(q0_mm, 8)
            for slot in range(2):
                v.memset(v0[slot][:, :, :, HD:HD + 1], 1.0).then_inc(ones_set, 1)
            v.memset(v1[:, :, :, P:P + 1], 1.0).then_inc(ones_set, 1)
            dve.wait_ge(bv_ld, 16)

            def values(b, slot, c):
                dve.wait_ge(v0_mm, b * 3 + c + 1)
                v.tensor_tensor(v0[slot][:, c, :, 0:HD], ps[0:TP, 3, :].rearrange("p (h d) -> p h d", h=H),
                                bv[0:TP].rearrange("p (h d) -> p h d", h=H), ALU.add).then_inc(v0_sv, 1)
                dve.wait_ge(k1_exp, b * 3 + c + 1)
                v.tensor_scalar(k1[:, c, :], ps[0:TP, 4, :], 0.0, None, ALU.max).then_inc(k1_relu, 1)
                dve.wait_ge(k1_relu, b * 3 + c + 1)
                v.scalar_tensor_tensor(k1[:, c, :], kexp, 1.0, k1[:, c, :], ALU.min, ALU.add).then_inc(k1_sv, 1)

            ks_flat = ks[:].rearrange("p b g -> p (b g)")

            def kv_save(b):
                for pair in range(2):
                    dve.wait_ge(kv_mm, b * 2 + pair + 1)
                    bank = ps[:, 3 + pair, 0:2 * 129].rearrange("p (g e) -> p g e", g=2)
                    for h in range(HG):
                        r = slice(h * HD, (h + 1) * HD)
                        v.tensor_scalar(kvc[r, bass.ds(b * G + 2 * pair, 2), :], bank[r, :, h * HD:(h + 1) * HD],
                                        1.0, None, ALU.mult)
                    v.tensor_copy(ks_flat[:, bass.ds(b * G + 2 * pair, 2)], bank[:, :, P]).then_inc(kv_sv, 1)

            dve.wait_ge(qbd_zero, 1)
            spread(0)
            for c in range(TC):
                values(0, 0, c)
            context_low(1)
            kv_save(0)

            def clip(b, g, guard):
                dve.wait_ge(sc_mm, b * 4 + g + 1)
                if guard:
                    dve.wait_ge(pv_mm, b * 4 + g - 1)
                v.tensor_scalar(probs[g % 2], ps[0:TP, 0:TC, 0:HG * S], -CLIP / SCALE, CLIP / SCALE,
                                ALU.max, ALU.min).then_inc(clipped, 1)

            def normalise(b, half, first):
                dve.wait_ge(pv_mm, b * 4 + 2 * half + 2)
                bank = ps[0:S, 6 + half, 0:8 * 33].rearrange("p (h e) -> p h e", h=8)
                v.tensor_copy(zsum[:, half, :], bank[:, :, HD]).then_inc(norm_step, 1)
                dve.wait_ge(norm_step, b * 6 + 3 * half + 1)
                v.scalar_tensor_tensor(zinv[:, half, :], zsum[:, half, :], P_EPS, zsum[:, half, :], ALU.mult, ALU.add
                                       ).then_inc(norm_step, 1)
                dve.wait_ge(norm_step, b * 6 + 3 * half + 2)
                v.reciprocal(zinv[:, half, :], zinv[:, half, :]).then_inc(norm_step, 1)
                dve.wait_ge(norm_step, b * 6 + 3 * half + 3)
                if not first:
                    dve.wait_ge(ct_mm, b)
                v.tensor_tensor(ctok[:, half * 256:(half + 1) * 256].rearrange("p (h d) -> p h d", h=8),
                                bank[:, :, 0:HD], zinv[:, half, :].unsqueeze(2).broadcast_to([S, 8, HD]),
                                ALU.mult).then_inc(normed, 1)

            def heads_low(b):
                dve.wait_ge(ct_high, b + 1)
                v.tensor_tensor(hT[1][:, :, bass.ds(b * S, S)], ps[:, 5, 0:KC * S].rearrange("p (k t) -> p k t", k=KC),
                                hT[0][:, :, bass.ds(b * S, S)].bitcast(F32), ALU.subtract).then_inc(ct_sv, 1)

            def batch(b, slot, first=False, split=True, summary=True):
                for g in range(G):
                    clip(b, g, not (first and g < 2))
                    if g == 1 and not first:
                        heads_low(b - 1)
                    if g == 2:
                        normalise(b, 0, first)
                    if g < 3:
                        values(b + 1, 1 - slot, g)
                keys_low(b + 1, 0)
                keys_low(b + 1, 1)
                spread(b + 1)
                keys_low(b + 1, 2)
                keys_low(b + 1, 3)
                if split:
                    context_low(b + 2)
                normalise(b, 1, first)
                if summary:
                    kv_save(b + 1)

            batch(0, 0, first=True)
            with dve.Fori(1, B - 4, 2) as b:
                batch(b, 1)
                batch(b + 1, 0)
            batch(B - 3, 1)
            batch(B - 2, 0, split=False, summary=False)

            bo, gamma, beta, down_s = (rows[:, i * D:(i + 1) * D] for i in range(4))

            def delta(t):
                dve.wait_ge(y_mm, t + 1)
                if t >= 5:
                    dve.wait_ge(ln_var, NT + t - 4)
                v.scalar_tensor_tensor(dtile[t % 5], ps[:, y_bank(t), :], rs[:, 0:1], bo, ALU.mult, ALU.add
                                       ).then_inc(y_sv, 1)
                dve.wait_ge(y_sv, t + 1)
                then(v.bn_stats(stats[:, 0, :], dtile[t % 5]))
                v.bn_aggr(dmv[:, t, :], stats[:, 0, :]).then_inc(d_var, 1)

            def residual(t):
                d = dtile[t % 5]
                dve.wait_ge(d_std, t + 1)
                then(v.reciprocal(drstd[:, t:t + 1], dstd[:, t:t + 1]))
                then(v.scalar_tensor_tensor(d, d, dmv[:, t, 0:1], gamma, ALU.subtract, ALU.mult))
                dve.wait_ge(beta_set, t + 1)
                then(v.scalar_tensor_tensor(x[:, t, :], d, drstd[:, t:t + 1], x[:, t, :], ALU.mult, ALU.add))
                ln_stats(NT + t)

            for g in range(G):
                clip(B - 1, g, True)
                if g == 0:
                    kv_save(B - 1)
                    dve.wait_ge(rows_ld, 16)
                    dve.wait_ge(tanh_set, 1)
                    v.tensor_scalar(beta, beta, tg[:, 0:1], None, ALU.mult).then_inc(rows_set, 1)
                    v.tensor_scalar(bo, bo, rs[:, 0:1], None, ALU.mult).then_inc(rows_set, 1)
                    v.tensor_scalar(gamma, gamma, tg[:, 0:1], None, ALU.mult).then_inc(rows_set, 1)
                    dve.wait_ge(rows_set, 3)
                    low("wo0", wo0)
                if g == 1:
                    heads_low(B - 2)
                if g == 2:
                    normalise(B - 1, 0, False)
                if g >= 2:
                    residual(g - 2)
                if g >= 1:
                    delta(g - 1)
                if g >= 2:
                    feed_low(g - 2, gu0[g - 2])
            normalise(B - 1, 1, False)
            delta(3)
            heads_low(B - 1)
            ln_norm(NT)
            residual(2)
            ln_norm(NT + 1)
            delta(4)
            residual(3)
            delta(5)
            ln_norm(NT + 2)
            ln_low(NT)
            ln_norm(NT + 3)
            ln_low(NT + 1)
            ln_low(NT + 2)
            ln_low(NT + 3)
            delta(6)
            residual(4)
            ln_norm(NT + 4)
            residual(5)
            ln_norm(NT + 5)
            residual(6)
            ln_low(NT + 4)
            ln_norm(NT + 6)
            ln_low(NT + 5)
            ln_low(NT + 6)
            v.tensor_scalar(down_s, down_s, tg[:, 2:3], None, ALU.mult).then_inc(rows_set, 1)

            def hidden(i, m, size, scale, silu, into):
                dve.wait_ge(ff_mm, i + 1)
                dve.wait_ge(ff_silu, i + 1)
                v.scalar_tensor_tensor(into[0:size].rearrange("p (n t) -> p n t", n=2),
                                       ps[0:size, 4 * (1 - m % 2) + 2:4 * (1 - m % 2) + 4, 0:HALF], scale,
                                       silu[0:size], ALU.mult, ALU.mult).then_inc(ff_h, 1)

            for m in range(MC):
                if m + 2 < MC:
                    feed_low(m + 2, gu0[m + 2])
                hidden(m, m, P, cols[:, 12 + MC + m:13 + MC + m], silu0[m % 2], h0[m])
            dve.wait_ge(rows_set, 4)
            for t in range(NT):
                dve.wait_ge(y_mm, NT + t + 1)
                v.tensor_tensor(ytmp, ps[:, y_bank(NT + t), :], down_s, ALU.mult).then_inc(y_sv, 1)
                dve.wait_ge(y_sv, NT + t + 1)
                then(v.tensor_tensor(x[:, t, :], x[:, t, :], ytmp, ALU.add))
                ln_stats(2 * NT + t)
                if t >= 1:
                    ln_norm(2 * NT + t - 1)
                if t == 1:
                    low("wq1", wq1)
                if t == 2:
                    low("wg1", wg1)
                if t == 3:
                    low("wo1", wo1)
                if t >= 2:
                    ln_low(2 * NT + t - 2)
            ln_norm(3 * NT - 1)
            ln_low(3 * NT - 2)
            ln_low(3 * NT - 1)

            def query(i):
                n, m = i // 4, i % 4
                dve.wait_ge(q1_exp, i + 1)
                v.tensor_scalar(qrelu, ps[:, 4 + i % 4, 0:HALF], 0.0, None, ALU.max).then_inc(q1_relu, 1)
                dve.wait_ge(q1_relu, i + 1)
                v.scalar_tensor_tensor(qT[:, m, n * HALF:(n + 1) * HALF], qexp, 1.0, qrelu, ALU.min, ALU.add
                                       ).then_inc(q1_sv, 1)
                dve.wait_ge(q1_sv, i + 1)

            def attend(b):
                dve.wait_ge(at_z, b + 1)
                then(v.reciprocal(zrec[b % 2], zrec[b % 2]))
                v.tensor_tensor(qT[:, :, b * S:(b + 1) * S], ps[:, b % 2, 0:G * S].rearrange("p (g t) -> p g t", g=G),
                                zrec[b % 2], ALU.mult).then_inc(at_sv, 1)

            def gated_low(i):
                n, m = i // 4, i % 4
                dve.wait_ge(at_high, i + 1)
                v.tensor_tensor(hT[1][:, m, n * HALF:(n + 1) * HALF], qT[:, m, n * HALF:(n + 1) * HALF],
                                hT[0][:, m, n * HALF:(n + 1) * HALF].bitcast(F32), ALU.subtract).then_inc(at_low, 1)

            for i in range(6):
                query(i)
                if i < HG:
                    r = slice(i * HD, (i + 1) * HD)
                    dve.wait_ge(kvbd_set, 1)
                    v.tensor_copy(kvbd[r, :, r], kvc[r, :, :]).then_inc(kvbd_set, 1)
            for b in range(2):
                attend(b)
                query(6 + b)
            for b in range(2, B):
                attend(b)
            for i in range(8):
                gated_low(i)
            for t in range(NT):
                dve.wait_ge(y_mm, 2 * NT + t + 1)
                v.scalar_tensor_tensor(x[:, t, :], ps[:, (2 * NT + t) % 2, :], tg[:, 1:2], x[:, t, :], ALU.mult, ALU.add
                                       ).then_inc(y_sv, 1)
                dve.wait_ge(y_sv, 2 * NT + t + 1)
                ln_stats(3 * NT + t)
                if t >= 1:
                    ln_norm(3 * NT + t - 1)
                if t >= 2:
                    ln_low(3 * NT + t - 2)
                if t in (3, 4):
                    feed_low(MC + t - 3, sh13[t - 3])
            ln_norm(4 * NT - 1)
            ln_low(4 * NT - 2)
            ln_low(4 * NT - 1)

            dve.wait_ge(lg_mm, 1)
            dve.wait_ge(tri_set, 4)
            lg = ps[:, 1, 0:RT].rearrange("p (t e) -> p t e", t=NT)
            then(v.tensor_reduce(rmax, lg, AX.X, ALU.max))
            v.tensor_tensor(prob, lg, rmax.unsqueeze(2).broadcast_to([P, NT, NE]), ALU.subtract).then_inc(lg_max, 1)
            dve.wait_ge(lg_exp, 1)
            v.memset(hmoe[:, EI:3 * P], 0.0).then_inc(lg_sv, 1)
            feed_low(MC + 2, sh13[2])
            then(v.tensor_reduce(rsum, prob, AX.X, ALU.add))
            then(v.reciprocal(rsum, rsum))
            then(v.tensor_tensor(prob, prob, rsum.unsqueeze(2).broadcast_to([P, NT, NE]), ALU.mult))
            for t in range(NT):
                then(v.max(top8[:, t, :], prob[:, t, :]))
                then(v.max_index(idx8[:, t, :], top8[:, t, :], prob[:, t, :]))
            then(v.tensor_copy(idxf, idx8[:, :, 0:2]))
            then(v.tensor_scalar(wtop[:], top8[:, :, 0:2], tg[:, 3:4], None, ALU.mult))
            ids = iota16.unsqueeze(1).broadcast_to([P, NT, NE])
            then(v.tensor_tensor(one0, ids, idxf[:, :, 0:1].broadcast_to([P, NT, NE]), ALU.is_equal))
            then(v.tensor_tensor(one1, ids, idxf[:, :, 1:2].broadcast_to([P, NT, NE]), ALU.is_equal))
            then(v.tensor_tensor(both, one0, one1, ALU.add))
            v.memset(scan[0][:, 0:16], 0.0).then_inc(both_set, 1)
            v.memset(scan[1][:, 0:16], 0.0)
            for m, size in enumerate(SH_CHUNKS):
                if 3 <= m + 2 < 6:
                    feed_low(MC + m + 2, sh13[m + 2])
                hidden(MC + m, m, size, 1.0, silu1[m % 2], hsh[m])

            dve.wait_ge(rank_mm, 1)
            rank = ps[:, 6, 0:RT].rearrange("p (t e) -> p t e", t=NT)
            total = ps[:, 7, 0:RT].rearrange("p (t e) -> p t e", t=NT)
            then(v.memset(cnt, 0.0))
            for t in range(NT):
                then(v.tensor_tensor(place_[:, t, :], rank[:, t, :], cnt, ALU.add))
                then(v.tensor_tensor(cnt, cnt, total[:, t, :], ALU.add))
            c3 = cmp[:, 0:NE * NT].rearrange("p (e k) -> p e k", e=NE)
            then(v.tensor_tensor(c3, cnt.unsqueeze(2).broadcast_to([P, NE, NT]),
                                 thr.unsqueeze(1).broadcast_to([P, NE, NT]), ALU.is_gt))
            then(v.tensor_reduce(ntile, c3, AX.X, ALU.add))
            then(v.tensor_scalar(scan[0][:, 16:32], ntile, 1.0, None, ALU.max))
            then(v.tensor_copy(ntile, scan[0][:, 16:32]))
            for i in range(4):
                a, b_ = scan[i % 2], scan[1 - i % 2]
                then(v.tensor_tensor(b_[:, 16:32], a[:, 16:32], a[:, 16 - 2 ** i:32 - 2 ** i], ALU.add))
            ends = scan[0][:, 16:32]
            then(v.tensor_tensor(nstart, ends, ntile, ALU.subtract))
            then(v.tensor_scalar(nstart, nstart, float(P), None, ALU.mult))
            then(v.tensor_tensor(place_, place_, nstart.unsqueeze(1).broadcast_to([P, NT, NE]), ALU.add))
            for j, one in enumerate((one0, one1)):
                then(v.tensor_tensor(tmp16, place_, one, ALU.mult))
                then(v.tensor_reduce(fdest, tmp16, AX.X, ALU.add))
                v.tensor_copy(dest[:, j, :], fdest).then_inc(dest_set, 1)
                dve.wait_ge(dest_set, j + 1)
            then(v.tensor_copy(expert_end[:], ends))
            for i in range(4):
                then(v.tensor_scalar(tile_count[:, i:i + 1], ends[:, NE - 1:NE], float(i - 3), None, ALU.add))
            c4 = cmp.rearrange("p (n e) -> p n e", n=32)
            then(v.tensor_tensor(c4, iota29.unsqueeze(2).broadcast_to([P, 32, NE]),
                                 ends.unsqueeze(1).broadcast_to([P, 32, NE]), ALU.is_ge))
            then(v.tensor_reduce(texpf, c4, AX.X, ALU.add))
            v.tensor_copy(tile_expert[:], texpf).then_inc(tables_set, 1)
            for t in range(NT):
                dve.wait_ge(y_mm, 3 * NT + t + 1)
                v.scalar_tensor_tensor(x[:, t, :], ps[:, (3 * NT + t) % 2, :], tg[:, 3:4], x[:, t, :], ALU.mult, ALU.add
                                       ).then_inc(y_sv, 1)

            dve.wait_ge(tables_set, 1)
            last3, last2, last1, tiles = counts(dve)

            def tile_hidden(n):
                dve.wait_ge(gu_mm, n + 1)
                dve.wait_ge(m_silu, n + 1)
                if not (isinstance(n, int) and n == 0):
                    dve.wait_ge(hx_tr, n)
                v.tensor_tensor(hmoe[:, 0:EI], ps[:, 5, 0:EI], smoe, ALU.mult).then_inc(m_h, 1)

            def tile_hidden_save(n):
                dve.wait_ge(hx_tr, n + 1)
                v.tensor_copy(hmoeT, ps[:, 7, 0:3 * P].rearrange("p (c t) -> p c t", c=3)).then_inc(hx_sv, 1)

            def tile_out(n, stored=None):
                dve.wait_ge(d_mm, n + 1)
                if stored is not None:
                    dve.wait_ge(y_st, stored)
                v.tensor_scalar(arena[:, bass.ds(A_YR + (n % 2) * D, D)], ps[:, 3, :], 1.0, None, ALU.mult
                                ).then_inc(d_sv, 1)

            tile_hidden(0)
            tile_hidden_save(0)
            tile_hidden(1)
            tile_out(0)
            tile_hidden_save(1)
            tile_hidden(2)
            tile_out(1)
            tile_hidden_save(2)
            with dve.Fori(3, tiles) as n:
                tile_hidden(n)
                tile_out(n - 1, n * 16 - 32)
                tile_hidden_save(n)
            tile_out(last1, last2 * 16)

            for t in range(NT):
                dve.wait_ge(back_ld[t], 32)
                for j in range(2):
                    last = v.scalar_tensor_tensor(x[:, t, :], back[t][j], wtop[:, t, j:j + 1], x[:, t, :],
                                                  ALU.mult, ALU.add)
                    if j == 0:
                        then(last)
                last.then_inc(out_st, 1)

        @block.gpsimd
        def _(pool):
            nc.gpsimd.memset(ident[:], 0.0).then_inc(pool_step, 1)
            pool.wait_ge(pool_step, 1)
            nc.gpsimd.affine_select(out=ident[:], in_=ident[:], compare_op=ALU.not_equal, fill=1.0, base=0,
                                    pattern=[[-1, P]], channel_multiplier=1).then_inc(consts_set, 1)
            pool.wait_ge(wq0_high, 1)
            nc.gpsimd.tensor_tensor(wq0[1][:, 2:4], wq0[2][:, 2:4], wq0[0][:, 2:4].bitcast(F32), ALU.subtract).then_inc(wq0_low, 1)
            nc.gpsimd.memset(queries_h[:].bitcast(F32), 0.0)
            pool.wait_ge(ln_out, NT)
            for g in range(G):
                last = nc.gpsimd.memset(queries_l[g][:].bitcast(F32), 0.0)
            last.then_inc(qbd_zero, 1)

            pool.wait_ge(rows_set, 1)
            for t in range(NT):
                if t == RT_AT:
                    pool.wait_ge(x_again, 16)
                nc.gpsimd.tensor_tensor(x[:, t, :], x[:, t, :], rows[:, 2 * D:3 * D], ALU.add).then_inc(beta_set, 1)

            pool.wait_ge(y_mm, 2 * NT)
            nc.gpsimd.memset(kvbd, 0.0).then_inc(kvbd_set, 1)
            nc.gpsimd.memset(ksbd, 0.0).then_inc(ksbd_set, 1)
            nc.gpsimd.memset(zero, 0.0).then_inc(zero_set, 1)
            pool.wait_ge(zero_set, 1)
            pool.dma_start(xs_dram.rearrange("(t p) d -> p t d", p=P),
                           zero.unsqueeze(1).broadcast_to([P, ROWS_MAX, D])).then_inc(filled, 16)
            for i in range(8):
                n, m = i // 4, i % 4
                pool.wait_ge(at_sv, 4 * n + 4)
                pool.wait_ge(g1_sv, i + 1)
                nc.gpsimd.tensor_tensor(qT[:, m, n * HALF:(n + 1) * HALF], qT[:, m, n * HALF:(n + 1) * HALF],
                                        gT[:, m, n * HALF:(n + 1) * HALF], ALU.mult).then_inc(gated, 1)
            pool.wait_ge(at_low, 8)
            nc.gpsimd.iota(iota16, pattern=[[1, NE]], base=0, channel_multiplier=0,
                           allow_small_or_imprecise_dtypes=True).then_inc(tri_set, 1)
            nc.gpsimd.iota(thr, pattern=[[P, NT]], base=0, channel_multiplier=0,
                           allow_small_or_imprecise_dtypes=True)
            nc.gpsimd.iota(iota29, pattern=[[1, 32]], base=0, channel_multiplier=0,
                           allow_small_or_imprecise_dtypes=True).then_inc(tri_set, 1)
            nc.gpsimd.memset(ones, 1.0).then_inc(tri_set, 1)
            pool.wait_ge(tri_set, 3)
            nc.gpsimd.affine_select(out=lower, in_=ones, compare_op=ALU.is_gt, fill=0.0, base=0,
                                    pattern=[[1, P]], channel_multiplier=-1).then_inc(tri_set, 1)
            pool.wait_ge(filled, 16)
            pool.wait_ge(dest_set, 2)
            pool.wait_ge(ln_out, 4 * NT)
            for j in range(2):
                for t in range(NT):
                    pool.indirect_dma_start(xs_dram, bass.IndirectOffsetOnAxis(dest[:, j, t:t + 1], 0),
                                            h3[:, t, :], None).then_inc(scattered, 16)
            pool.wait_ge(scattered, 16 * 2 * NT)
            pool.wait_ge(tables_set, 1)
            last3, last2, last1, tiles = counts(pool)

            def load(n):
                pool.dma_start(arena[:, bass.ds(A_XR + (n % 2) * D, D)], xs_dram[bass.ds(n * P, P), :]
                               ).then_inc(xg_ld, 16)

            def place(n):
                nc.gpsimd.tensor_copy(xg, arena[:, bass.ds(A_XR + (n % 2) * D, D)]).then_inc(xs_rdy, 1)

            def store(n, stored=None):
                pool.wait_ge(d_sv, n + 1)
                if stored is not None:
                    pool.wait_ge(y_st, stored)
                pool.dma_start(xs_dram[bass.ds(n * P, P), :], arena[:, bass.ds(A_YR + (n % 2) * D, D)]
                               ).then_inc(y_st, 16)

            load(0)
            pool.wait_ge(xg_ld, 16)
            load(1)
            place(0)
            pool.wait_ge(xg_ld, 32)
            pool.wait_ge(xs_rdy, 1)
            load(2)
            pool.wait_ge(xg_tr, 1)
            place(1)
            pool.wait_ge(xg_ld, 48)
            pool.wait_ge(xs_rdy, 2)
            load(3)
            pool.wait_ge(xg_tr, 2)
            place(2)
            store(0)
            with pool.Fori(3, last1) as n:
                pool.wait_ge(xg_ld, n * 16 + 16)
                pool.wait_ge(xs_rdy, n)
                load(n + 1)
                pool.wait_ge(xg_tr, n)
                place(n)
                store(n - 2, n * 16 - 32)
            pool.wait_ge(xg_ld, tiles * 16)
            pool.wait_ge(xg_tr, last1)
            place(last1)
            store(last3, last3 * 16)
            store(last2, last2 * 16)
            store(last1, last1 * 16)
            pool.wait_ge(y_st, tiles * 16)
            pool.sem_inc(pool_held, 1)
            for t in range(NT):
                for j in range(2):
                    pool.indirect_dma_start(back[t][j], None, xs_dram,
                                            bass.IndirectOffsetOnAxis(dest[:, j, t:t + 1], 0)).then_inc(back_ld[t], 16)


def kernel(**inputs):
    import numpy as np
    import concourse.bacc as bacc
    from concourse.bass_utils import run_bass_kernel_spmd

    a = {k: np.asarray(v) for k, v in inputs.items()}

    def w_t(w):
        o, i = w.shape
        return np.ascontiguousarray(w.T.reshape(i // P, P, o).transpose(1, 0, 2))

    def col(v):
        return v.reshape(-1, P).T

    def gate_up_chunks(gate, up, at, size):
        return np.concatenate([w_t(gate[at:at + size]), w_t(up[at:at + size])], axis=1)

    c = np.ascontiguousarray
    feeds = {
        "x": c(a["x"].reshape(TOK, D)),
        "ctx": c(np.pad(a["ctx_2048"].transpose(0, 2, 1), ((0, 0), (0, 0), (0, TE - T)))
                 .reshape(B, KC, P, TE).transpose(0, 2, 1, 3)),
        "mask": c(a["mask_BxS2_ik0"].reshape(B, TC, TP).transpose(2, 0, 1).reshape(TP, B * TC)),
        "cols": c(np.concatenate([col(a["L0_xattn_bq"]), col(a["L0_xattn_bk"]), col(a["L1_xattn_bg"]),
                                  col(a["L0_ffn_gate_s"]), col(a["L0_ffn_up_s"])], axis=1)),
        "rows": c(np.concatenate([a["L0_xattn_bv"], a["L0_xattn_bo"], a["L0_xattn_ln_gamma"],
                                  a["L0_xattn_ln_beta"], a["L0_ffn_down_s"]])),
        "scal": c(np.concatenate([a["g_xattn"], a["g_ffn"], a["L0_xattn_residual_scale"].reshape(1)])),
        "wq0": w_t(a["L0_xattn_Wq"]),
        "wk0": w_t(a["L0_xattn_Wk"]),
        "wv0": w_t(a["L0_xattn_Wv"]),
        "wo0": w_t(a["L0_xattn_Wo"]),
        "gu0": c(np.stack([gate_up_chunks(a["L0_ffn_gate_w"], a["L0_ffn_up_w"], m * P, P) for m in range(MC)])),
        "wd0": w_t(a["L0_ffn_down_w"]),
        "wq1": w_t(a["L1_xattn_Wq"]),
        "wg1": w_t(a["L1_xattn_Wg"]),
        "wkv1": w_t(a["L1_xattn_Wkv"]),
        "wo1": w_t(a["L1_xattn_Wo"]),
        "gate": w_t(a["L1_ffn_gate_w"]),
        "sh13": c(np.concatenate([gate_up_chunks(a["L1_ffn_sw1"], a["L1_ffn_sw3"], at, z).reshape(P, 2 * KC * z)
                                  for at, z in zip(SH_AT, SH_CHUNKS)], axis=1)),
        "sh2": c(a["L1_ffn_sw2"].T),
        "e13": c(np.concatenate([a["L1_ffn_w1"], a["L1_ffn_w3"]], axis=1).transpose(0, 2, 1)
                 .reshape(NE, KC, P, 2 * EI).transpose(0, 2, 1, 3).reshape(NE, P, KC * 2 * EI)),
        "e2": c(a["L1_ffn_w2"].transpose(0, 2, 1)),
    }
    nc = bacc.Bacc("TRN2", target_bir_lowering=False, num_devices=1)
    args = [nc.dram_tensor(f"in_{k}", v.shape, mybir.dt.from_np(v.dtype), kind="ExternalInput").ap()
            for k, v in feeds.items()]
    result = nc.dram_tensor("out_x", (TOK, D), F32, kind="ExternalOutput").ap()
    flamingo(nc, *args, result)
    r = run_bass_kernel_spmd(nc, [{f"in_{k}": v for k, v in feeds.items()}], core_ids=[0])
    return r.results[0]["out_x"].reshape(B, S, D)
```
